# Optimizing a Trainium2 kernel written in Bass

```python
import numpy as np
import jax
import jax.numpy as jnp

def _softmax(x, axis=-1):
    return jax.nn.softmax(x, axis=axis)

def _gelu(x):
    return jax.nn.gelu(x, approximate=True)

def _silu(x):
    return jax.nn.silu(x)

def _sigmoid(x):
    return jax.nn.sigmoid(x)

def _layernorm(x, axis=-1, eps=1e-05):
    m = jnp.mean(x, axis=axis, keepdims=True)
    v = jnp.var(x, axis=axis, keepdims=True)
    return (x - m) / jnp.sqrt(v + eps)

def _scatter_add(tgt, idx, src, axis=0):
    return tgt.at[idx].add(src)

def _segment_sum(src, seg, n):
    return jax.ops.segment_sum(src, seg, n)
kernel_name = 'mk_conv_preact_d4_conv_nchw512_r2_212d87'

def setup_inputs(seed: int=0):
    np.random.seed(seed)
    _w = jnp.asarray

    def _rec_inputs():
        import jax
        import jax.numpy as jnp
        _gk = jax.random.key(seed)
        x = 7.22e-05 + 1 * jax.random.normal(jax.random.fold_in(_gk, 1), (4, 256, 32, 32), jnp.float32)
        return x
    x = _rec_inputs()

    def _L0_conv_setup():
        import jax, jax.numpy as jnp
        import numpy as np
        from jax import lax
        DIM = 256
        HEADS = 8
        SR = 2
        EPS = 1e-05

        def _conv1x1(x, w, b):
            return jnp.einsum('oc,bchw->bohw', w, x) + b[None, :, None, None]
        key = jax.random.key(seed)
        ks = jax.random.split(key, 8)
        B, C, H, W = (4, DIM, 32, 32)
        s = 1.0 / np.sqrt(C)
        return {'x': jax.random.normal(ks[0], (B, C, H, W), jnp.float32), 'q_w': jax.random.normal(ks[1], (C, C), jnp.float32) * s, 'q_b': jnp.zeros((C,), jnp.float32), 'kv_w': jax.random.normal(ks[2], (2 * C, C), jnp.float32) * s, 'kv_b': jnp.zeros((2 * C,), jnp.float32), 'ds_w': jax.random.normal(ks[3], (C, C, SR, SR), jnp.float32) * (s / SR), 'ds_b': jnp.zeros((C,), jnp.float32), 'ln_w': jnp.ones((C,), jnp.float32), 'ln_b': jnp.zeros((C,), jnp.float32), 'proj_w': jax.random.normal(ks[4], (C, C), jnp.float32) * s, 'proj_b': jnp.zeros((C,), jnp.float32)}
    _L0_conv_all = _L0_conv_setup()
    _L0_conv_in = {k: v for k, v in _L0_conv_all.items() if k in ('q_w', 'q_b', 'kv_w', 'kv_b', 'ds_w', 'ds_b', 'ln_w', 'ln_b', 'proj_w', 'proj_b')}
    del _L0_conv_all

    def _L1_conv_setup():
        import jax, jax.numpy as jnp
        import numpy as np
        EPS = 1e-05

        def layernorm(x, g, b):
            mu = x.mean(-1, keepdims=True)
            var = x.var(-1, keepdims=True)
            return (x - mu) * jax.lax.rsqrt(var + EPS) * g + b

        def cross_scan(x, g):
            B, D, H, W = x.shape
            if g in (1, 3):
                u = x.reshape(B, D, H * W)
            else:
                u = jnp.transpose(x, (0, 1, 3, 2)).reshape(B, D, H * W)
            if g in (3, 4):
                u = u[:, :, ::-1]
            return u

        def cross_merge(y, g, H, W):
            B, D, L = y.shape
            if g in (3, 4):
                y = y[:, :, ::-1]
            if g in (2, 4):
                y = jnp.transpose(y.reshape(B, D, W, H), (0, 1, 3, 2)).reshape(B, D, L)
            return y

        def ss2d(x, g, in_proj_w, cw, cb, xp_w, dtp_w, dtp_b, A_log, Ds, og, ob, op_w):
            B, H, W, d = x.shape
            D = in_proj_w.shape[0] // 2
            xz = jnp.einsum('bhwc,ec->bhwe', x, in_proj_w)
            xd, z = jnp.split(xz, 2, axis=-1)
            z = jax.nn.silu(z)
            xc = jnp.transpose(xd, (0, 3, 1, 2))
            xc = jax.lax.conv_general_dilated(xc, cw, (1, 1), 'SAME', feature_group_count=D)
            xc = jax.nn.silu(xc + cb[None, :, None, None])
            u = cross_scan(xc, g)
            R = dtp_w.shape[1]
            N = A_log.shape[1]
            x_dbl = jnp.einsum('bdl,cd->bcl', u, xp_w)
            dt, Bm, Cm = jnp.split(x_dbl, [R, R + N], axis=1)
            delta = jax.nn.softplus(jnp.einsum('brl,dr->bdl', dt, dtp_w) + dtp_b[None, :, None])
            A = -jnp.exp(A_log)
            dA = jnp.exp(jnp.einsum('bdl,dn->lbdn', delta, A))
            dBu = jnp.einsum('bdl,bnl->lbdn', delta * u, Bm)
            Cs = jnp.transpose(Cm, (2, 0, 1))

            def step(h, inp):
                a, bu, c = inp
                h = a * h + bu
                return (h, jnp.einsum('bdn,bn->bd', h, c))
            h0 = jnp.zeros((B, D, N), dtype=u.dtype)
            _, ys = jax.lax.scan(step, h0, (dA, dBu, Cs))
            y = jnp.transpose(ys, (1, 2, 0)) + Ds[None, :, None] * u
            y = cross_merge(y, g, H, W)
            y = layernorm(jnp.transpose(y, (0, 2, 1)), og, ob).reshape(B, H, W, D)
            return jnp.einsum('bhwe,ce->bhwc', y * z, op_w)
        key = jax.random.key(seed)
        ks = jax.random.split(key, 12)
        B, C, H, W = (8, 256, 32, 32)
        G = 4
        d = C // G
        D, R, N = (d, 8, 1)
        red = C // 16
        s = 0.02
        f32 = jnp.float32
        return dict(x=jax.random.normal(ks[0], (B, C, H, W), f32), ln_g=jnp.ones((C,), f32), ln_b=jnp.zeros((C,), f32), fc1_w=jax.random.normal(ks[1], (red, C), f32) * s, fc1_b=jnp.zeros((red,), f32), fc2_w=jax.random.normal(ks[2], (C, red), f32) * s, fc2_b=jnp.zeros((C,), f32), in_proj_w=jax.random.normal(ks[3], (G, 2 * D, d), f32) * s, conv_w=jax.random.normal(ks[4], (G, D, 1, 3, 3), f32) * s, conv_b=jnp.zeros((G, D), f32), x_proj_w=jax.random.normal(ks[5], (G, R + 2 * N, D), f32) * s, dt_proj_w=jax.random.normal(ks[6], (G, D, R), f32) * s, dt_proj_b=jax.random.normal(ks[7], (G, D), f32) * 0.1, A_log=jax.random.uniform(ks[8], (G, D, N), f32), Ds_p=jnp.ones((G, D), f32), onorm_g=jnp.ones((G, D), f32), onorm_b=jnp.zeros((G, D), f32), out_proj_w=jax.random.normal(ks[9], (G, d, D), f32) * s, proj_w=jax.random.normal(ks[10], (C, C), f32) * s, proj_b=jnp.zeros((C,), f32), skip_scale=jnp.ones((1,), f32))
    _L1_conv_all = _L1_conv_setup()
    _L1_conv_in = {k: v for k, v in _L1_conv_all.items() if k in ('ln_g', 'ln_b', 'fc1_w', 'fc1_b', 'fc2_w', 'fc2_b', 'in_proj_w', 'conv_w', 'conv_b', 'x_proj_w', 'dt_proj_w', 'dt_proj_b', 'A_log', 'Ds_p', 'onorm_g', 'onorm_b', 'out_proj_w', 'proj_w', 'proj_b', 'skip_scale')}
    del _L1_conv_all

    def _L2_conv_setup():
        import jax, jax.numpy as jnp
        import numpy as np
        B, C, H, W = (8, 256, 32, 32)
        NUM_HEADS = 8
        HEAD_DIM = C // NUM_HEADS
        EPS = 1e-05

        def _layer_norm_lastdim(x):
            mu = jnp.mean(x, axis=-1, keepdims=True)
            var = jnp.mean(jnp.square(x - mu), axis=-1, keepdims=True)
            return (x - mu) * jax.lax.rsqrt(var + EPS)
        key = jax.random.key(seed)
        k1, k2, k3 = jax.random.split(key, 3)
        x = jax.random.normal(k1, (B, C, H, W), dtype=jnp.float32)
        lim_qkv = float(np.sqrt(6.0 / (C + 3 * C)))
        qkv_w = jax.random.uniform(k2, (3 * C, C), dtype=jnp.float32, minval=-lim_qkv, maxval=lim_qkv)
        qkv_b = jnp.zeros((3 * C,), dtype=jnp.float32)
        lim_p = float(np.sqrt(6.0 / (C + C)))
        proj_w = jax.random.uniform(k3, (C, C), dtype=jnp.float32, minval=-lim_p, maxval=lim_p)
        proj_b = jnp.zeros((C,), dtype=jnp.float32)
        return {'x': x, 'qkv_w': qkv_w, 'qkv_b': qkv_b, 'proj_w': proj_w, 'proj_b': proj_b}
    _L2_conv_all = _L2_conv_setup()
    _L2_conv_in = {k: v for k, v in _L2_conv_all.items() if k in ('qkv_w', 'qkv_b', 'proj_w', 'proj_b')}
    del _L2_conv_all

    def _L3_conv_setup():
        import jax, jax.numpy as jnp
        import numpy as np
        KERNELS = (1, 3, 5, 7, 9, 11, 13)

        def _maxpool_same(x, k):
            if k == 1:
                return x
            return jax.lax.reduce_window(x, -jnp.inf, jax.lax.max, window_dimensions=(1, 1, k, k), window_strides=(1, 1, 1, 1), padding='SAME')
        key = jax.random.key(seed)
        k_x, k_w1, k_b1, k_w2, k_b2 = jax.random.split(key, 5)
        b, c, h, w = (8, 256, 32, 32)
        c16 = c // 16
        x = jax.random.normal(k_x, (b, c, h, w), dtype=jnp.float32)
        w1 = jax.random.normal(k_w1, (c16, c), dtype=jnp.float32) * (1.0 / np.sqrt(c))
        b1 = jax.random.normal(k_b1, (c16,), dtype=jnp.float32) * 0.1
        w2 = jax.random.normal(k_w2, (c, c16), dtype=jnp.float32) * (1.0 / np.sqrt(c16))
        b2 = jax.random.uniform(k_b2, (c,), dtype=jnp.float32, minval=0.0, maxval=6.0)
        return {'x': x, 'w1': w1, 'b1': b1, 'w2': w2, 'b2': b2}
    _L3_conv_all = _L3_conv_setup()
    _L3_conv_in = {k: v for k, v in _L3_conv_all.items() if k in ('w1', 'b1', 'w2', 'b2')}
    del _L3_conv_all
    return {'x': x, 'L0_conv_q_w': _L0_conv_in['q_w'], 'L0_conv_q_b': _L0_conv_in['q_b'], 'L0_conv_kv_w': _L0_conv_in['kv_w'], 'L0_conv_kv_b': _L0_conv_in['kv_b'], 'L0_conv_ds_w': _L0_conv_in['ds_w'], 'L0_conv_ds_b': _L0_conv_in['ds_b'], 'L0_conv_ln_w': _L0_conv_in['ln_w'], 'L0_conv_ln_b': _L0_conv_in['ln_b'], 'L0_conv_proj_w': _L0_conv_in['proj_w'], 'L0_conv_proj_b': _L0_conv_in['proj_b'], 'L1_conv_ln_g': _L1_conv_in['ln_g'], 'L1_conv_ln_b': _L1_conv_in['ln_b'], 'L1_conv_fc1_w': _L1_conv_in['fc1_w'], 'L1_conv_fc1_b': _L1_conv_in['fc1_b'], 'L1_conv_fc2_w': _L1_conv_in['fc2_w'], 'L1_conv_fc2_b': _L1_conv_in['fc2_b'], 'L1_conv_in_proj_w': _L1_conv_in['in_proj_w'], 'L1_conv_conv_w': _L1_conv_in['conv_w'], 'L1_conv_conv_b': _L1_conv_in['conv_b'], 'L1_conv_x_proj_w': _L1_conv_in['x_proj_w'], 'L1_conv_dt_proj_w': _L1_conv_in['dt_proj_w'], 'L1_conv_dt_proj_b': _L1_conv_in['dt_proj_b'], 'L1_conv_A_log': _L1_conv_in['A_log'], 'L1_conv_Ds_p': _L1_conv_in['Ds_p'], 'L1_conv_onorm_g': _L1_conv_in['onorm_g'], 'L1_conv_onorm_b': _L1_conv_in['onorm_b'], 'L1_conv_out_proj_w': _L1_conv_in['out_proj_w'], 'L1_conv_proj_w': _L1_conv_in['proj_w'], 'L1_conv_proj_b': _L1_conv_in['proj_b'], 'L1_conv_skip_scale': _L1_conv_in['skip_scale'], 'L2_conv_qkv_w': _L2_conv_in['qkv_w'], 'L2_conv_qkv_b': _L2_conv_in['qkv_b'], 'L2_conv_proj_w': _L2_conv_in['proj_w'], 'L2_conv_proj_b': _L2_conv_in['proj_b'], 'L3_conv_w1': _L3_conv_in['w1'], 'L3_conv_b1': _L3_conv_in['b1'], 'L3_conv_w2': _L3_conv_in['w2'], 'L3_conv_b2': _L3_conv_in['b2']}

def reference(x, L0_conv_q_w, L0_conv_q_b, L0_conv_kv_w, L0_conv_kv_b, L0_conv_ds_w, L0_conv_ds_b, L0_conv_ln_w, L0_conv_ln_b, L0_conv_proj_w, L0_conv_proj_b, L1_conv_ln_g, L1_conv_ln_b, L1_conv_fc1_w, L1_conv_fc1_b, L1_conv_fc2_w, L1_conv_fc2_b, L1_conv_in_proj_w, L1_conv_conv_w, L1_conv_conv_b, L1_conv_x_proj_w, L1_conv_dt_proj_w, L1_conv_dt_proj_b, L1_conv_A_log, L1_conv_Ds_p, L1_conv_onorm_g, L1_conv_onorm_b, L1_conv_out_proj_w, L1_conv_proj_w, L1_conv_proj_b, L1_conv_skip_scale, L2_conv_qkv_w, L2_conv_qkv_b, L2_conv_proj_w, L2_conv_proj_b, L3_conv_w1, L3_conv_b1, L3_conv_w2, L3_conv_b2):
    import jax
    import jax.numpy as jnp

    def _L0_conv_ref(x, q_w, q_b, kv_w, kv_b, ds_w, ds_b, ln_w, ln_b, proj_w, proj_b):
        import jax, jax.numpy as jnp
        import numpy as np
        from jax import lax
        DIM = 256
        HEADS = 8
        SR = 2
        EPS = 1e-05

        def _conv1x1(x, w, b):
            return jnp.einsum('oc,bchw->bohw', w, x) + b[None, :, None, None]
        B, C, H, W = x.shape
        heads, sr = (HEADS, SR)
        hd = C // heads
        scale = hd ** (-0.5)
        q = _conv1x1(x, q_w, q_b)
        x_ds = lax.conv_general_dilated(x, ds_w, window_strides=(sr, sr), padding='VALID', dimension_numbers=('NCHW', 'OIHW', 'NCHW')) + ds_b[None, :, None, None]
        mu = jnp.mean(x_ds, axis=1, keepdims=True)
        var = jnp.var(x_ds, axis=1, keepdims=True)
        x_ds = (x_ds - mu) * lax.rsqrt(var + EPS)
        x_ds = x_ds * ln_w[None, :, None, None] + ln_b[None, :, None, None]
        kv = _conv1x1(x_ds, kv_w, kv_b)
        k, v = jnp.split(kv, 2, axis=1)
        Nq = H * W
        Nk = H // sr * (W // sr)
        q = q.reshape(B * heads, hd, Nq) * scale
        k = k.reshape(B * heads, hd, Nk)
        v = v.reshape(B * heads, hd, Nk)
        attn = jax.nn.softmax(jnp.einsum('bcm,bcn->bmn', q, k), axis=-1)
        out = jnp.einsum('bmn,bcn->bcm', attn, v).reshape(B, C, H, W)
        out = _conv1x1(out, proj_w, proj_b)
        return out

    def _L1_conv_ref(x, ln_g, ln_b, fc1_w, fc1_b, fc2_w, fc2_b, in_proj_w, conv_w, conv_b, x_proj_w, dt_proj_w, dt_proj_b, A_log, Ds_p, onorm_g, onorm_b, out_proj_w, proj_w, proj_b, skip_scale):
        import jax, jax.numpy as jnp
        import numpy as np
        EPS = 1e-05

        def layernorm(x, g, b):
            mu = x.mean(-1, keepdims=True)
            var = x.var(-1, keepdims=True)
            return (x - mu) * jax.lax.rsqrt(var + EPS) * g + b

        def cross_scan(x, g):
            B, D, H, W = x.shape
            if g in (1, 3):
                u = x.reshape(B, D, H * W)
            else:
                u = jnp.transpose(x, (0, 1, 3, 2)).reshape(B, D, H * W)
            if g in (3, 4):
                u = u[:, :, ::-1]
            return u

        def cross_merge(y, g, H, W):
            B, D, L = y.shape
            if g in (3, 4):
                y = y[:, :, ::-1]
            if g in (2, 4):
                y = jnp.transpose(y.reshape(B, D, W, H), (0, 1, 3, 2)).reshape(B, D, L)
            return y

        def ss2d(x, g, in_proj_w, cw, cb, xp_w, dtp_w, dtp_b, A_log, Ds, og, ob, op_w):
            B, H, W, d = x.shape
            D = in_proj_w.shape[0] // 2
            xz = jnp.einsum('bhwc,ec->bhwe', x, in_proj_w)
            xd, z = jnp.split(xz, 2, axis=-1)
            z = jax.nn.silu(z)
            xc = jnp.transpose(xd, (0, 3, 1, 2))
            xc = jax.lax.conv_general_dilated(xc, cw, (1, 1), 'SAME', feature_group_count=D)
            xc = jax.nn.silu(xc + cb[None, :, None, None])
            u = cross_scan(xc, g)
            R = dtp_w.shape[1]
            N = A_log.shape[1]
            x_dbl = jnp.einsum('bdl,cd->bcl', u, xp_w)
            dt, Bm, Cm = jnp.split(x_dbl, [R, R + N], axis=1)
            delta = jax.nn.softplus(jnp.einsum('brl,dr->bdl', dt, dtp_w) + dtp_b[None, :, None])
            A = -jnp.exp(A_log)
            dA = jnp.exp(jnp.einsum('bdl,dn->lbdn', delta, A))
            dBu = jnp.einsum('bdl,bnl->lbdn', delta * u, Bm)
            Cs = jnp.transpose(Cm, (2, 0, 1))

            def step(h, inp):
                a, bu, c = inp
                h = a * h + bu
                return (h, jnp.einsum('bdn,bn->bd', h, c))
            h0 = jnp.zeros((B, D, N), dtype=u.dtype)
            _, ys = jax.lax.scan(step, h0, (dA, dBu, Cs))
            y = jnp.transpose(ys, (1, 2, 0)) + Ds[None, :, None] * u
            y = cross_merge(y, g, H, W)
            y = layernorm(jnp.transpose(y, (0, 2, 1)), og, ob).reshape(B, H, W, D)
            return jnp.einsum('bhwe,ce->bhwc', y * z, op_w)
        B, C, H, W = x.shape
        L = H * W
        xn = layernorm(jnp.transpose(x.reshape(B, C, L), (0, 2, 1)), ln_g, ln_b)
        z = xn.mean(axis=1)
        gate = jax.nn.sigmoid(jax.nn.relu(z @ fc1_w.T + fc1_b) @ fc2_w.T + fc2_b)
        x4 = xn.reshape(B, H, W, C)
        chunks = jnp.split(x4, 4, axis=-1)
        ys = [ss2d(chunks[g], g + 1, in_proj_w[g], conv_w[g], conv_b[g], x_proj_w[g], dt_proj_w[g], dt_proj_b[g], A_log[g], Ds_p[g], onorm_g[g], onorm_b[g], out_proj_w[g]) for g in range(4)]
        xm = jnp.concatenate(ys, axis=-1) * skip_scale * x4
        xm = xm.reshape(B, L, C) * gate[:, None, :]
        xm = layernorm(xm, ln_g, ln_b)
        out = xm @ proj_w.T + proj_b
        return jnp.transpose(out, (0, 2, 1)).reshape(B, proj_w.shape[0], H, W)

    def _L2_conv_ref(x, qkv_w, qkv_b, proj_w, proj_b):
        import jax, jax.numpy as jnp
        import numpy as np
        B, C, H, W = (8, 256, 32, 32)
        NUM_HEADS = 8
        HEAD_DIM = C // NUM_HEADS
        EPS = 1e-05

        def _layer_norm_lastdim(x):
            mu = jnp.mean(x, axis=-1, keepdims=True)
            var = jnp.mean(jnp.square(x - mu), axis=-1, keepdims=True)
            return (x - mu) * jax.lax.rsqrt(var + EPS)
        b, c, h, w = x.shape
        n = h * w
        nh, hd = (NUM_HEADS, c // NUM_HEADS)
        xt = x.transpose(0, 2, 3, 1).reshape(b, n, c)
        x_norm = _layer_norm_lastdim(xt)
        qkv = jnp.einsum('bnc,oc->bno', x_norm, qkv_w) + qkv_b
        qkv = qkv.reshape(b, n, 3, nh, hd)
        q, k, v = (qkv[:, :, 0], qkv[:, :, 1], qkv[:, :, 2])
        scale = float(hd) ** (-0.5)
        attn = jnp.einsum('bnhi,bnhj->bhij', q, k) * scale
        attn = jnp.clip(attn, -50.0, 50.0)
        attn = jax.nn.softmax(attn, axis=-1)
        attn = jnp.where(jnp.isnan(attn), 1.0 / hd, attn)
        out = jnp.einsum('bhij,bnhj->bhin', attn, v)
        out = out.reshape(b, c, n)
        out = jnp.einsum('oc,bcn->bon', proj_w, out) + proj_b[None, :, None]
        return out.reshape(b, c, h, w)

    def _L3_conv_ref(x, w1, b1, w2, b2):
        import jax, jax.numpy as jnp
        import numpy as np
        KERNELS = (1, 3, 5, 7, 9, 11, 13)

        def _maxpool_same(x, k):
            if k == 1:
                return x
            return jax.lax.reduce_window(x, -jnp.inf, jax.lax.max, window_dimensions=(1, 1, k, k), window_strides=(1, 1, 1, 1), padding='SAME')
        b, c, h, w = x.shape
        n_k = len(KERNELS)
        gap = jnp.mean(x, axis=(2, 3))
        hmid = jax.nn.relu(jnp.einsum('bc,ec->be', gap, w1) + b1)
        score = jnp.einsum('be,ce->bc', hmid, w2) + b2
        s = jax.nn.relu(score)
        q_s = jnp.clip(jnp.floor(jax.lax.stop_gradient(s)), 0, n_k - 2).astype(jnp.int32)
        q_b = q_s + 1
        pools = jnp.stack([_maxpool_same(x, k) for k in KERNELS], axis=2)
        s_out = jnp.take_along_axis(pools, q_s[:, :, None, None, None], axis=2)[:, :, 0]
        b_out = jnp.take_along_axis(pools, q_b[:, :, None, None, None], axis=2)[:, :, 0]
        frac_b = (s - q_s.astype(s.dtype))[:, :, None, None]
        frac_s = (q_b.astype(s.dtype) - s)[:, :, None, None]
        return frac_b * b_out + frac_s * s_out + x

    def _gn(v, G=32, eps=1e-05):
        B_, C_, H_, W_ = v.shape
        g = v.reshape(B_, G, C_ // G, H_, W_)
        m = jnp.mean(g, axis=(2, 3, 4), keepdims=True)
        s = jnp.var(g, axis=(2, 3, 4), keepdims=True)
        return ((g - m) / jnp.sqrt(s + eps)).reshape(v.shape)

    def _ln_c(v, eps=1e-06):
        m = jnp.mean(v, axis=1, keepdims=True)
        s = jnp.var(v, axis=1, keepdims=True)
        return (v - m) / jnp.sqrt(s + eps)

    def _ln_t(v, eps=1e-05):
        m = jnp.mean(v, axis=-1, keepdims=True)
        s = jnp.var(v, axis=-1, keepdims=True)
        return (v - m) / jnp.sqrt(s + eps)

    def _to_tokens(v):
        B_, C_, H_, W_ = v.shape
        return v.reshape(B_, C_, H_ * W_).transpose(0, 2, 1)

    def _from_tokens(t, like):
        B_, C_, H_, W_ = like.shape
        return t.transpose(0, 2, 1).reshape(B_, C_, H_, W_)
    x = x + _L0_conv_ref(_gn(x), L0_conv_q_w, L0_conv_q_b, L0_conv_kv_w, L0_conv_kv_b, L0_conv_ds_w, L0_conv_ds_b, L0_conv_ln_w, L0_conv_ln_b, L0_conv_proj_w, L0_conv_proj_b)
    x = x + _L1_conv_ref(_gn(x), L1_conv_ln_g, L1_conv_ln_b, L1_conv_fc1_w, L1_conv_fc1_b, L1_conv_fc2_w, L1_conv_fc2_b, L1_conv_in_proj_w, L1_conv_conv_w, L1_conv_conv_b, L1_conv_x_proj_w, L1_conv_dt_proj_w, L1_conv_dt_proj_b, L1_conv_A_log, L1_conv_Ds_p, L1_conv_onorm_g, L1_conv_onorm_b, L1_conv_out_proj_w, L1_conv_proj_w, L1_conv_proj_b, L1_conv_skip_scale)
    x = x + _L2_conv_ref(_gn(x), L2_conv_qkv_w, L2_conv_qkv_b, L2_conv_proj_w, L2_conv_proj_b)
    x = x + _L3_conv_ref(_gn(x), L3_conv_w1, L3_conv_b1, L3_conv_w2, L3_conv_b2)
    return x

_drawn_inputs = setup_inputs


def setup_inputs(seed=0):
    import zlib

    import numpy as np

    out = dict(_drawn_inputs(seed))
    spreads = {'L0_conv_q_b': (0.0, 0.272),
     'L0_conv_kv_b': (0.0, 0.1),
     'L0_conv_ds_b': (0.0, 0.1),
     'L0_conv_ln_w': (1.0, 0.2),
     'L0_conv_ln_b': (0.0, 0.1),
     'L0_conv_proj_b': (0.0, 0.1),
     'L1_conv_ln_g': (1.0, 0.2),
     'L1_conv_ln_b': (0.0, 0.1),
     'L1_conv_fc1_b': (0.0, 0.8),
     'L1_conv_fc2_b': (0.0, 0.484),
     'L1_conv_conv_b': (0.0, 0.1),
     'L1_conv_Ds_p': (1.0, 0.2),
     'L1_conv_onorm_g': (1.0, 0.2),
     'L1_conv_onorm_b': (0.0, 0.1),
     'L1_conv_proj_b': (0.0, 0.1),
     'L2_conv_qkv_b': (0.0, 0.1),
     'L2_conv_proj_b': (0.0, 0.1)}
    factors = {'L1_conv_fc1_w': 8.0,
     'L1_conv_fc2_w': 8.0,
     'L1_conv_x_proj_w': 64.0,
     'L1_conv_dt_proj_w': 64.0,
     'L1_conv_dt_proj_b': 64.0,
     'L1_conv_A_log': 64.0,
     'L3_conv_b1': 3.805}
    for name, (base, spread) in spreads.items():
        noise = np.random.default_rng([zlib.crc32(name.encode()), seed]).standard_normal(out[name].shape)
        drawn = base * np.exp(spread * noise) if base else spread * noise
        out[name] = jnp.asarray(drawn.astype(out[name].dtype))
    for name, factor in factors.items():
        out[name] = (out[name] * factor).astype(out[name].dtype)
    return out
```

```python
import concourse.bass as bass
from concourse import mybir
from contextlib import ExitStack

B, C, H, W = 4, 256, 32, 32
N = H * W
P = 128
CC = C // P
HALF = 512
HEADS, HD = 8, 32
NK = N // 4
QT = N // P
GROUPS = 4
TAPS = 9
KPOOL = 7
LOWEST = -3.0e38
SOFTPLUS_LINEAR = 20.0
EXP_LN_TABLE, SILU_TABLE = 6, 18
COLS = ["q_b", "k_b", "v_b", "ds_b", "kv_ln_w", "kv_ln_b", "pb0", "ln_g", "ln_b", "fc2_b", "skip",
        "conv_b", "dt_b", "A_log", "Ds", "og", "ob", "pb1", "v2_b", "pb2", "w2_b"]
MATS = ["ident", "mean256", "mean64", "center64", "mean_group"]

PE_STEPS = """
gn0 ds q0 q1 mean0 msq0 k vT s0_0 s0_1 s1_0 s1_1 s2_0 s2_1 s3_0 s3_1 mT0 s4_0 s4_1 st0_0 st0_1 s5_0
s5_1 st1_0 st1_1 pv0 s6_0 s6_1 st2_0 st2_1 pv1 s7_0 s7_1 mT1 st3_0 st3_1 pv2 st4_0 st4_1 pv3 st5_0
st5_1 pv4 st6_0 st6_1 pv5 st7_0 st7_1 pv6 pv7 oT0 oT1 proj0_0 proj0_1 gn1 mean1 msq1 xd0 xd1 z0 z1
fc1 fc2 v0 v1 B0 C0 B1 C1 yc0 yc1 yv0 yv1 op0 op1 mean2 msq2 proj1_0 proj1_1 gn2 mean3 msq3 xnT0
xnT1 gram rows T1 A PAT WE be out0 out1 gn3 w1 w2
"""
ACT_STEPS = """
gn_ln0 gn_rstd0 xds0 xds1 sq_ds qf0 qf1 ln_ln0 ln_rstd0 kf0 kf1 p0_0 p0_1 p1_0 p1_1 p2_0 p2_1 p3_0
p3_1 p4_0 p4_1 p5_0 p5_1 p6_0 p6_1 p7_0 p7_1 oc0 oc1 gn_ln1 gn_rstd1 sq1_0 sq1_1 ln_ln1 ln_rstd1 xn0
xn1 xn2 xn3 u0 u1 z0 z1 gate_exp v0 v1 ev0 lv0 ev1 lv1 dA0 dA1 yc0 ysq0 yc1 ysq1 yln0 yrs0 yln1 yrs1
sq2_0 sq2_1 ln_ln2 ln_rstd2 gn_ln2 gn_rstd2 sq3_0 sq3_1 ln_ln3 ln_rstd3 xnt0 xnt1 t1 aexp0 aexp1 pat
we gn_ln3 gn_rstd3
"""
DVE_STEPS = """
gn_st0_00 gn_st0_01 gn_st0_10 gn_st0_11 gn_m20 gn_m0 gn_sq0 gn_ex20 gn_gm0 gn_gm20 gn_var0 gn_b0
g0_0 g0_1 ln_mean0 ln_m20 ln_var0 c0_0 c0_1 n0_0 n0_1 qh0 qh1 kh vt mx0_0 mx0_1 mx1_0 mx1_1 mx2_0
mx2_1 mx3_0 mx3_1 mh0 ml0 mx4_0 mx4_1 mx5_0 mx5_1 rz0 o0 mx6_0 mx6_1 rz1 o1 mx7_0 mx7_1 mh1 ml1 rz2
o2 rz3 o3 rz4 o4 rz5 o5 rz6 o6 rz7 o7 x1_0 x1_1 gn_st1_00 gn_st1_01 gn_st1_10 gn_st1_11 gn_m21 gn_m1
gn_sq1 gn_ex21 gn_gm1 gn_gm21 gn_var1 gn_b1 g1_0 g1_1 ln_mean1 ln_m21 ln_var1 c1_0 c1_1 n1_0 n1_1
gap1 hm1 gate_in gate_1p gate gs vmin0 vmin1 delta0 delta1 dbu0 scan0 hc0 y0 dbu1 scan1 hc1 y1 yn0
ya0 yz0 yn1 ya1 yz1 xm0 xm1 xm2 xm3 ln_mean2 ln_m22 ln_var2 c2_0 c2_1 n2_0 n2_1 x2_0 x2_1 gn_st2_00
gn_st2_01 gn_st2_10 gn_st2_11 gn_m22 gn_m2 gn_sq2 gn_ex22 gn_gm2 gn_gm22 gn_var2 gn_b2 g2_0 g2_1
ln_mean3 ln_m23 ln_var3 c3_0 c3_1 n3_0 n3_1 xnt_ones gram srow ab0 aok0 ab1 aok1 ab2 aok2 ab3 aok3
aclip anan arow amax arec arok afill ap0 ap1 abd0 abd1 abd2 abd3 be x3_0 x3_1 gn_st3_00 gn_st3_01
gn_st3_10 gn_st3_11 gn_m23 gn_m3 gn_sq3 gn_ex23 gap3 gn_gm3 gn_gm23 gn_var3 gn_b3 gap3a gap3b hm3
sc0 sc cge0 cge1 qs eq fb fs0 fs ws0 ws1 wb0 wb1 cf0 cf1 c1 c0 coef
"""
POOL_STEPS = """
ql0 ql1 kl du0 du1
"""
PE_SETUP = """
fold wd fold0
"""
ACT_SETUP = """
expA negA
"""
DVE_SETUP = """
eps0 eps1 qbs kb vb pb1 wk0 wv0 wp10 wk1 wv1 wp11 wd pb0 wtap0_0 wtap0_1 wtap1_1 wtap1_2
"""
POOL_SETUP = """
kst1 vt1 abd xnp pa pb hb
"""
DVE_POOLS = """
hp1 h1_0 h1_1 vp1 u1_0 v1_0 u1_1 v1_1 hp2 h2_0 h2_1 vp2 u2_0 v2_0 u2_1 v2_1 hp3 h3_0 h3_1 vp3 u3_0
v3_0 u3_1 v3_1 hp4 h4_0 h4_1 vp4 u4_0 v4_0 u4_1 v4_1 hp5 h5_0 h5_1 vp5 u5_0 v5_0 u5_1 v5_1 hp6 h6_0
h6_1 vp6 u6_0 v6_0 u6_1 v6_1
"""
ACT_POOLS = """
a0 a1 y1_0 y1_1 y2_0 y2_1 y3_0 y3_1 y4_0 y4_1 y5_0 y5_1 y6_0 y6_1
"""
ADD_POOLS = """
add1 add2 add3 add4 add5 add6
"""


class Steps:

    def __init__(self, sem, text):
        self.sem, self.labels, self.said = sem, text.split(), []
        self.index = {x: n for n, x in enumerate(self.labels)}

    def step(self, label):
        n = len(self.said) % max(len(self.labels), 1)
        assert self.labels[n] == label, (label, self.labels[n])
        self.said.append(label)
        return self.sem, 1

    def at(self, b, label):
        return self.sem, b * len(self.labels) + self.index[label] + 1


def program(nc, x, cols, mats, wq, wk, wv, wds, wp0, small16, w1s, ipx, ipz, cw, xpr, dtp, xb, xc, opw,
            wp1, w2q, w2k, w2v, wp2, rows, kidx, out):
    f32, f16 = mybir.dt.float32, mybir.dt.float16
    i32 = mybir.dt.int32
    ALU, ACT, AX = mybir.AluOpType, mybir.ActivationFunctionType, mybir.AxisListType
    SCALE = HD ** -0.5
    ctx = ExitStack()
    with ctx:
        def sb(name, shape, dt=f32):
            return ctx.enter_context(nc.sbuf_tensor(name, shape, dt))

        def sem(name):
            return ctx.enter_context(nc.semaphore(name))

        COL = sb("COL", [P, CC, len(COLS)])
        MAT = sb("MAT", [P, len(MATS), P])
        WQ, WK, WV, WP0 = (sb(n, [P, CC, C]) for n in ("WQ", "WK", "WV", "WP0"))
        WDS = sb("WDS", [P, CC, 4, C])
        S16 = sb("S16", [16, 2 * C + 2])
        W1S = sb("W1S", [P, CC, 32])
        IPX, IPZ, XB, XC, WD, OPW = (sb(n, [P, CC, P]) for n in ("IPX", "IPZ", "XB", "XC", "WD", "OPW"))
        XPR, DTP = sb("XPR", [16, CC, P]), sb("DTP", [16, CC, P])
        WTAP = sb("WTAP", [P, CC, TAPS, P])
        WP1, W2Q, W2K, W2V, WP2 = (sb(n, [P, CC, C]) for n in ("WP1", "W2Q", "W2K", "W2V", "WP2"))
        ROWS = sb("ROWS", [1, 2 * C + 1])
        KIDX = sb("KIDX", [P, KPOOL + 1])
        EPS = sb("EPS", [P, 2])
        QBS, KB, VB, PB0, PB1, NEGA = (sb(n, [P, CC]) for n in ("QBS", "KB", "VB", "PB0", "PB1", "NEGA"))

        def mat(name):
            return MAT[:, MATS.index(name), :]

        def col(name, cc):
            return COL[:, cc, COLS.index(name):COLS.index(name) + 1]

        X0, XR, G, SQ = (sb(n, [P, CC, N]) for n in ("X0", "XR", "G", "SQ"))
        KST = sb("KST", [P, HEADS, NK], f16)
        PT = sb("PT", [P, 4, N])
        MEAN, VAR, RSTD = PT[:, 0, :], PT[:, 1, :], PT[:, 2, :]
        WORK = sb("WORK", [P, HEADS * N // 2])
        QST = WORK[:, :].bitcast(f16).rearrange("p (h n) -> p h n", h=HEADS)
        TA, TB = sb("TA", [P, CC, N]), sb("TB", [P, CC, N])
        U = WORK[:, 0:CC * N].rearrange("p (c n) -> p c n", c=CC)
        XNT = WORK[:, 0:QT * (C + 1)].rearrange("p (t c) -> p t c", t=QT)
        T1, PAT, WE = (WORK[:, QT * (C + 1) + n * CC * C:QT * (C + 1) + (n + 1) * CC * C]
                       .rearrange("p (c n) -> p c n", c=CC) for n in range(3))
        XNP = sb("XNP", [P, CC, H + 2, W + 2])
        VT = sb("VT", [P, 2, HEADS, HD + 1])
        XDS, KF = sb("XDS", [P, CC, NK]), sb("KF", [P, CC, NK])
        KH, KL = sb("KH", [P, CC, NK], f16), sb("KL", [P, CC, NK], f16)
        QF = TA
        QH, QL = (TB[:, n, :].bitcast(f16).rearrange("p (c n) -> p c n", c=CC) for n in range(2))
        OT, OC = TA[:, :, :].rearrange("p c n -> p (c n)").rearrange("p (t c) -> p t c", t=QT), TB
        NEGMAX = sb("NEGMAX", [P, HEADS, QT])
        MH, ML = sb("MH", [32, 2, P], f16), sb("ML", [32, 2, P], f16)
        RZ = sb("RZ", [P, QT])
        STAT, MSQ, MV = sb("STAT", [P, CC, 2, 6]), sb("MSQ", [P, CC, 4]), sb("MV", [P, CC, 2])
        GM, GA, GR, GB = sb("GM", [P, CC, 2]), sb("GA", [P, CC]), sb("GR", [P, CC]), sb("GB", [P, CC])
        GAP = sb("GAP", [P, CC])
        HM = sb("HM", [16, 1])
        GT, GS = sb("GT", [P, CC]), sb("GS", [P, CC])
        GRAM = sb("GRAM", [P, CC, C + 1])
        SROW = sb("SROW", [1, 2 * C])
        AB, AP_, ABD = sb("AB", [P, CC, HD]), sb("AP_", [P, CC, HD]), sb("ABD", [P, CC, P])
        AOK, AEX = sb("AOK", [P, CC, HD]), sb("AEX", [P, CC, HD])
        AMX, ASUM, ANN = sb("AMX", [P, CC]), sb("ASUM", [P, CC]), sb("ANN", [P, CC])
        BE = sb("BE", [P, CC])
        PA_, PB_ = sb("PA_", [P, CC * (H + 2), W + 2]), sb("PB_", [P, CC * (H + 2), W + 2])
        HB = sb("HB", [P, CC * (H + 2), W])
        PP = sb("PP", [P, CC * (H + 2) // 2, W])
        ACC, YK = sb("ACC", [P, CC, N]), sb("YK", [P, CC, N])
        SC, CGE, QS = sb("SC", [P, CC]), sb("CGE", [P, CC, KPOOL + 1]), sb("QS", [P, CC])
        FB, FS, EQ = sb("FB", [P, CC]), sb("FS", [P, CC]), sb("EQ", [P, CC, KPOOL])
        WKP, COEF, C0, C1 = sb("WKP", [P, CC, KPOOL]), sb("COEF", [P, CC, KPOOL]), sb("C0", [P, CC]), sb("C1", [P, CC])

        SLOT = {n: ctx.enter_context(nc.psum_tensor(n, [P, 2 * HALF], f32)) for n in ("SA0", "SA1", "SD0", "SD1")}

        pe = Steps(sem("pe_steps"), PE_STEPS)
        act = Steps(sem("act_steps"), ACT_STEPS)
        dve = Steps(sem("dve_steps"), DVE_STEPS)
        pool = Steps(sem("pool_steps"), POOL_STEPS)
        pe_set = Steps(sem("pe_setup_steps"), PE_SETUP)
        act_set = Steps(sem("act_setup_steps"), ACT_SETUP)
        dve_set = Steps(sem("dve_setup_steps"), DVE_SETUP)
        pool_set = Steps(sem("pool_setup_steps"), POOL_SETUP)
        dve_mp = Steps(sem("dve_maxpool_steps"), DVE_POOLS)
        act_mp = Steps(sem("act_maxpool_steps"), ACT_POOLS)
        add_mp = Steps(sem("pool_maxpool_steps"), ADD_POOLS)
        x_loaded, early_loaded, late_loaded = sem("x_loaded"), sem("early_weights_loaded"), sem("late_weights_loaded")
        stacked, maxed, stored = sem("q_k_stacked"), sem("max_rows_stacked"), sem("out_stored")
        EARLY, LATE = [], []
        STACK_DMAS, MAX_DMAS = 24, 4

        block = ctx.enter_context(nc.Block())

        def images(eng, first_turn, turn):
            first_turn(0)
            with eng.Fori(1, B) as b:
                turn(b)

        def first(b):
            return isinstance(b, int) and b == 0

        def interior(t, cc, dy=1, dx=1):
            r = cc * (H + 2) + dy
            return t[:, r:r + H, dx:dx + W]

        @block.sync
        def _(sp):
            x_v = x.rearrange("b (c p) h w -> p (b c) (h w)", p=P)
            out_v = out.rearrange("b (c p) h w -> p (b c) (h w)", p=P)
            sp.dma_start(X0[:, :, :], x_v[:, 0:CC, :]).then_inc(x_loaded, 16)
            for dst, src in ((MAT, mats), (COL, cols), (WK, wk), (WV, wv), (WP0, wp0), (WP1, wp1),
                             (XPR, xpr), (DTP, dtp), (WDS, wds), (WQ, wq)):
                sp.dma_start(dst[tuple(slice(None) for _ in dst.shape)], src).then_inc(early_loaded, 16)

            def stack(b):
                sp.wait_ge(*pool.at(b, "kl"))
                for j in range(4):
                    for quad, src in ((0, KH), (1, KH), (2, KL)):
                        sp.dma_start(KST[32 * quad:32 * quad + 32, j:HEADS:4, :], src[32 * j:32 * j + 32, :, :])\
                          .then_inc(stacked, 16)
                sp.wait_ge(*pool.at(b, "ql1"))
                for j in range(4):
                    for quad, src in ((0, QH), (1, QL), (2, QH)):
                        sp.dma_start(QST[32 * quad:32 * quad + 32, j:HEADS:4, :], src[32 * j:32 * j + 32, :, :])\
                          .then_inc(stacked, 16)
                for g in range(2):
                    sp.wait_ge(*dve.at(b, f"ml{g}"))
                    for r, src in ((96, MH), (97, ML)):
                        sp.dma_start(QST[r:r + 1, 4 * g:4 * g + 4, :].rearrange("a h (t q) -> a (h t) q", t=QT),
                                     src[:, g, :]).then_inc(maxed, 16)

            def store(b):
                sp.wait_ge(*add_mp.at(b, "add6"))
                sp.dma_start(out_v[:, bass.ds(b * CC, CC), :], ACC[:, :, :]).then_inc(stored, 16)

            def turn(b):
                stack(b)
                if not first(b):
                    store(b - 1)
                if first(b):
                    sp.wait_ge(*dve.at(b, "x1_1"))
                    sp.dma_start(X0[:, :, :], x_v[:, CC:2 * CC, :]).then_inc(x_loaded, 16)

            turn(0)
            with sp.Fori(1, B - 1) as b:
                turn(b)
                sp.wait_ge(*dve.at(b, "x1_1"))
                sp.dma_start(X0[:, :, :], x_v[:, bass.ds(b * CC + CC, CC), :]).then_inc(x_loaded, 16)
            turn(B - 1)
            store(B - 1)
            sp.wait_ge(stored, 16 * B)

        EARLY_N, LATE_N = 10, 14

        @block.scalar
        def _(e):
            for dst, src in ((S16, small16), (W1S, w1s), (IPX, ipx), (IPZ, ipz), (XB, xb), (XC, xc), (OPW, opw),
                             (W2Q, w2q), (W2K, w2k), (W2V, w2v), (WP2, wp2), (ROWS, rows), (KIDX, kidx)):
                e.dma_start(dst[tuple(slice(None) for _ in dst.shape)], src).then_inc(late_loaded, 16)
            e.dma_start(PT[:, 0:3, 0:768].rearrange("p a n -> p a n"), cw.partition_broadcast(P)).then_inc(late_loaded, 16)

            def table(n):
                e.add_instruction(mybir.InstLoadActFuncSet(act_func_set_id=n, name=nc.get_next_instruction_name(),
                                                           engine=mybir.EngineType.Activation))

            def group_norm(b, l):
                e.wait_ge(*dve.at(b, f"gn_var{l}"))
                e.activation(GR[:, :], GA[:, :], ACT.Ln, bias=EPS[:, 0:1]).then_inc(*act.step(f"gn_ln{l}"))
                e.wait_ge(*act.at(b, f"gn_ln{l}"))
                e.activation(GR[:, :], GR[:, :], ACT.Exp, scale=-0.5).then_inc(*act.step(f"gn_rstd{l}"))

            def squares(b, l, src, ready):
                for cc in range(CC):
                    e.wait_ge(*dve.at(b, ready[cc]))
                    e.activation(SQ[:, cc, :], src[:, cc, :], ACT.Square).then_inc(*act.step(f"sq{l}_{cc}"))

            def rstd(b, l, n=N):
                e.wait_ge(*dve.at(b, f"ln_var{l}"))
                e.activation(RSTD[:, 0:n], VAR[:, 0:n], ACT.Ln, bias=EPS[:, 0:1]).then_inc(*act.step(f"ln_ln{l}"))
                e.wait_ge(*act.at(b, f"ln_ln{l}"))
                e.activation(RSTD[:, 0:n], RSTD[:, 0:n], ACT.Exp, scale=-0.5).then_inc(*act.step(f"ln_rstd{l}"))

            def attention(b):
                group_norm(b, 0)
                e.wait_ge(*pe.at(b, "ds"))
                for cc in range(CC):
                    e.activation(XDS[:, cc, :], SLOT["SA0"][:, cc * NK:(cc + 1) * NK], ACT.Identity,
                                 bias=col("ds_b", cc)).then_inc(*act.step(f"xds{cc}"))
                e.wait_ge(*act.at(b, "xds1"))
                e.activation(SQ[:, 0, 0:CC * NK].rearrange("p (c n) -> p c n", c=CC), XDS[:, :, :],
                             ACT.Square).then_inc(*act.step("sq_ds"))
                for cc in range(CC):
                    e.wait_ge(*pe.at(b, f"q{cc}"))
                    e.activation(QF[:, cc, :], SLOT[f"SA{1 - cc}"][:, :], ACT.Identity, bias=QBS[:, cc:cc + 1],
                                 scale=SCALE).then_inc(*act.step(f"qf{cc}"))
                rstd(b, 0, NK)
                e.wait_ge(*pe.at(b, "k"))
                for cc in range(CC):
                    e.activation(KF[:, cc, :], SLOT["SA1"][:, cc * NK:(cc + 1) * NK], ACT.Identity,
                                 bias=KB[:, cc:cc + 1]).then_inc(*act.step(f"kf{cc}"))
                for h in range(HEADS):
                    if h >= 2:
                        e.wait_ge(*pe.at(b, f"pv{h - 2}"))
                    for kt in range(2):
                        e.wait_ge(*pe.at(b, f"st{h}_{kt}"))
                        e.activation(PT[:, 2 * (h % 2) + kt, :], SLOT[f"SA{kt}"][:, :], ACT.Exp)\
                         .then_inc(*act.step(f"p{h}_{kt}"))
                    if 1 <= h < 7:
                        maxpool(b, h)
                for cc in range(CC):
                    e.wait_ge(*pe.at(b, f"oT{cc}"))
                    e.activation(OC[:, cc, :], SLOT[f"SA{cc}"][:, :], ACT.Copy).then_inc(*act.step(f"oc{cc}"))

            def scan_block(b):
                group_norm(b, 1)
                squares(b, 1, G, ("g1_0", "g1_1"))
                rstd(b, 1)
                for g in range(GROUPS):
                    cc, lo = g // 2, 64 * (g % 2)
                    e.wait_ge(*dve.at(b, f"n1_{cc}"))
                    dst = XNP[lo:lo + 64, cc, 1:1 + H, 1:1 + W]
                    if g % 2:
                        dst = dst.rearrange("p h w -> p w h")
                    if g >= 2:
                        dst = dst[:, ::-1, ::-1]
                    e.activation(dst, G[lo:lo + 64, cc, :].rearrange("p (h w) -> p h w", h=H), ACT.Identity,
                                 bias=COL[lo:lo + 64, cc, COLS.index("ln_b"):COLS.index("ln_b") + 1],
                                 scale=COL[lo:lo + 64, cc, COLS.index("ln_g"):COLS.index("ln_g") + 1],
                                 accum_out=GAP[lo:lo + 64, cc:cc + 1]).then_inc(*act.step(f"xn{g}"))
                table(SILU_TABLE)
                for cc in range(CC):
                    e.wait_ge(*pe.at(b, f"xd{cc}"))
                    e.activation(U[:, cc, :], SLOT[f"SA{cc}"][:, :], ACT.Silu, bias=col("conv_b", cc))\
                     .then_inc(*act.step(f"u{cc}"))
                for cc in range(CC):
                    e.wait_ge(*pe.at(b, f"z{cc}"))
                    e.activation(TA[:, cc, :], SLOT[f"SA{cc}"][:, :], ACT.Silu).then_inc(*act.step(f"z{cc}"))
                table(EXP_LN_TABLE)
                e.wait_ge(*dve.at(b, "gate_in"))
                e.activation(GT[:, :], GT[:, :], ACT.Exp, scale=-1.0).then_inc(*act.step("gate_exp"))
                for cc in range(CC):
                    e.wait_ge(*pe.at(b, f"v{cc}"))
                    e.activation(PT[:, 2 * cc, :], SLOT[f"SA{cc}"][:, :], ACT.Identity, bias=col("dt_b", cc))\
                     .then_inc(*act.step(f"v{cc}"))
                for cc in range(CC):
                    e.wait_ge(*dve.at(b, f"vmin{cc}"))
                    e.activation(PT[:, 2 * cc + 1, :], PT[:, 2 * cc + 1, :], ACT.Exp).then_inc(*act.step(f"ev{cc}"))
                    e.wait_ge(*act.at(b, f"ev{cc}"))
                    e.activation(PT[:, 2 * cc + 1, :], PT[:, 2 * cc + 1, :], ACT.Ln, bias=EPS[:, 1:2])\
                     .then_inc(*act.step(f"lv{cc}"))
                for cc in range(CC):
                    e.wait_ge(*dve.at(b, f"delta{cc}"))
                    e.wait_ge(*act_set.at(0, "expA"))
                    e.activation(PT[:, 2 * cc + 1, :], PT[:, 2 * cc, :], ACT.Exp, scale=NEGA[:, cc:cc + 1])\
                     .then_inc(*act.step(f"dA{cc}"))
                for cc in range(CC):
                    e.wait_ge(*pe.at(b, f"yc{cc}"))
                    e.activation(TB[:, cc, :], SLOT[f"SA{cc}"][:, :], ACT.Copy).then_inc(*act.step(f"yc{cc}"))
                    e.activation(SQ[:, cc, :], SLOT[f"SA{cc}"][:, :], ACT.Square).then_inc(*act.step(f"ysq{cc}"))
                for cc in range(CC):
                    e.wait_ge(*pe.at(b, f"yv{cc}"))
                    e.activation(PT[:, cc, :], SLOT[f"SA{cc}"][:, :], ACT.Ln, bias=EPS[:, 0:1])\
                     .then_inc(*act.step(f"yln{cc}"))
                    e.wait_ge(*act.at(b, f"yln{cc}"))
                    e.activation(PT[:, cc, :], PT[:, cc, :], ACT.Exp, scale=-0.5).then_inc(*act.step(f"yrs{cc}"))
                squares(b, 2, TB, ("xm1", "xm3"))
                rstd(b, 2)

            def channel_block(b):
                group_norm(b, 2)
                squares(b, 3, G, ("g2_0", "g2_1"))
                rstd(b, 3)
                for t in range(2):
                    e.wait_ge(*pe.at(b, f"xnT{t}"))
                    e.activation(XNT[:, 4 * t:4 * t + 4, 0:C],
                                 SLOT[f"SA{t}"][:, :].rearrange("p (t c) -> p t c", t=4),
                                 ACT.Copy).then_inc(*act.step(f"xnt{t}"))
                e.wait_ge(*pe.at(b, "T1"))
                e.activation(T1[:, :, :], SLOT["SA0"][:, 0:CC * C].rearrange("p (c n) -> p c n", c=CC), ACT.Copy)\
                 .then_inc(*act.step("t1"))
                for cc in range(CC):
                    e.wait_ge(*dve.at(b, "amax"))
                    e.activation(AEX[:, cc, :], AB[:, cc, :], ACT.Exp, bias=AMX[:, cc:cc + 1],
                                 accum_out=ASUM[:, cc:cc + 1]).then_inc(*act.step(f"aexp{cc}"))
                e.wait_ge(*pe.at(b, "PAT"))
                e.activation(PAT[:, :, :], SLOT["SA1"][:, 0:CC * C].rearrange("p (c n) -> p c n", c=CC), ACT.Copy)\
                 .then_inc(*act.step("pat"))
                e.wait_ge(*pe.at(b, "WE"))
                e.activation(WE[:, :, :], SLOT["SA0"][:, 0:CC * C].rearrange("p (c n) -> p c n", c=CC), ACT.Copy)\
                 .then_inc(*act.step("we"))
                group_norm(b, 3)

            def maxpool_first(b):
                if not first(b):
                    e.wait_ge(stored, 16 * b)
                e.wait_ge(*dve.at(b, "coef"))
                for cc in range(CC):
                    e.activation(ACC[:, cc, :].rearrange("p (h w) -> p h w", h=H), interior(PA_, cc), ACT.Identity,
                                 bias=C1[:, cc:cc + 1], scale=C0[:, cc:cc + 1]).then_inc(*act_mp.step(f"a{cc}"))

            def maxpool_level(b, k):
                src = PA_ if k % 2 == 0 else PB_
                e.wait_ge(*dve_mp.at(b, f"v{k}_1"))
                if k > 1:
                    e.wait_ge(*add_mp.at(b, f"add{k - 1}"))
                elif not first(b):
                    e.wait_ge(*add_mp.at(b - 1, "add6"))
                for cc in range(CC):
                    e.activation(YK[:, cc, :].rearrange("p (h w) -> p h w", h=H), interior(src, cc), ACT.Copy,
                                 scale=COEF[:, cc, k:k + 1]).then_inc(*act_mp.step(f"y{k}_{cc}"))

            def maxpool(b, k):
                if first(b):
                    return
                if k == 1:
                    maxpool_first(b - 1)
                maxpool_level(b - 1, k)

            def turn(b):
                attention(b)
                scan_block(b)
                channel_block(b)

            table(EXP_LN_TABLE)
            e.wait_ge(early_loaded, 16 * EARLY_N)
            e.activation(NEGA[:, :], COL[:, :, COLS.index("A_log")], ACT.Exp).then_inc(*act_set.step("expA"))
            e.wait_ge(*act_set.at(0, "expA"))
            e.wait_ge(*dve_set.at(0, "eps0"))
            e.activation(NEGA[:, :], NEGA[:, :], ACT.Copy, scale=-1.0).then_inc(*act_set.step("negA"))
            e.wait_ge(*act_set.at(0, "negA"))
            e.wait_ge(*dve_set.at(0, "eps1"))
            images(e, turn, turn)
            maxpool_first(B - 1)
            for k in range(1, KPOOL):
                maxpool_level(B - 1, k)

        @block.gpsimd
        def _(e):
            e.memset(KST[96:98, :, :], 1.0).then_inc(*pool_set.step("kst1"))
            e.wait_ge(*pool_set.at(0, "kst1"))
            e.memset(VT[:, :, :, HD:HD + 1], 1.0).then_inc(*pool_set.step("vt1"))
            e.memset(ABD[:, :, :], 0.0).then_inc(*pool_set.step("abd"))
            e.memset(XNP[:, :, :, :], 0.0).then_inc(*pool_set.step("xnp"))
            for t, n in ((PA_, "pa"), (PB_, "pb"), (HB, "hb")):
                e.memset(t[:, :, :], LOWEST).then_inc(*pool_set.step(n))

            def maxpool(b):
                for k in range(1, KPOOL):
                    e.wait_ge(*act_mp.at(b, f"y{k}_1"))
                    if k > 1:
                        e.wait_ge(*add_mp.at(b, f"add{k - 1}"))
                    e.tensor_tensor(ACC[:, :, :], ACC[:, :, :], YK[:, :, :], ALU.add).then_inc(*add_mp.step(f"add{k}"))

            def split(b):
                for cc in range(CC):
                    e.wait_ge(*dve.at(b, f"qh{cc}"))
                    e.tensor_tensor(QL[:, cc, :], QF[:, cc, :], QH[:, cc, :], ALU.subtract)\
                     .then_inc(*pool.step(f"ql{cc}"))
                e.wait_ge(*dve.at(b, "kh"))
                e.tensor_tensor(KL[:, :, :], KF[:, :, :], KH[:, :, :], ALU.subtract).then_inc(*pool.step("kl"))

            def scan_block(b):
                for cc in range(CC):
                    e.wait_ge(*dve.at(b, f"delta{cc}"))
                    e.tensor_tensor(SQ[:, cc, :], PT[:, 2 * cc, :], U[:, cc, :], ALU.mult)\
                     .then_inc(*pool.step(f"du{cc}"))

            def turn(b):
                split(b)
                if not first(b):
                    maxpool(b - 1)
                scan_block(b)

            images(e, turn, turn)
            maxpool(B - 1)

        @block.vector
        def _(e):
            e.memset(EPS[:, 0:1], 1e-5).then_inc(*dve_set.step("eps0"))
            e.memset(EPS[:, 1:2], 1.0).then_inc(*dve_set.step("eps1"))
            e.wait_ge(early_loaded, 16 * EARLY_N)
            e.tensor_scalar(QBS[:, :], COL[:, :, COLS.index("q_b")], SCALE, None, ALU.mult).then_inc(*dve_set.step("qbs"))
            e.wait_ge(*pe_set.at(0, "fold"))
            FOLD = SLOT["SD0"]
            e.tensor_tensor(KB[:, :], FOLD[:, 0:2], COL[:, :, COLS.index("k_b")], ALU.add).then_inc(*dve_set.step("kb"))
            e.tensor_tensor(VB[:, :], FOLD[:, 2:4], COL[:, :, COLS.index("v_b")], ALU.add).then_inc(*dve_set.step("vb"))
            e.tensor_tensor(PB1[:, :], FOLD[:, 4:6], COL[:, :, COLS.index("pb1")], ALU.add).then_inc(*dve_set.step("pb1"))
            for cc in range(CC):
                for t, w, n in ((WK, "kv_ln_w", "wk"), (WV, "kv_ln_w", "wv"), (WP1, "ln_g", "wp1")):
                    e.tensor_scalar(t[:, cc, :], t[:, cc, :], col(w, cc), None, ALU.mult)\
                     .then_inc(*dve_set.step(f"{n}{cc}"))
            e.wait_ge(*pe_set.at(0, "wd"))
            e.tensor_copy(WD[:, :, :], SLOT["SD1"][:, 0:CC * P].rearrange("p (c n) -> p c n", c=CC)).then_inc(*dve_set.step("wd"))
            e.wait_ge(*pe_set.at(0, "fold0"))
            e.tensor_tensor(PB0[:, :], FOLD[:, 0:2], COL[:, :, COLS.index("pb0")], ALU.add).then_inc(*dve_set.step("pb0"))
            e.wait_ge(late_loaded, 16 * LATE_N)
            CW = PT[:, 0:3, 0:768].rearrange("p a (t d) -> p a t d", d=P)
            for cc in range(CC):
                for a in range(3):
                    lo, hi = max(6 * a, 9 * cc), min(6 * a + 6, 9 * cc + 9)
                    if lo < hi:
                        e.tensor_tensor(WTAP[:, cc, lo - 9 * cc:hi - 9 * cc, :],
                                        IPX[:, cc, :].unsqueeze(1).broadcast_to([P, hi - lo, P]),
                                        CW[:, a, lo - 6 * a:hi - 6 * a, :], ALU.mult).then_inc(*dve_set.step(f"wtap{cc}_{a}"))

            def group_norm(b, l, src, dst):
                for cc in range(CC):
                    for half in range(2):
                        e.bn_stats(STAT[:, cc, half, :], src(cc, half)).then_inc(*dve.step(f"gn_st{l}_{cc}{half}"))
                means, m2s = (STAT[:, :, :, :].rearrange("p c a (s t) -> p c (a s) t", t=3)[:, :, :, n] for n in (1, 2))
                e.wait_ge(*dve.at(b, f"gn_st{l}_11"))
                e.tensor_tensor(MSQ[:, :, :], means, means, ALU.mult).then_inc(*dve.step(f"gn_m2{l}"))
                e.tensor_reduce(MV[:, :, 0], means, AX.X, ALU.add).then_inc(*dve.step(f"gn_m{l}"))
                e.wait_ge(*dve.at(b, f"gn_m2{l}"))
                e.scalar_tensor_tensor(out=MSQ[:, :, :], in0=m2s, scalar=4.0 / N, in1=MSQ[:, :, :], op0=ALU.mult,
                                       op1=ALU.add).then_inc(*dve.step(f"gn_sq{l}"))
                e.wait_ge(*dve.at(b, f"gn_sq{l}"))
                e.tensor_reduce(MV[:, :, 1], MSQ[:, :, :], AX.X, ALU.add).then_inc(*dve.step(f"gn_ex2{l}"))
                if l == 3:
                    e.tensor_scalar(GAP[:, :], MV[:, :, 0], 0.25, None, ALU.mult).then_inc(*dve.step("gap3"))
                e.wait_ge(*pe.at(b, f"gn{l}"))
                e.tensor_copy(GM[:, :, :], SLOT["SD0"][:, 0:4].rearrange("p (c s) -> p c s", c=CC)).then_inc(*dve.step(f"gn_gm{l}"))
                e.wait_ge(*dve.at(b, f"gn_gm{l}"))
                e.tensor_tensor(GA[:, :], GM[:, :, 0], GM[:, :, 0], ALU.mult).then_inc(*dve.step(f"gn_gm2{l}"))
                e.wait_ge(*dve.at(b, f"gn_gm2{l}"))
                e.tensor_tensor(GA[:, :], GM[:, :, 1], GA[:, :], ALU.subtract).then_inc(*dve.step(f"gn_var{l}"))
                e.wait_ge(*act.at(b, f"gn_rstd{l}"))
                e.scalar_tensor_tensor(out=GB[:, :], in0=GM[:, :, 0], scalar=-1.0, in1=GR[:, :], op0=ALU.mult,
                                       op1=ALU.mult).then_inc(*dve.step(f"gn_b{l}"))
                e.wait_ge(*dve.at(b, f"gn_b{l}"))
                if dst is not None:
                    for cc in range(CC):
                        e.tensor_scalar(G[:, cc, :], dst(cc), GR[:, cc:cc + 1], GB[:, cc:cc + 1], ALU.mult, ALU.add)\
                         .then_inc(*dve.step(f"g{l}_{cc}"))

            def layer_norm(b, l, t, n, lo_mean, lo_sq):
                e.wait_ge(*pe.at(b, f"mean{l}"))
                e.tensor_copy(MEAN[:, 0:n], lo_mean).then_inc(*dve.step(f"ln_mean{l}"))
                e.wait_ge(*dve.at(b, f"ln_mean{l}"))
                e.scalar_tensor_tensor(out=VAR[:, 0:n], in0=MEAN[:, 0:n], scalar=-1.0, in1=MEAN[:, 0:n], op0=ALU.mult,
                                       op1=ALU.mult).then_inc(*dve.step(f"ln_m2{l}"))
                e.wait_ge(*dve.at(b, f"ln_m2{l}"))
                e.wait_ge(*pe.at(b, f"msq{l}"))
                e.tensor_tensor(VAR[:, 0:n], VAR[:, 0:n], lo_sq, ALU.add).then_inc(*dve.step(f"ln_var{l}"))
                for cc in range(CC):
                    e.tensor_tensor(t[:, cc, :], t[:, cc, :], MEAN[:, 0:n], ALU.subtract).then_inc(*dve.step(f"c{l}_{cc}"))
                e.wait_ge(*act.at(b, f"ln_rstd{l}"))
                for cc in range(CC):
                    e.wait_ge(*dve.at(b, f"c{l}_{cc}"))
                    e.tensor_tensor(t[:, cc, :], t[:, cc, :], RSTD[:, 0:n], ALU.mult).then_inc(*dve.step(f"n{l}_{cc}"))

            def attention(b):
                e.wait_ge(x_loaded, 16 * b + 16)
                group_norm(b, 0, lambda cc, h: X0[:, cc, h * HALF:(h + 1) * HALF], lambda cc: X0[:, cc, :])
                layer_norm(b, 0, XDS, NK, SLOT["SD0"][:, 0:NK], SLOT["SD0"][:, HALF:HALF + NK])
                for cc in range(CC):
                    e.wait_ge(*act.at(b, f"qf{cc}"))
                    e.tensor_copy(QH[:, cc, :], QF[:, cc, :]).then_inc(*dve.step(f"qh{cc}"))
                e.wait_ge(*act.at(b, "kf1"))
                e.tensor_copy(KH[:, :, :], KF[:, :, :]).then_inc(*dve.step("kh"))
                e.wait_ge(*pe.at(b, "vT"))
                e.tensor_copy(VT[:, :, :, 0:HD],
                              SLOT["SD1"][:, 0:2 * C].rearrange("p (k h d) -> p k h d", k=2, h=HEADS)).then_inc(*dve.step("vt"))

                def maxima(h):
                    for half in range(2):
                        e.wait_ge(*pe.at(b, f"s{h}_{half}"))
                        e.tensor_reduce(NEGMAX[:, h, 4 * half:4 * half + 4],
                                        SLOT[f"SD{half}"][:, :].rearrange("p (t k) -> p t k", t=4), AX.X, ALU.max,
                                        negate=True).then_inc(*dve.step(f"mx{h}_{half}"))

                def max_rows(g):
                    e.wait_ge(*pe.at(b, f"mT{g}"))
                    e.tensor_copy(MH[:, g, :], SLOT["SD0"][0:32, 0:P]).then_inc(*dve.step(f"mh{g}"))
                    e.wait_ge(*dve.at(b, f"mh{g}"))
                    e.tensor_tensor(ML[:, g, :], SLOT["SD0"][0:32, 0:P], MH[:, g, :], ALU.subtract).then_inc(*dve.step(f"ml{g}"))

                def weighted(h):
                    e.wait_ge(*pe.at(b, f"pv{h}"))
                    o = SLOT["SD1"][:, 0:QT * (HD + 1)].rearrange("p (t d) -> p t d", t=QT)
                    e.reciprocal(RZ[:, :], o[:, :, HD]).then_inc(*dve.step(f"rz{h}"))
                    e.wait_ge(*dve.at(b, f"rz{h}"))
                    e.tensor_tensor(OT[:, :, h * HD:(h + 1) * HD], o[:, :, 0:HD],
                                    RZ[:, :].unsqueeze(2).broadcast_to([P, QT, HD]), ALU.mult).then_inc(*dve.step(f"o{h}"))

                for h in range(4):
                    maxima(h)
                max_rows(0)
                for h in range(HEADS):
                    if h < 4:
                        maxima(4 + h)
                        if h == 3:
                            max_rows(1)
                    if h >= 1:
                        weighted(h - 1)
                    if 1 <= h < 7 and not first(b):
                        maxpool_level(b - 1, h)
                weighted(HEADS - 1)
                for cc in range(CC):
                    e.wait_ge(*pe.at(b, f"proj0_{cc}"))
                    e.scalar_tensor_tensor(out=XR[:, cc, :], in0=SLOT[f"SD{cc}"][:, :], scalar=PB0[:, cc:cc + 1],
                                           in1=X0[:, cc, :], op0=ALU.add, op1=ALU.add).then_inc(*dve.step(f"x1_{cc}"))

            def scan_block(b):
                e.wait_ge(*dve.at(b, "x1_1"))
                group_norm(b, 1, lambda cc, h: XR[:, cc, h * HALF:(h + 1) * HALF], lambda cc: XR[:, cc, :])
                layer_norm(b, 1, G, N, SLOT["SD1"][:, :], SLOT["SD0"][:, :])
                e.wait_ge(*act.at(b, "xn3"))
                e.tensor_scalar(GAP[:, :], GAP[:, :], 1.0 / N, None, ALU.mult).then_inc(*dve.step("gap1"))
                e.wait_ge(*pe.at(b, "fc1"))
                e.tensor_scalar(HM[:, :], SLOT["SD0"][0:16, 0:1], S16[:, 2 * C:2 * C + 1], 0.0, ALU.add, ALU.max)\
                 .then_inc(*dve.step("hm1"))
                e.wait_ge(*pe.at(b, "fc2"))
                e.tensor_tensor(GT[:, :], SLOT["SD1"][:, 0:2], COL[:, :, COLS.index("fc2_b")], ALU.add).then_inc(*dve.step("gate_in"))
                e.wait_ge(*act.at(b, "gate_exp"))
                e.tensor_scalar(GT[:, :], GT[:, :], 1.0, None, ALU.add).then_inc(*dve.step("gate_1p"))
                e.wait_ge(*dve.at(b, "gate_1p"))
                e.reciprocal(GS[:, :], GT[:, :]).then_inc(*dve.step("gate"))
                e.wait_ge(*dve.at(b, "gate"))
                e.tensor_tensor(GS[:, :], GS[:, :], COL[:, :, COLS.index("skip")], ALU.mult).then_inc(*dve.step("gs"))
                for cc in range(CC):
                    e.wait_ge(*act.at(b, f"v{cc}"))
                    e.tensor_scalar(PT[:, 2 * cc + 1, :], PT[:, 2 * cc, :], SOFTPLUS_LINEAR, None, ALU.min)\
                     .then_inc(*dve.step(f"vmin{cc}"))
                for cc in range(CC):
                    e.wait_ge(*act.at(b, f"lv{cc}"))
                    e.tensor_tensor(PT[:, 2 * cc, :], PT[:, 2 * cc, :], PT[:, 2 * cc + 1, :], ALU.max)\
                     .then_inc(*dve.step(f"delta{cc}"))
                for cc in range(CC):
                    e.wait_ge(*pool.at(b, f"du{cc}"))
                    e.wait_ge(*pe.at(b, f"B{cc}"))
                    e.tensor_tensor(SQ[:, cc, :], SQ[:, cc, :], SLOT["SD0"][:, :], ALU.mult).then_inc(*dve.step(f"dbu{cc}"))
                    e.wait_ge(*dve.at(b, f"dbu{cc}"))
                    e.wait_ge(*act.at(b, f"dA{cc}"))
                    e.tensor_tensor_scan(PT[:, 2 * cc, :], PT[:, 2 * cc + 1, :], SQ[:, cc, :], 0.0, ALU.mult, ALU.add)\
                     .then_inc(*dve.step(f"scan{cc}"))
                    e.wait_ge(*dve.at(b, f"scan{cc}"))
                    e.wait_ge(*pe.at(b, f"C{cc}"))
                    e.tensor_tensor(PT[:, 2 * cc, :], PT[:, 2 * cc, :], SLOT["SD1"][:, :], ALU.mult).then_inc(*dve.step(f"hc{cc}"))
                    e.wait_ge(*dve.at(b, f"hc{cc}"))
                    e.scalar_tensor_tensor(out=U[:, cc, :], in0=U[:, cc, :], scalar=col("Ds", cc), in1=PT[:, 2 * cc, :],
                                           op0=ALU.mult, op1=ALU.add).then_inc(*dve.step(f"y{cc}"))
                for cc in range(CC):
                    e.wait_ge(*act.at(b, f"yrs{cc}"))
                    e.tensor_tensor(TB[:, cc, :], TB[:, cc, :], PT[:, cc, :], ALU.mult).then_inc(*dve.step(f"yn{cc}"))
                    e.wait_ge(*dve.at(b, f"yn{cc}"))
                    e.tensor_scalar(TB[:, cc, :], TB[:, cc, :], col("og", cc), col("ob", cc), ALU.mult, ALU.add)\
                     .then_inc(*dve.step(f"ya{cc}"))
                    e.wait_ge(*dve.at(b, f"ya{cc}"))
                    e.tensor_tensor(TA[:, cc, :], TB[:, cc, :], TA[:, cc, :], ALU.mult).then_inc(*dve.step(f"yz{cc}"))
                for g in range(GROUPS):
                    cc, lo = g // 2, 64 * (g % 2)
                    e.wait_ge(*pe.at(b, f"op{cc}"))
                    dst = TB[lo:lo + 64, cc, :].rearrange("p (h w) -> p h w", h=H)
                    if g % 2:
                        dst = dst.rearrange("p h w -> p w h")
                    if g >= 2:
                        dst = dst[:, ::-1, ::-1]
                    e.scalar_tensor_tensor(out=dst, in0=SLOT[f"SD{cc}"][lo:lo + 64, :].rearrange("p (h w) -> p h w", h=H),
                                           scalar=GS[lo:lo + 64, cc:cc + 1], in1=XNP[lo:lo + 64, cc, 1:1 + H, 1:1 + W],
                                           op0=ALU.mult, op1=ALU.mult).then_inc(*dve.step(f"xm{g}"))
                e.wait_ge(*dve.at(b, "xm3"))
                layer_norm(b, 2, TB, N, SLOT["SD0"][:, :], SLOT["SD1"][:, :])
                for cc in range(CC):
                    e.wait_ge(*pe.at(b, f"proj1_{cc}"))
                    e.scalar_tensor_tensor(out=XR[:, cc, :], in0=SLOT[f"SD{cc}"][:, :], scalar=PB1[:, cc:cc + 1],
                                           in1=XR[:, cc, :], op0=ALU.add, op1=ALU.add).then_inc(*dve.step(f"x2_{cc}"))

            def channel_block(b):
                e.wait_ge(*dve.at(b, "x2_1"))
                group_norm(b, 2, lambda cc, h: XR[:, cc, h * HALF:(h + 1) * HALF], lambda cc: XR[:, cc, :])
                layer_norm(b, 3, G, N, SLOT["SD1"][:, :], SLOT["SD0"][:, :])
                if True:
                    e.memset(XNT[:, :, C:C + 1], 1.0).then_inc(*dve.step("xnt_ones"))
                e.wait_ge(*pe.at(b, "gram"))
                e.tensor_copy(GRAM[:, :, :], SLOT["SD0"][:, :].rearrange("p (c n) -> p c n", c=CC)[:, :, 0:C + 1])\
                 .then_inc(*dve.step("gram"))
                e.wait_ge(*pe.at(b, "rows"))
                e.tensor_copy(SROW[:, :], SLOT["SD1"][0:1, 0:2 * C]).then_inc(*dve.step("srow"))
                e.wait_ge(*pe.at(b, "A"))
                S = SLOT["SD0"][:, 0:CC * P].rearrange("p (c j) -> p c j", c=CC)
                for j in range(4):
                    blk = slice(HD * j, HD * j + HD)
                    e.tensor_scalar(AB[blk, :, :], S[blk, :, blk], SCALE, 50.0, ALU.mult, ALU.min).then_inc(*dve.step(f"ab{j}"))
                    e.tensor_copy(AOK[blk, :, :], S[blk, :, blk]).then_inc(*dve.step(f"aok{j}"))
                e.wait_ge(*dve.at(b, "aok3"))
                e.tensor_scalar(AB[:, :, :], AB[:, :, :], -50.0, None, ALU.max).then_inc(*dve.step("aclip"))
                e.tensor_tensor(AOK[:, :, :], AOK[:, :, :], AOK[:, :, :], ALU.is_equal).then_inc(*dve.step("anan"))
                e.wait_ge(*dve.at(b, "anan"))
                e.tensor_reduce(ANN[:, :], AOK[:, :, :], AX.X, ALU.min).then_inc(*dve.step("arow"))
                e.tensor_reduce(AMX[:, :], AB[:, :, :], AX.X, ALU.max, negate=True).then_inc(*dve.step("amax"))
                e.wait_ge(*act.at(b, "aexp1"))
                e.reciprocal(ASUM[:, :], ASUM[:, :]).then_inc(*dve.step("arec"))
                e.wait_ge(*dve.at(b, "arec"))
                e.tensor_tensor(ASUM[:, :], ASUM[:, :], ANN[:, :], ALU.mult).then_inc(*dve.step("arok"))
                e.tensor_scalar(ANN[:, :], ANN[:, :], -1.0 / HD, 1.0 / HD, ALU.mult, ALU.add).then_inc(*dve.step("afill"))
                e.wait_ge(*dve.at(b, "afill"))
                for cc in range(CC):
                    e.tensor_scalar(AP_[:, cc, :], AEX[:, cc, :], ASUM[:, cc:cc + 1], ANN[:, cc:cc + 1], ALU.mult, ALU.add)\
                     .then_inc(*dve.step(f"ap{cc}"))
                e.wait_ge(*dve.at(b, "ap1"))
                for j in range(4):
                    blk = slice(HD * j, HD * j + HD)
                    e.tensor_copy(ABD[blk, :, blk], AP_[blk, :, :]).then_inc(*dve.step(f"abd{j}"))
                e.wait_ge(*pe.at(b, "be"))
                e.tensor_tensor(BE[:, :], SLOT["SD1"][:, 0:2], COL[:, :, COLS.index("pb2")], ALU.add).then_inc(*dve.step("be"))
                e.wait_ge(*dve.at(b, "be"))
                if not first(b):
                    e.wait_ge(*act_mp.at(b - 1, "y6_1"))
                for cc in range(CC):
                    e.wait_ge(*pe.at(b, f"out{cc}"))
                    e.scalar_tensor_tensor(out=interior(PA_, cc), in0=SLOT[f"SD{cc}"][:, :].rearrange("p (h w) -> p h w", h=H),
                                           scalar=BE[:, cc:cc + 1], in1=XR[:, cc, :].rearrange("p (h w) -> p h w", h=H),
                                           op0=ALU.add, op1=ALU.add).then_inc(*dve.step(f"x3_{cc}"))
                e.wait_ge(*dve.at(b, "x3_1"))
                group_norm(b, 3, lambda cc, h: PA_[:, cc * (H + 2) + 1 + 16 * h:cc * (H + 2) + 17 + 16 * h, 1:1 + W], None)
                e.tensor_tensor(GAP[:, :], GAP[:, :], GR[:, :], ALU.mult).then_inc(*dve.step("gap3a"))
                e.wait_ge(*dve.at(b, "gap3a"))
                e.tensor_tensor(GAP[:, :], GAP[:, :], GB[:, :], ALU.add).then_inc(*dve.step("gap3b"))
                e.wait_ge(*pe.at(b, "w1"))
                e.tensor_scalar(HM[:, :], SLOT["SD0"][0:16, 0:1], S16[:, 2 * C + 1:2 * C + 2], 0.0, ALU.add, ALU.max)\
                 .then_inc(*dve.step("hm3"))
                e.wait_ge(*pe.at(b, "w2"))
                e.tensor_tensor(SC[:, :], SLOT["SD1"][:, 0:2], COL[:, :, COLS.index("w2_b")], ALU.add).then_inc(*dve.step("sc0"))
                e.wait_ge(*dve.at(b, "sc0"))
                e.tensor_scalar(SC[:, :], SC[:, :], 0.0, None, ALU.max).then_inc(*dve.step("sc"))
                e.wait_ge(*dve.at(b, "sc"))
                for cc in range(CC):
                    e.tensor_scalar(CGE[:, cc, :], KIDX[:, :], SC[:, cc:cc + 1], None, ALU.is_le).then_inc(*dve.step(f"cge{cc}"))
                e.wait_ge(*dve.at(b, "cge1"))
                e.tensor_reduce(QS[:, :], CGE[:, :, 1:6], AX.X, ALU.add).then_inc(*dve.step("qs"))
                e.tensor_tensor(EQ[:, :, :], CGE[:, :, 0:KPOOL], CGE[:, :, 1:KPOOL + 1], ALU.subtract).then_inc(*dve.step("eq"))
                e.wait_ge(*dve.at(b, "eq"))
                e.tensor_tensor(FB[:, :], SC[:, :], QS[:, :], ALU.subtract).then_inc(*dve.step("fb"))
                e.wait_ge(*dve.at(b, "fb"))
                e.tensor_scalar(FS[:, :], QS[:, :], 1.0, None, ALU.add).then_inc(*dve.step("fs0"))
                e.wait_ge(*dve.at(b, "fs0"))
                e.tensor_tensor(FS[:, :], FS[:, :], SC[:, :], ALU.subtract).then_inc(*dve.step("fs"))
                e.wait_ge(*dve.at(b, "fs"))
                for cc in range(CC):
                    e.tensor_scalar(WKP[:, cc, :], EQ[:, cc, :], FS[:, cc:cc + 1], None, ALU.mult).then_inc(*dve.step(f"ws{cc}"))
                e.wait_ge(*dve.at(b, "ws1"))
                for cc in range(CC):
                    e.scalar_tensor_tensor(out=WKP[:, cc, 1:KPOOL], in0=EQ[:, cc, 0:KPOOL - 1], scalar=FB[:, cc:cc + 1],
                                           in1=WKP[:, cc, 1:KPOOL], op0=ALU.mult, op1=ALU.add).then_inc(*dve.step(f"wb{cc}"))
                e.wait_ge(*dve.at(b, "wb1"))
                for cc in range(CC):
                    e.tensor_scalar(COEF[:, cc, :], WKP[:, cc, :], GR[:, cc:cc + 1], None, ALU.mult).then_inc(*dve.step(f"cf{cc}"))
                e.tensor_scalar(C1[:, :], GB[:, :], 2.0, None, ALU.mult).then_inc(*dve.step("c1"))
                e.wait_ge(*dve.at(b, "c1"))
                e.tensor_tensor(C0[:, :], COEF[:, :, 0], GR[:, :], ALU.add).then_inc(*dve.step("c0"))
                e.wait_ge(*dve.at(b, "c0"))
                e.tensor_scalar(C0[:, :], C0[:, :], 1.0, None, ALU.add).then_inc(*dve.step("coef"))

            def maxpool_level(b, k):
                src, dst = (PA_, PB_) if k % 2 else (PB_, PA_)
                R = CC * (H + 2)
                if k == 1:
                    e.wait_ge(*dve.at(b, "x3_1"))
                else:
                    e.wait_ge(*dve_mp.at(b, f"v{k - 1}_1"))
                pair = PP[:, 0:R // 2, :].rearrange("p a (b j) -> p (a b) j", j=W // 2)
                e.tensor_tensor(pair[:, 0:R - 2, :], src[:, 1:R - 1, 1:1 + W:2], src[:, 1:R - 1, 2:2 + W:2], ALU.max)\
                 .then_inc(*dve_mp.step(f"hp{k}"))
                e.wait_ge(*dve_mp.at(b, f"hp{k}"))
                for s in range(2):
                    e.tensor_tensor(HB[:, 1:R - 1, s:W:2], src[:, 1:R - 1, 3 * s:3 * s + W - 1:2], pair[:, 0:R - 2, :], ALU.max)\
                     .then_inc(*dve_mp.step(f"h{k}_{s}"))
                e.wait_ge(*dve_mp.at(b, f"h{k}_1"))
                e.tensor_tensor(PP[:, 0:R // 2 - 1, :], HB[:, 1:R - 1:2, :], HB[:, 2:R:2, :], ALU.max).then_inc(*dve_mp.step(f"vp{k}"))
                e.wait_ge(*dve_mp.at(b, f"vp{k}"))
                if k >= 2:
                    e.wait_ge(*act_mp.at(b, f"y{k - 2}_1" if k > 2 else "a1"))
                for cc in range(CC):
                    lo = cc * (H + 2)
                    for s in range(2):
                        e.tensor_tensor(dst[:, lo + 1 + s:lo + 1 + H:2, 1:1 + W],
                                        HB[:, lo + 3 * s:lo + 3 * s + H - 1:2, :],
                                        PP[:, lo // 2:lo // 2 + H // 2, :], ALU.max)\
                         .then_inc(*dve_mp.step(f"v{k}_{cc}" if s else f"u{k}_{cc}"))

            def turn(b):
                attention(b)
                scan_block(b)
                channel_block(b)

            e.wait_ge(*pool_set.at(0, "hb"))
            images(e, turn, turn)
            for k in range(1, KPOOL):
                maxpool_level(B - 1, k)

        @block.tensor
        def _(e):
            e.wait_ge(early_loaded, 16 * EARLY_N)

            def columns(slot, at, w, name_or_tile):
                for m in range(CC):
                    for cc in range(CC):
                        v = col(name_or_tile, cc) if isinstance(name_or_tile, str) else name_or_tile[:, cc:cc + 1]
                        mm = e.matmul(SLOT[slot][:, at + m:at + m + 1], w[:, cc, m * P:(m + 1) * P], v,
                                      start=(cc == 0), stop=(cc == CC - 1))
                return mm

            columns("SD0", 0, WK, "kv_ln_b")
            columns("SD0", 2, WV, "kv_ln_b")
            columns("SD0", 4, WP1, "ln_b").then_inc(*pe_set.step("fold"))
            for cc in range(CC):
                mm = e.matmul(SLOT["SD1"][:, cc * P:(cc + 1) * P], XPR[:, cc, :], DTP[:, cc, :], start=True, stop=True)
            mm.then_inc(*pe_set.step("wd"))
            e.wait_ge(*dve_set.at(0, "pb1"))
            columns("SD0", 0, WP0, VB).then_inc(*pe_set.step("fold0"))

            state = {}

            def take(b, slot, engine, label, last):
                if slot in state:
                    who, what, prev = state[slot]
                    e.wait_ge(*who.at(b, what))
                elif not first(b):
                    e.wait_ge(*LAST[slot][0].at(b - 1, LAST[slot][1]))
                else:
                    if slot == "SD0":
                        e.wait_ge(*dve_set.at(0, "pb0"))
                    if slot == "SD1":
                        e.wait_ge(*dve_set.at(0, "wd"))
                state[slot] = (engine, label, last)
                return SLOT[slot]

            LAST = {"SA0": (act, "we"), "SA1": (act, "pat"), "SD0": (dve, "hm3"), "SD1": (dve, "sc0")}

            def group_norm(b, l):
                s = take(b, "SD0", dve, f"gn_gm{l}", 0)
                e.wait_ge(*dve.at(b, f"gn_ex2{l}"))
                e.matmul(s[:, 0:4], mat("mean_group"), MV[:, :, :].rearrange("p c s -> p (c s)"), start=True, stop=True)\
                 .then_inc(*pe.step(f"gn{l}"))

            def project(s, w, src, m):
                for half in range(2):
                    for cc in range(CC):
                        mm = e.matmul(s[:, half * HALF:(half + 1) * HALF], w[:, cc, m * P:(m + 1) * P],
                                      src[:, cc, half * HALF:(half + 1) * HALF], start=(cc == 0), stop=(cc == CC - 1))
                return mm

            def spread_sum(s, w, src):
                for half in range(2):
                    for cc in range(CC):
                        mm = e.matmul(s[:, half * HALF:(half + 1) * HALF], w, src[:, cc, half * HALF:(half + 1) * HALF],
                                      start=(cc == 0), stop=(cc == CC - 1))
                return mm

            def layer_norm(b, l, src, slots, ready):
                s = take(b, slots[0], dve, f"ln_mean{l}", 0)
                e.wait_ge(*dve.at(b, ready))
                spread_sum(s, mat("mean256"), src).then_inc(*pe.step(f"mean{l}"))
                s = take(b, slots[1], dve, f"ln_var{l}", 0)
                e.wait_ge(*act.at(b, f"sq{l}_1"))
                spread_sum(s, mat("mean256"), SQ).then_inc(*pe.step(f"msq{l}"))

            def attention(b):
                group_norm(b, 0)
                s = take(b, "SA0", act, "xds1", 0)
                e.wait_ge(*dve.at(b, "g0_1"))
                for m in range(CC):
                    for n in range(4 * CC):
                        cc, dy, dx = n // 4, n % 4 // 2, n % 2
                        src = G[:, cc, :].rearrange("p (h w) -> p h w", h=H)[:, dy::2, dx::2]
                        mm = e.matmul(s[:, m * NK:(m + 1) * NK], WDS[:, cc, n % 4, m * P:(m + 1) * P], src,
                                      start=(n == 0), stop=(n == 4 * CC - 1))
                mm.then_inc(*pe.step("ds"))
                for m in range(CC):
                    s = take(b, f"SA{1 - m}", act, f"qf{m}", 0)
                    project(s, WQ, G, m).then_inc(*pe.step(f"q{m}"))
                s = take(b, "SD0", dve, "ln_var0", 0)
                e.wait_ge(*act.at(b, "sq_ds"))
                for at, src in ((0, XDS), (HALF, SQ[:, 0, 0:CC * NK].rearrange("p (c n) -> p c n", c=CC))):
                    for cc in range(CC):
                        mm = e.matmul(s[:, at:at + NK], mat("mean256"), src[:, cc, :], start=(cc == 0), stop=(cc == CC - 1))
                    if at == 0:
                        mm.then_inc(*pe.step("mean0"))
                mm.then_inc(*pe.step("msq0"))
                s = take(b, "SA1", act, "kf1", 0)
                e.wait_ge(*dve.at(b, "n0_1"))
                if first(b):
                    e.wait_ge(*dve_set.at(0, "wp11"))
                for m in range(CC):
                    for cc in range(CC):
                        mm = e.matmul(s[:, m * NK:(m + 1) * NK], WK[:, cc, m * P:(m + 1) * P], XDS[:, cc, :],
                                      start=(cc == 0), stop=(cc == CC - 1))
                mm.then_inc(*pe.step("k"))
                s = take(b, "SD1", dve, "vt", 0)
                for kt in range(2):
                    for cc in range(CC):
                        mm = e.matmul(s[:, kt * C:(kt + 1) * C], XDS[:, cc, kt * P:(kt + 1) * P], WV[:, cc, :],
                                      start=(cc == 0), stop=(cc == CC - 1))
                mm.then_inc(*pe.step("vT"))
                e.wait_ge(stacked, 16 * STACK_DMAS * b + 16 * STACK_DMAS)
                if first(b):
                    e.wait_ge(*pool_set.at(0, "vt1"))

                def scores(h):
                    for half in range(2):
                        s = take(b, f"SD{half}", dve, f"mx{h}_{half}", 0)
                        for t in range(4):
                            qt = 4 * half + t
                            mm = e.matmul(s[:, t * NK:(t + 1) * NK], QST[0:96, h, qt * P:(qt + 1) * P], KST[0:96, h, :],
                                          start=True, stop=True)
                        mm.then_inc(*pe.step(f"s{h}_{half}"))

                def max_rows(g):
                    s = take(b, "SD0", dve, f"ml{g}", 0)
                    e.wait_ge(*dve.at(b, f"mx{4 * g + 3}_1"))
                    e.transpose(s[0:32, 0:P], NEGMAX[:, 4 * g:4 * g + 4, :].rearrange("p h t -> p (h t)"), mat("ident"))\
                     .then_inc(*pe.step(f"mT{g}"))

                def scores_t(h):
                    if h % 4 == 0:
                        e.wait_ge(maxed, 16 * MAX_DMAS * b + 16 * 2 * (h // 4 + 1))
                    for kt in range(2):
                        s = take(b, f"SA{kt}", act, f"p{h}_{kt}", 0)
                        for half in range(2):
                            mm = e.matmul(s[:, half * HALF:(half + 1) * HALF], KST[0:98, h, kt * P:(kt + 1) * P],
                                          QST[0:98, h, half * HALF:(half + 1) * HALF], start=True, stop=True)
                        mm.then_inc(*pe.step(f"st{h}_{kt}"))

                def weighted(h):
                    s = take(b, "SD1", dve, f"o{h}", 0)
                    e.wait_ge(*act.at(b, f"p{h}_1"))
                    for qt in range(QT):
                        for kt in range(2):
                            mm = e.matmul(s[:, qt * (HD + 1):(qt + 1) * (HD + 1)],
                                          PT[:, 2 * (h % 2) + kt, qt * P:(qt + 1) * P], VT[:, kt, h, :],
                                          start=(kt == 0), stop=(kt == 1))
                    mm.then_inc(*pe.step(f"pv{h}"))

                for h in range(4):
                    scores(h)
                max_rows(0)
                for h in range(HEADS):
                    if h < 4:
                        scores(4 + h)
                        if h == 3:
                            max_rows(1)
                    scores_t(h)
                    if h >= 1:
                        weighted(h - 1)
                weighted(HEADS - 1)
                for cc in range(CC):
                    s = take(b, f"SA{cc}", act, f"oc{cc}", 0)
                    e.wait_ge(*dve.at(b, f"o{4 * cc + 3}"))
                    for qt in range(QT):
                        mm = e.transpose(s[:, qt * P:(qt + 1) * P], OT[:, qt, cc * P:(cc + 1) * P], mat("ident"))
                    mm.then_inc(*pe.step(f"oT{cc}"))
                for m in range(CC):
                    s = take(b, f"SD{m}", dve, f"x1_{m}", 0)
                    e.wait_ge(*act.at(b, "oc1"))
                    project(s, WP0, OC, m).then_inc(*pe.step(f"proj0_{m}"))

            def scan_block(b):
                group_norm(b, 1)
                layer_norm(b, 1, G, ("SD1", "SD0"), "g1_1")
                e.wait_ge(*act.at(b, "xn3"))
                if first(b):
                    e.wait_ge(*dve_set.at(0, "wtap1_2"))
                    e.wait_ge(late_loaded, 16 * LATE_N)
                for cc in range(CC):
                    s = take(b, f"SA{cc}", act, f"u{cc}", 0)
                    for half in range(2):
                        for n in range(TAPS):
                            dy, dx = n // 3, n % 3
                            mm = e.matmul(s[:, half * HALF:(half + 1) * HALF], WTAP[:, cc, n, :],
                                          XNP[:, cc, dy + 16 * half:dy + 16 * half + 16, dx:dx + W],
                                          start=(n == 0), stop=(n == TAPS - 1))
                    mm.then_inc(*pe.step(f"xd{cc}"))
                for cc in range(CC):
                    s = take(b, f"SA{cc}", act, f"z{cc}", 0)
                    for half in range(2):
                        mm = e.matmul(s[:, half * HALF:(half + 1) * HALF], IPZ[:, cc, :],
                                      XNP[:, cc, 1 + 16 * half:17 + 16 * half, 1:1 + W], start=True, stop=True)
                    mm.then_inc(*pe.step(f"z{cc}"))
                s = take(b, "SD0", dve, "hm1", 0)
                e.wait_ge(*dve.at(b, "gap1"))
                for cc in range(CC):
                    mm = e.matmul(s[0:16, 0:1], W1S[:, cc, 0:16], GAP[:, cc:cc + 1], start=(cc == 0), stop=(cc == 1))
                mm.then_inc(*pe.step("fc1"))
                s = take(b, "SD1", dve, "gate_in", 0)
                e.wait_ge(*dve.at(b, "hm1"))
                for m in range(CC):
                    mm = e.matmul(s[:, m:m + 1], S16[:, m * P:(m + 1) * P], HM[:, :], start=True, stop=True)
                mm.then_inc(*pe.step("fc2"))

                def by_chunk(slot, engine, label, w, cc, step, src=U):
                    s = take(b, slot, engine, label, 0)
                    for half in range(2):
                        mm = e.matmul(s[:, half * HALF:(half + 1) * HALF], w, src[:, cc, half * HALF:(half + 1) * HALF],
                                      start=True, stop=True)
                    mm.then_inc(*pe.step(step))

                for cc in range(CC):
                    e.wait_ge(*act.at(b, f"u{cc}"))
                    by_chunk(f"SA{cc}", act, f"v{cc}", WD[:, cc, :], cc, f"v{cc}")
                for cc in range(CC):
                    by_chunk("SD0", dve, f"dbu{cc}", XB[:, cc, :], cc, f"B{cc}")
                    by_chunk("SD1", dve, f"hc{cc}", XC[:, cc, :], cc, f"C{cc}")
                for cc in range(CC):
                    e.wait_ge(*dve.at(b, f"y{cc}"))
                    by_chunk(f"SA{cc}", act, f"ysq{cc}", mat("center64"), cc, f"yc{cc}")
                for cc in range(CC):
                    e.wait_ge(*act.at(b, f"ysq{cc}"))
                    by_chunk(f"SA{cc}", act, f"yln{cc}", mat("mean64"), cc, f"yv{cc}", SQ)
                for cc in range(CC):
                    e.wait_ge(*dve.at(b, f"yz{cc}"))
                    by_chunk(f"SD{cc}", dve, f"xm{2 * cc + 1}", OPW[:, cc, :], cc, f"op{cc}", TA)
                layer_norm(b, 2, TB, ("SD0", "SD1"), "xm3")
                for m in range(CC):
                    s = take(b, f"SD{m}", dve, f"x2_{m}", 0)
                    e.wait_ge(*dve.at(b, "n2_1"))
                    project(s, WP1, TB, m).then_inc(*pe.step(f"proj1_{m}"))

            def channel_block(b):
                group_norm(b, 2)
                layer_norm(b, 3, G, ("SD1", "SD0"), "g2_1")
                for t in range(2):
                    s = take(b, f"SA{t}", act, f"xnt{t}", 0)
                    e.wait_ge(*dve.at(b, "n3_1"))
                    for i in range(4):
                        for cc in range(CC):
                            mm = e.transpose(s[:, i * C + cc * P:i * C + (cc + 1) * P],
                                             G[:, cc, (4 * t + i) * P:(4 * t + i + 1) * P], mat("ident"))
                    mm.then_inc(*pe.step(f"xnT{t}"))
                s = take(b, "SD0", dve, "gram", 0)
                e.wait_ge(*act.at(b, "xnt1"))
                e.wait_ge(*dve.at(b, "xnt_ones"))
                for m in range(CC):
                    for t in range(QT):
                        mm = e.matmul(s[:, m * HALF:m * HALF + C + 1], XNT[:, t, m * P:(m + 1) * P], XNT[:, t, :],
                                      start=(t == 0), stop=(t == QT - 1))
                mm.then_inc(*pe.step("gram"))
                s = take(b, "SD1", dve, "srow", 0)
                e.wait_ge(*dve.at(b, "gram"))
                for cc in range(CC):
                    e.matmul(s[0:1, cc * P:(cc + 1) * P], GRAM[:, cc, C:C + 1], mat("ident"), start=True, stop=True)
                for cc in range(CC):
                    e.matmul(s[0:1, C:2 * C], GRAM[:, cc, C:C + 1], W2Q[:, cc, :], start=(cc == 0), stop=False)
                e.matmul(s[0:1, C:2 * C], ROWS[:, 2 * C:2 * C + 1], ROWS[:, 0:C], start=False, stop=True)\
                 .then_inc(*pe.step("rows"))
                s = take(b, "SA0", act, "t1", 0)
                e.wait_ge(*dve.at(b, "srow"))
                for m in range(CC):
                    for cc in range(CC):
                        e.matmul(s[:, m * C:(m + 1) * C], GRAM[:, cc, m * P:(m + 1) * P], W2Q[:, cc, :], start=(cc == 0), stop=False)
                    mm = e.matmul(s[:, m * C:(m + 1) * C], SROW[:, m * P:(m + 1) * P], ROWS[:, 0:C], start=False, stop=True)
                mm.then_inc(*pe.step("T1"))
                s = take(b, "SD0", dve, "aok3", 0)
                e.wait_ge(*act.at(b, "t1"))
                for m in range(CC):
                    for cc in range(CC):
                        e.matmul(s[:, m * P:(m + 1) * P], T1[:, cc, m * P:(m + 1) * P], W2K[:, cc, m * P:(m + 1) * P],
                                 start=(cc == 0), stop=False)
                    mm = e.matmul(s[:, m * P:(m + 1) * P], SROW[:, C + m * P:C + (m + 1) * P],
                                  ROWS[:, C + m * P:C + (m + 1) * P], start=False, stop=True)
                mm.then_inc(*pe.step("A"))
                s = take(b, "SA1", act, "pat", 0)
                e.wait_ge(*dve.at(b, "abd3"))
                for m in range(CC):
                    mm = e.matmul(s[:, m * C:(m + 1) * C], ABD[:, m, :], WP2[:, m, :], start=True, stop=True)
                mm.then_inc(*pe.step("PAT"))
                s = take(b, "SA0", act, "we", 0)
                e.wait_ge(*act.at(b, "pat"))
                for m in range(CC):
                    for cc in range(CC):
                        mm = e.matmul(s[:, m * C:(m + 1) * C], W2V[:, cc, m * P:(m + 1) * P], PAT[:, cc, :],
                                      start=(cc == 0), stop=(cc == 1))
                mm.then_inc(*pe.step("WE"))
                take(b, "SD1", dve, "be", 0)
                columns("SD1", 0, PAT, "v2_b").then_inc(*pe.step("be"))
                for m in range(CC):
                    s = take(b, f"SD{m}", dve, f"x3_{m}", 0)
                    e.wait_ge(*act.at(b, "we"))
                    project(s, WE, G, m).then_inc(*pe.step(f"out{m}"))
                group_norm(b, 3)
                s = take(b, "SD0", dve, "hm3", 0)
                e.wait_ge(*dve.at(b, "gap3b"))
                for cc in range(CC):
                    mm = e.matmul(s[0:16, 0:1], W1S[:, cc, 16:32], GAP[:, cc:cc + 1], start=(cc == 0), stop=(cc == 1))
                mm.then_inc(*pe.step("w1"))
                s = take(b, "SD1", dve, "sc0", 0)
                e.wait_ge(*dve.at(b, "hm3"))
                for m in range(CC):
                    mm = e.matmul(s[:, m:m + 1], S16[:, C + m * P:C + (m + 1) * P], HM[:, :], start=True, stop=True)
                mm.then_inc(*pe.step("w2"))

            def turn(b):
                state.clear()
                attention(b)
                scan_block(b)
                channel_block(b)
                for slot, (who, what) in LAST.items():
                    assert state[slot][:2] == (who, what), (slot, state[slot][1])

            images(e, turn, turn)

        return {"PE_STEPS": pe, "ACT_STEPS": act, "DVE_STEPS": dve, "POOL_STEPS": pool, "PE_SETUP": pe_set,
                "ACT_SETUP": act_set, "DVE_SETUP": dve_set, "POOL_SETUP": pool_set, "DVE_POOLS": dve_mp,
                "ACT_POOLS": act_mp, "ADD_POOLS": add_mp}


def _arrays(i):
    import numpy as np
    f = {k: np.ascontiguousarray(v) for k, v in i.items()}

    def t2(w):
        return w.T.reshape(CC, P, -1).transpose(1, 0, 2)

    def vec(v):
        return np.asarray(v).reshape(CC, P).T

    def pairs(blocks, rows=64):
        a = np.zeros((2 * rows, CC, P), np.float32)
        for g in range(GROUPS):
            h = g % 2
            a[rows * h:rows * h + rows, g // 2, 64 * h:64 * h + 64] = blocks[g]
        return a

    L0, L1, L2, L3 = "L0_conv_", "L1_conv_", "L2_conv_", "L3_conv_"
    kvw, kvb = f[L0 + "kv_w"], f[L0 + "kv_b"]
    vecs = dict(q_b=f[L0 + "q_b"], k_b=kvb[:C], v_b=kvb[C:], ds_b=f[L0 + "ds_b"], kv_ln_w=f[L0 + "ln_w"],
                kv_ln_b=f[L0 + "ln_b"], pb0=f[L0 + "proj_b"], ln_g=f[L1 + "ln_g"], ln_b=f[L1 + "ln_b"],
                fc2_b=f[L1 + "fc2_b"], skip=np.broadcast_to(f[L1 + "skip_scale"], (C,)), conv_b=f[L1 + "conv_b"],
                dt_b=f[L1 + "dt_proj_b"], A_log=f[L1 + "A_log"], Ds=f[L1 + "Ds_p"], og=f[L1 + "onorm_g"],
                ob=f[L1 + "onorm_b"], pb1=f[L1 + "proj_b"], v2_b=f[L2 + "qkv_b"][2 * C:], pb2=f[L2 + "proj_b"],
                w2_b=f[L3 + "b2"])
    eye, one = np.eye(P, dtype=np.float32), np.ones((P, P), np.float32)
    b64 = np.kron(np.eye(2), np.ones((64, 64))).astype(np.float32) / 64
    b8 = np.kron(np.eye(16), np.ones((8, 8))).astype(np.float32) / 32
    kern = []
    for g in range(GROUPS):
        k = f[L1 + "conv_w"][g, :, 0]
        k = k.transpose(0, 2, 1) if g % 2 else k
        kern.append(k[:, ::-1, ::-1] if g >= 2 else k)
    cw = np.stack([np.concatenate([kern[2 * c].reshape(64, 9), kern[2 * c + 1].reshape(64, 9)]).T for c in range(CC)])
    ip, xp = f[L1 + "in_proj_w"], f[L1 + "x_proj_w"]
    qkv, qb = f[L2 + "qkv_w"], f[L2 + "qkv_b"]
    kidx = np.broadcast_to(np.array([-1, 1, 2, 3, 4, 5, np.float32(3.4e38), np.float32(3.4e38)], np.float32), (P, 8))
    a = dict(
        x=f["x"], cols=np.stack([vec(vecs[n]) for n in COLS], -1),
        mats=np.stack([eye, one / 256, b64, eye - b64, b8], 1),
        wq=t2(f[L0 + "q_w"]), wk=t2(kvw[:C]), wv=t2(kvw[C:]),
        wds=f[L0 + "ds_w"].transpose(1, 2, 3, 0).reshape(CC, P, 4, C).transpose(1, 0, 2, 3), wp0=t2(f[L0 + "proj_w"]),
        small16=np.concatenate([f[L1 + "fc2_w"].T, f[L3 + "w2"].T, f[L1 + "fc1_b"][:, None], f[L3 + "b1"][:, None]], 1),
        w1s=np.concatenate([t2(f[L1 + "fc1_w"]), t2(f[L3 + "w1"])], 2),
        ipx=pairs([ip[g, :64].T for g in range(GROUPS)]), ipz=pairs([ip[g, 64:].T for g in range(GROUPS)]),
        cw=cw.reshape(3, 768),
        xpr=pairs([xp[g, :8] for g in range(GROUPS)], 8), dtp=pairs([f[L1 + "dt_proj_w"][g].T for g in range(GROUPS)], 8),
        xb=pairs([np.broadcast_to(xp[g, 8][:, None], (64, 64)) for g in range(GROUPS)]),
        xc=pairs([np.broadcast_to(xp[g, 9][:, None], (64, 64)) for g in range(GROUPS)]),
        opw=pairs([f[L1 + "out_proj_w"][g].T for g in range(GROUPS)]), wp1=t2(f[L1 + "proj_w"]),
        w2q=t2(qkv[:C]), w2k=t2(qkv[C:2 * C]), w2v=qkv[2 * C:].reshape(CC, P, C).transpose(1, 0, 2), wp2=t2(f[L2 + "proj_w"]),
        rows=np.concatenate([qb[:C], qb[C:2 * C], np.array([N], np.float32)])[None], kidx=kidx)
    return {k: np.ascontiguousarray(v) for k, v in a.items()}


def kernel(**inputs):
    import concourse.bacc as _bacc
    from concourse import mybir as _mybir
    from concourse.bass_utils import run_bass_kernel_spmd as _run

    nc = _bacc.Bacc("TRN2", target_bir_lowering=False, num_devices=1)
    arrays, args = {}, []
    for name, v in _arrays(inputs).items():
        arrays[f"in_{name}"] = v
        args.append(nc.dram_tensor(f"in_{name}", v.shape, _mybir.dt.from_np(v.dtype), kind="ExternalInput").ap())
    args.append(nc.dram_tensor("out_0", (B, C, H, W), _mybir.dt.float32, kind="ExternalOutput").ap())
    program(nc, *args)
    r = _run(nc, [arrays], core_ids=[0])
    return r.results[0]["out_0"]
```

```python
import concourse.bass as bass
from concourse import mybir
from contextlib import ExitStack

B, C, H, W = 4, 256, 32, 32
N = H * W
P = 128
CC = C // P
HALF = 512
HEADS, HD = 8, 32
NK = N // 4
QT = N // P
GROUPS = 4
TAPS = 9
KPOOL = 7
LOWEST = -3.0e38
SOFTPLUS_LINEAR = 20.0
EXP_LN_TABLE, SILU_TABLE = 6, 18
STREAMS = "ABM"
COLS = ["q_b", "k_b", "v_b", "ds_b", "kv_ln_w", "kv_ln_b", "pb0", "ln_g", "ln_b", "fc2_b", "skip",
        "conv_b", "dt_b", "A_log", "Ds", "og", "ob", "pb1", "v2_b", "pb2", "w2_b"]
MATS = ["ident", "mean256", "mean64", "center64", "mean_group"]

PE_A = """
gn0 ds q0_0 q0_1 q1_0 q1_1 msq0 k vT s0_0 s0_1 s0_2 s0_3 s1_0 s1_1 s1_2 s1_3 s2_0 s2_1 s2_2 s2_3
s3_0 s3_1 s3_2 s3_3 mT0 s4_0 s4_1 s4_2 s4_3 st0_0_0 st0_0_1 st0_1_0 st0_1_1 s5_0 s5_1 s5_2 s5_3
st1_0_0 st1_0_1 st1_1_0 st1_1_1 pv0 s6_0 s6_1 s6_2 s6_3 st2_0_0 st2_0_1 st2_1_0 st2_1_1 pv1 s7_0
s7_1 s7_2 s7_3 mT1 st3_0_0 st3_0_1 st3_1_0 st3_1_1 pv2 st4_0_0 st4_0_1 st4_1_0 st4_1_1 pv3 st5_0_0
st5_0_1 st5_1_0 st5_1_1 pv4 st6_0_0 st6_0_1 st6_1_0 st6_1_1 pv5 st7_0_0 st7_0_1 st7_1_0 st7_1_1 pv6
pv7 oT0_0 oT0_1 oT1_0 oT1_1 proj0_0_0 proj0_0_1 proj0_1_0 proj0_1_1 gn1 mean1_0 mean1_1 msq1_0
msq1_1 xd0_0 xd0_1 xd1_0 xd1_1
"""
PE_B = """
z0_0 z0_1 z1_0 z1_1 fc1 fc2 v0_0 v0_1 v1_0 v1_1 B0_0 B0_1 C0_0 C0_1 B1_0 B1_1 C1_0 C1_1 yc0_0 yc0_1
yc1_0 yc1_1 yv0_0 yv0_1 yv1_0 yv1_1 op0_0 op0_1 op1_0 op1_1 mean2_0 mean2_1 msq2_0 msq2_1 proj1_0_0
proj1_0_1 proj1_1_0 proj1_1_1 gn2 mean3_0 mean3_1 msq3_0 msq3_1 xnT0 xnT1 xnT2 xnT3 gram0 gram1 rows
T1 A PAT WE be out_0_0 out_0_1 out_1_0 out_1_1 gn3 w1 w2
"""
ACT_A = """
gn_ln0 gn_rstd0 xds0 xds1 sq_ds qf0_0 qf0_1 qf1_0 qf1_1 ln_ln0 ln_rstd0 kf0 kf1 p0_0_0 p0_0_1 p0_1_0
p0_1_1 p1_0_0 p1_0_1 p1_1_0 p1_1_1 p2_0_0 p2_0_1 p2_1_0 p2_1_1 p3_0_0 p3_0_1 p3_1_0 p3_1_1 p4_0_0
p4_0_1 p4_1_0 p4_1_1 p5_0_0 p5_0_1 p5_1_0 p5_1_1 p6_0_0 p6_0_1 p6_1_0 p6_1_1 p7_0_0 p7_0_1 p7_1_0
p7_1_1 oc0_0 oc0_1 oc1_0 oc1_1 gn_ln1 gn_rstd1 sq1_0 sq1_1 ln_mean1_0 ln_m21_0 ln_mean1_1 ln_m21_1
ln_ln1 ln_rstd1 xn0 xn1 xn2 xn3 xd0_0 xd0_1 xd1_0 xd1_1
"""
ACT_B = """
xr0 xr z0_0 z0_1 z1_0 z1_1 gate_exp u0 u1 zs v0_0 v0_1 v1_0 v1_1 ev0 lv0 ev1 lv1 dA0 dA1 yc0_0
ysq0_0 yc0_1 ysq0_1 yc1_0 ysq1_0 yc1_1 ysq1_1 yln0_0 yln0_1 yrs0 yln1_0 yln1_1 yrs1 ya0 ya1 sq2_0
sq2_1 ln_mean2_0 ln_m22_0 ln_mean2_1 ln_m22_1 ln_ln2 ln_rstd2 gn_ln2 gn_rstd2 sq3_0 sq3_1 ln_mean3_0
ln_m23_0 ln_mean3_1 ln_m23_1 ln_ln3 ln_rstd3 xnt0 xnt1 xnt2 xnt3 t1 aexp0 aexp1 pat we gn_ln3
gn_rstd3
"""
ACT_M = """
a0 a1 y1_0_0 y1_0_1 y1_1_0 y1_1_1 y2_0_0 y2_0_1 y2_1_0 y2_1_1 y3_0_0 y3_0_1 y3_1_0 y3_1_1 y4_0_0
y4_0_1 y4_1_0 y4_1_1 y5_0_0 y5_0_1 y5_1_0 y5_1_1 y6_0_0 y6_0_1 y6_1_0 y6_1_1
"""
DVE_A = """
gn_st0_00 gn_st0_01 gn_st0_10 gn_st0_11 gn_m20 gn_m0 gn_sq0 gn_ex20 gn_gm0 gn_gm20 gn_var0 gn_b0
g0_0 g0_1 ln_mean0 ln_m20 ln_var0 c0_0 c0_1 n0_0 n0_1 kh qh0 qh1 vt mx0_0 mx0_1 mx0_2 mx0_3 mx1_0
mx1_1 mx1_2 mx1_3 mx2_0 mx2_1 mx2_2 mx2_3 mx3_0 mx3_1 mx3_2 mx3_3 mh0 ml0 mx4_0 mx4_1 mx4_2 mx4_3
mx5_0 mx5_1 mx5_2 mx5_3 rz0 o0 mx6_0 mx6_1 mx6_2 mx6_3 rz1 o1 mx7_0 mx7_1 mx7_2 mx7_3 mh1 ml1 rz2 o2
rz3 o3 rz4 o4 rz5 o5 rz6 o6 rz7 o7 x1_0_0 x1_0_1 x1_1_0 x1_1_1 gn_st1_00 gn_st1_01 gn_st1_10
gn_st1_11 gn_m21 gn_m1 gn_sq1 gn_ex21 gn_gm1 gn_gm21 gn_var1 gn_b1 g1_0 g1_1 ln_var1_0 ln_var1 n1_0
n1_1
"""
DVE_B = """
gap1 hm1 gate_in gate_1p vmin0 vmin1 gate gs delta0 delta1 dbu0_0 dbu0_1 scan0 hc0_0 hc0_1 y0 dbu1_0
dbu1_1 scan1 hc1_0 hc1_1 y1 yn0 yn1 yz0 yz1 xm0_0 xm1_0 xm0_1 xm1_1 xm2_0 xm3_0 xm2_1 xm3_1
ln_var2_0 ln_var2 n2_0 n2_1 x2_0_0 x2_0_1 x2_1_0 x2_1_1 xnt_ones gn_st2_00 gn_st2_01 gn_st2_10
gn_st2_11 gn_m22 gn_m2 gn_sq2 gn_ex22 gn_gm2 gn_gm22 gn_var2 gn_b2 g2_0 g2_1 ln_var3_0 ln_var3 n3_0
n3_1 gram0 gram1 srow ab0 aok0 ab1 aok1 ab2 aok2 ab3 aok3 aclip anan amax arow arec arok afill ap0
ap1 abd0 abd1 abd2 abd3 be x3_0_0 x3_0_1 x3_1_0 x3_1_1 gn_st3_00 gn_st3_01 gn_st3_10 gn_st3_11
gn_m23 gn_m3 gn_sq3 gn_ex23 gap3 gn_gm3 gn_gm23 gn_var3 gn_b3 gap3a gap3b hm3 sc0 sc cge0 cge1 qs eq
fb fs0 fs ws0 ws1 wb0 wb1 cf0 cf1 c1 c0 coef
"""
DVE_M = """
hp1_0 h1_0_0 h1_0_1 vp1_0 u1_0 v1_0 hp1_1 h1_1_0 h1_1_1 vp1_1 u1_1 v1_1 hp2_0 h2_0_0 h2_0_1 vp2_0
u2_0 v2_0 hp2_1 h2_1_0 h2_1_1 vp2_1 u2_1 v2_1 hp3_0 h3_0_0 h3_0_1 vp3_0 u3_0 v3_0 hp3_1 h3_1_0
h3_1_1 vp3_1 u3_1 v3_1 hp4_0 h4_0_0 h4_0_1 vp4_0 u4_0 v4_0 hp4_1 h4_1_0 h4_1_1 vp4_1 u4_1 v4_1 hp5_0
h5_0_0 h5_0_1 vp5_0 u5_0 v5_0 hp5_1 h5_1_0 h5_1_1 vp5_1 u5_1 v5_1 hp6_0 h6_0_0 h6_0_1 vp6_0 u6_0
v6_0 hp6_1 h6_1_0 h6_1_1 vp6_1 u6_1 v6_1
"""
POOL_A = """
kl ql0 ql1 c1_0 c1_1
"""
POOL_B = """
du0 du1 c2_0 c2_1 c3_0 c3_1
"""
POOL_M = """
add1_0_0 add1_0_1 add1_1_0 add1_1_1 add2_0_0 add2_0_1 add2_1_0 add2_1_1 add3_0_0 add3_0_1 add3_1_0
add3_1_1 add4_0_0 add4_0_1 add4_1_0 add4_1_1 add5_0_0 add5_0_1 add5_1_0 add5_1_1 add6_0_0 add6_0_1
add6_1_0 add6_1_1
"""
PE_SETUP = """
fold wd fold0
"""
ACT_SETUP = """
expA negA
"""
DVE_SETUP = """
eps0 eps1 qbs kb vb pb1 wk0 wv0 wp10 wk1 wv1 wp11 wd pb0
"""
POOL_SETUP = """
kst1 vt1 abd xnp pa pb hb wtap0_0 wtap0_1 wtap1_1 wtap1_2
"""
PE_ORDER = """
B9 A1 B3 A1 B1 A5 B2 A2 B11 A2 B1 A2 B1 A19 B1 A4 B1 A8 B2 A2 B1 A3 B1 A4 B1 A2 B1 A1 B1 A3 B1 A5 B1
A5 B1 A5 B1 A1 B2 A6 B1 A1 B2 A3 B1 A2 B1 A4 B2 A1 B1 A1 B1 A3 B7 A1 B1 A1 B1 A1 B1 A1
"""
ACT_ORDER = """
B11 A2 B1 M1 B6 A3 M1 A1 M1 A2 M1 A1 M2 A2 M2 A2 M2 B16 M2 A4 B1 A4 B1 M2 B4 M2 A3 B2 A1 M2 A8 B2 M1
B2 A2 M1 B1 A2 B1 M4 A2 M1 B2 A1 M1 A1 B2 A4 B3 A2 B1 A5 B1 A3 B2 A3 B1 A2 B1 A4 B2 A3
"""
DVE_ORDER = """
B1 M6 B3 M6 A14 B4 M1 B1 M1 B5 M11 A7 B3 A4 B5 M8 B1 M1 B2 A16 B1 A2 B1 A4 B4 A4 B3 M5 A3 M4 A2 M1
B1 A1 M1 B1 M3 B2 A3 M3 B1 A2 B1 A3 B1 M1 B10 A2 B3 M2 B3 M1 A2 M16 A2 M1 B3 A1 B1 A5 B1 A11 B1 A1
B1 A6 B19 A1 B2 A3 B21
"""
POOL_ORDER = """
B2 M6 A3 M6 B2 M11 B2 M1 A2
"""


def unpack(order):
    return [s for word in order.split() for s in word[0] * int(word[1:])]


class Steps:

    def __init__(self, sem, text, lead=1):
        self.lead = lead
        self.sem, self.labels, self.said = sem, text.split(), []
        self.index = {x: n for n, x in enumerate(self.labels)}

    def step(self, label):
        n = len(self.said) % max(len(self.labels), 1)
        assert self.labels[n] == label, (label, self.labels[n])
        self.said.append(label)
        return self.sem, 1

    def at(self, b, label):
        return self.sem, (b + self.lead) * len(self.labels) + self.index[label] + 1

    def start(self):
        return self.sem, max(self.lead * len(self.labels), 1)


def program(nc, x, cols, mats, wq, wk, wv, wds, wp0, small16, w1s, ipx, ipz, cw, xpr, dtp, xb, xc, opw,
            wp1, w2q, w2k, w2v, wp2, rows, kidx, out):
    f32, f16 = mybir.dt.float32, mybir.dt.float16
    ALU, ACT, AX = mybir.AluOpType, mybir.ActivationFunctionType, mybir.AxisListType
    SCALE = HD ** -0.5
    ctx = ExitStack()
    with ctx:
        def sb(name, shape, dt=f32):
            return ctx.enter_context(nc.sbuf_tensor(name, shape, dt))

        def sem(name):
            return ctx.enter_context(nc.semaphore(name))

        COL = sb("COL", [P, CC, len(COLS)])
        MAT = sb("MAT", [P, len(MATS), P])
        WQ, WK, WV, WP0 = (sb(n, [P, CC, C]) for n in ("WQ", "WK", "WV", "WP0"))
        WDS = sb("WDS", [P, CC, 4, C])
        S16 = sb("S16", [16, 2 * C + 2])
        W1S = sb("W1S", [P, CC, 32])
        IPZ, XB, XC, WD, OPW = (sb(n, [P, CC, P]) for n in ("IPZ", "XB", "XC", "WD", "OPW"))
        WTAP = sb("WTAP", [P, CC, TAPS, P])
        WP1, W2Q, W2K, W2V, WP2 = (sb(n, [P, CC, C]) for n in ("WP1", "W2Q", "W2K", "W2V", "WP2"))
        ROWS = sb("ROWS", [1, 2 * C + 1])
        KIDX = sb("KIDX", [P, KPOOL + 1])
        EPS = sb("EPS", [P, 2])
        QBS, KB, VB, PB0, PB1, NEGA = (sb(n, [P, CC]) for n in ("QBS", "KB", "VB", "PB0", "PB1", "NEGA"))

        def mat(name):
            return MAT[:, MATS.index(name), :]

        def col(name, cc):
            return COL[:, cc, COLS.index(name):COLS.index(name) + 1]

        X0, XR = sb("X0", [P, CC, N]), sb("XR", [P, CC, N])
        GA0 = sb("GA0", [P, CC, N])
        OT = GA0[:, :, :].rearrange("p c n -> p (c n)").rearrange("p (t c) -> p t c", t=QT)
        PT = sb("PT", [P, 4, N])
        QF, OC = PT[:, 0:2, :], PT[:, 0:2, :]
        QH, QL = (PT[:, n, :].bitcast(f16).rearrange("p (c n) -> p c n", c=CC) for n in (2, 3))
        QST = sb("QST", [P, HEADS, N], f16)
        KST = sb("KST", [P, HEADS, NK], f16)
        VT = sb("VT", [P, 2, HEADS, HD + 1])
        XDS, SQD = sb("XDS", [P, CC, NK]), sb("SQD", [P, CC, NK])
        KF = SQD
        KH, KL = sb("KH", [P, CC, NK], f16), sb("KL", [P, CC, NK], f16)
        MEAN0, VAR0 = sb("MEAN0", [P, NK]), sb("VAR0", [P, NK])
        NEGMAX = sb("NEGMAX", [P, HEADS, QT])
        MH, ML = sb("MH", [32, 2, P], f16), sb("ML", [32, 2, P], f16)
        RZ = sb("RZ", [P, 2, QT])
        G, SQ, PS = sb("G", [P, CC, N]), sb("SQ", [P, CC, N]), sb("PS", [P, 4, N])
        MEAN, VAR = PS[:, 0, :], PS[:, 2, :]
        XM = PS[:, 1::2, :]
        UB = sb("UB", [P, QT * (C + 1)])
        U = UB[:, 0:CC * N].rearrange("p (c n) -> p c n", c=CC)
        XNT = UB[:, :].rearrange("p (t c) -> p t c", t=QT)
        GRAM = PS[:, 0, 0:CC * (C + 1)].rearrange("p (c n) -> p c n", c=CC)
        SROW = PS[0:1, 2, 0:2 * C]
        T1, PAT = (PS[:, 1, n * CC * C:(n + 1) * CC * C].rearrange("p (c n) -> p c n", c=CC) for n in range(2))
        WE = PS[:, 3, 0:CC * C].rearrange("p (c n) -> p c n", c=CC)
        XNP = sb("XNP", [P, CC, H + 2, W + 2])
        GN = {s: [sb(f"{n}_{s}", shape) for n, shape in (("STAT", [P, CC, 2, 6]), ("MSQ", [P, CC, 4]), ("MV", [P, CC, 2]),
                                                        ("GM", [P, CC, 2]), ("GV", [P, CC]), ("GR", [P, CC]), ("GB", [P, CC]))]
              for s in "AB"}
        GAPX, GAP, HM = sb("GAPX", [P, CC]), sb("GAP", [P, CC]), sb("HM", [16, 1])
        GT, GS = sb("GT", [P, CC]), sb("GS", [P, CC])
        AB, AP_, ABD = sb("AB", [P, CC, HD]), sb("AP_", [P, CC, HD]), sb("ABD", [P, CC, P])
        AOK, AEX = sb("AOK", [P, CC, HD]), sb("AEX", [P, CC, HD])
        AMX, ASUM, ANN = sb("AMX", [P, CC]), sb("ASUM", [P, CC]), sb("ANN", [P, CC])
        BE = sb("BE", [P, CC])
        PA_, PB_ = sb("PA_", [P, CC * (H + 2), W + 2]), sb("PB_", [P, CC * (H + 2), W + 2])
        HB, PH = sb("HB", [P, H + 2, W]), sb("PH", [P, H, W // 2])
        PV = PH[:, :, :].rearrange("p h w -> p (h w)").rearrange("p (h w) -> p h w", w=W)
        ACC, YK = sb("ACC", [P, CC, N]), sb("YK", [P, 2, HALF])
        SC, CGE, QS = sb("SC", [P, CC]), sb("CGE", [P, CC, KPOOL + 1]), sb("QS", [P, CC])
        FB, FS, EQ = sb("FB", [P, CC]), sb("FS", [P, CC]), sb("EQ", [P, CC, KPOOL])
        WKP, COEF, C0, C1 = sb("WKP", [P, CC, KPOOL]), sb("COEF", [P, CC, KPOOL]), sb("C0", [P, CC]), sb("C1", [P, CC])
        CW = PS[:, 0:3, 0:768]
        IPX = PS[:, 3, 0:CC * P].rearrange("p (c n) -> p c n", c=CC)
        XPR, DTP = (SQ[0:16, n, 0:CC * P].rearrange("p (c n) -> p c n", c=CC) for n in range(2))

        SLOT = {n: ctx.enter_context(nc.psum_tensor(n, [P, HALF], f32))
                for n in ("aA0", "aA1", "aD0", "aD1", "bA0", "bA1", "bD0", "bD1")}

        pe_a, pe_b = Steps(sem("pe_a_steps"), PE_A), Steps(sem("pe_b_steps"), PE_B)
        act_a, act_b, act_m = Steps(sem("act_a_steps"), ACT_A), Steps(sem("act_b_steps"), ACT_B), Steps(sem("act_m_steps"), ACT_M)
        dve_a, dve_b, dve_m = Steps(sem("dve_a_steps"), DVE_A), Steps(sem("dve_b_steps"), DVE_B), Steps(sem("dve_m_steps"), DVE_M)
        pool_a, pool_b, pool_m = (Steps(sem(n), t) for n, t in
                                  (("pool_a_steps", POOL_A), ("pool_b_steps", POOL_B), ("pool_m_steps", POOL_M)))
        pe_set, act_set = Steps(sem("pe_setup_steps"), PE_SETUP, 0), Steps(sem("act_setup_steps"), ACT_SETUP, 0)
        dve_set, pool_set = Steps(sem("dve_setup_steps"), DVE_SETUP, 0), Steps(sem("pool_setup_steps"), POOL_SETUP, 0)
        mats_loaded = sem("mats_loaded")
        x_loaded, early_loaded, late_loaded = sem("x_loaded"), sem("early_weights_loaded"), sem("late_weights_loaded")
        stacked, maxed, stored = sem("q_k_stacked"), sem("max_rows_stacked"), sem("out_stored")
        EARLY_N, LATE_N = 9, 14
        STACK_DMAS, MAX_DMAS = 24, 4
        NORM = {"A": (pe_a, act_a, dve_a, pool_a, "a", PT[:, 2:4, :], PT[:, 0, :], PT[:, 1, :]),
                "B": (pe_b, act_b, dve_b, pool_b, "b", SQ, MEAN, VAR)}
        BLOCKS = [(m, half) for m in range(CC) for half in range(2)]

        block = ctx.enter_context(nc.Block())

        def take_turn(streams, order, t, active="ABM"):
            going = {s: streams[s](t - STREAMS.index(s)) for s in active if s in streams}
            for s in order:
                if s in going:
                    next(going[s], None)
            for s in going:
                assert next(going[s], "end") == "end", s

        def run(eng, streams, order, before_b=None, setup=None):
            order = unpack(order)
            take_turn({"A": lambda b: streams["A"](b, setup)}, order, 0, "A")
            if before_b:
                before_b()
            take_turn(streams, order, 1, "AB")
            with eng.Fori(2, B) as t:
                take_turn(streams, order, t)
            take_turn(streams, order, B, "BM")
            take_turn(streams, order, B + 1, "M")

        def hs(half):
            return slice(half * HALF, (half + 1) * HALF)

        def interior(t, cc, dy=1, dx=1):
            r = cc * (H + 2) + dy
            return t[:, r:r + H, dx:dx + W]

        @block.sync
        def _(sp):
            x_v = x.rearrange("b (c p) h w -> p (b c) (h w)", p=P)
            out_v = out.rearrange("b (c p) h w -> p (b c) (h w)", p=P)
            sp.sem_inc(stored, 16)
            sp.dma_start(X0[:, :, :], x_v[:, 0:CC, :]).then_inc(x_loaded, 16)
            sp.dma_start(MAT[:, :, :], mats).then_inc(mats_loaded, 16)
            for dst, src in ((COL, cols), (WDS, wds), (WQ, wq), (WK, wk), (WV, wv), (WP0, wp0),
                             (WP1, wp1), (XPR, xpr), (DTP, dtp)):
                sp.dma_start(dst[tuple(slice(None) for _ in dst.shape)], src).then_inc(early_loaded, 16)

            def stack(b):
                sp.wait_ge(*pool_a.at(b, "kl"))
                for j in range(4):
                    for quad, src in ((0, KH), (1, KH), (2, KL)):
                        sp.dma_start(KST[32 * quad:32 * quad + 32, j:HEADS:4, :], src[32 * j:32 * j + 32, :, :])\
                          .then_inc(stacked, 16)
                sp.wait_ge(*pool_a.at(b, "ql1"))
                for j in range(4):
                    for quad, src in ((0, QH), (1, QL), (2, QH)):
                        sp.dma_start(QST[32 * quad:32 * quad + 32, j:HEADS:4, :], src[32 * j:32 * j + 32, :, :])\
                          .then_inc(stacked, 16)

            def max_rows(b, g):
                sp.wait_ge(*dve_a.at(b, f"ml{g}"))
                for r, src in ((96, MH), (97, ML)):
                    sp.dma_start(QST[r:r + 1, 4 * g:4 * g + 4, :].rearrange("a h (t q) -> a (h t) q", t=QT),
                                 src[:, g, :]).then_inc(maxed, 16)

            def next_image(b):
                sp.wait_ge(*act_b.at(b, "xr"))
                sp.wait_ge(*dve_a.at(b, "g1_1"))
                sp.dma_start(X0[:, :, :], x_v[:, bass.ds(b * CC + CC, CC), :]).then_inc(x_loaded, 16)

            def store(b):
                sp.wait_ge(*pool_m.at(b, "add6_1_1"))
                sp.dma_start(out_v[:, bass.ds(b * CC, CC), :], ACC[:, :, :]).then_inc(stored, 16)

            def turn(t, active="ABM"):
                if "A" in active:
                    if "B" in active:
                        next_image(t - 1)
                    stack(t)
                    max_rows(t, 0)
                    max_rows(t, 1)
                if "M" in active:
                    store(t - 2)

            turn(0, "A")
            turn(1, "AB")
            with sp.Fori(2, B) as t:
                turn(t)
            turn(B, "BM")
            turn(B + 1, "M")
            sp.wait_ge(stored, 16 * (B + 1))

        @block.scalar
        def _(e):
            for dst, src in ((S16, small16), (W1S, w1s), (IPX, ipx), (IPZ, ipz), (XB, xb), (XC, xc), (OPW, opw),
                             (W2Q, w2q), (W2K, w2k), (W2V, w2v), (WP2, wp2), (ROWS, rows), (KIDX, kidx)):
                e.dma_start(dst[tuple(slice(None) for _ in dst.shape)], src).then_inc(late_loaded, 16)
            e.dma_start(CW, cw.partition_broadcast(P)).then_inc(late_loaded, 16)
            for s in (act_a, act_b, act_m):
                e.sem_inc(*s.start())

            def table(n):
                e.add_instruction(mybir.InstLoadActFuncSet(act_func_set_id=n, name=nc.get_next_instruction_name(),
                                                           engine=mybir.EngineType.Activation))

            def group_norm(b, l, act, dve):
                GV, GR = GN["A" if l < 2 else "B"][4:6]
                e.wait_ge(*dve.at(b, f"gn_var{l}"))
                e.activation(GR[:, :], GV[:, :], ACT.Ln, bias=EPS[:, 0:1]).then_inc(*act.step(f"gn_ln{l}"))
                yield
                e.wait_ge(*act.at(b, f"gn_ln{l}"))
                e.activation(GR[:, :], GR[:, :], ACT.Exp, scale=-0.5).then_inc(*act.step(f"gn_rstd{l}"))
                yield

            def rstd(b, l, var, act, dve):
                e.wait_ge(*dve.at(b, f"ln_var{l}"))
                e.activation(var, var, ACT.Ln, bias=EPS[:, 0:1]).then_inc(*act.step(f"ln_ln{l}"))
                yield
                e.wait_ge(*act.at(b, f"ln_ln{l}"))
                e.activation(var, var, ACT.Exp, scale=-0.5).then_inc(*act.step(f"ln_rstd{l}"))
                yield

            def down(b):
                e.wait_ge(*pe_a.at(b, "ds"))
                for cc in range(CC):
                    e.activation(XDS[:, cc, :], SLOT["aA0"][:, cc * NK:(cc + 1) * NK], ACT.Identity,
                                 bias=col("ds_b", cc)).then_inc(*act_a.step(f"xds{cc}"))
                    yield
                e.wait_ge(*act_a.at(b, "xds1"))
                e.activation(SQD[:, :, :], XDS[:, :, :], ACT.Square).then_inc(*act_a.step("sq_ds"))
                yield

            def query(b):
                for m, half in BLOCKS:
                    e.wait_ge(*pe_a.at(b, f"q{m}_{half}"))
                    e.activation(QF[:, m, hs(half)], SLOT[f"aA{half}"][:, :], ACT.Identity, bias=QBS[:, m:m + 1],
                                 scale=SCALE).then_inc(*act_a.step(f"qf{m}_{half}"))
                    yield

            def keys(b):
                e.wait_ge(*pe_a.at(b, "k"))
                for cc in range(CC):
                    e.activation(KF[:, cc, :], SLOT["aA0"][:, cc * NK:(cc + 1) * NK], ACT.Identity,
                                 bias=KB[:, cc:cc + 1]).then_inc(*act_a.step(f"kf{cc}"))
                    yield

            def probabilities(b, h):
                if h >= 2:
                    e.wait_ge(*pe_a.at(b, f"pv{h - 2}"))
                for kt, half in BLOCKS:
                    e.wait_ge(*pe_a.at(b, f"st{h}_{kt}_{half}"))
                    e.activation(PT[:, 2 * (h % 2) + kt, hs(half)], SLOT[f"aA{half}"][:, :], ACT.Exp)\
                     .then_inc(*act_a.step(f"p{h}_{kt}_{half}"))
                    yield

            def transpose(b):
                for cc, half in BLOCKS:
                    e.wait_ge(*pe_a.at(b, f"oT{cc}_{half}"))
                    e.activation(OC[:, cc, hs(half)], SLOT[f"aA{half}"][:, :], ACT.Copy).then_inc(*act_a.step(f"oc{cc}_{half}"))
                    yield

            def sums(b, l, src, ready):
                pe, act, dve, _, banks, squares, mean, var = NORM["A" if l == 1 else "B"]
                for cc in range(CC):
                    e.wait_ge(*dve.at(b, ready[cc]))
                    e.activation(squares[:, cc, :], src[:, cc, :], ACT.Square).then_inc(*act.step(f"sq{l}_{cc}"))
                    yield
                for half in range(2):
                    e.wait_ge(*pe.at(b, f"mean{l}_{half}"))
                    e.activation(mean[:, hs(half)], SLOT[f"{banks}A{half}"][:, :], ACT.Copy).then_inc(*act.step(f"ln_mean{l}_{half}"))
                    yield
                    e.activation(var[:, hs(half)], SLOT[f"{banks}A{half}"][:, :], ACT.Square).then_inc(*act.step(f"ln_m2{l}_{half}"))
                    yield

            def scan_order(b):
                yield from rstd(b, 1, NORM["A"][7], act_a, dve_a)
                e.wait_ge(*dve_b.at(b - 1, "xm3_1"))
                for g in range(GROUPS):
                    cc, lo = g // 2, 64 * (g % 2)
                    e.wait_ge(*dve_a.at(b, f"n1_{cc}"))
                    dst = XNP[lo:lo + 64, cc, 1:1 + H, 1:1 + W]
                    if g % 2:
                        dst = dst.rearrange("p h w -> p w h")
                    if g >= 2:
                        dst = dst[:, ::-1, ::-1]
                    e.activation(dst, GA0[lo:lo + 64, cc, :].rearrange("p (h w) -> p h w", h=H), ACT.Identity,
                                 bias=COL[lo:lo + 64, cc, COLS.index("ln_b"):COLS.index("ln_b") + 1],
                                 scale=COL[lo:lo + 64, cc, COLS.index("ln_g"):COLS.index("ln_g") + 1],
                                 accum_out=GAPX[lo:lo + 64, cc:cc + 1]).then_inc(*act_a.step(f"xn{g}"))
                    yield

            def copy_image(b):
                for cc in range(CC):
                    e.activation(XR[:, cc, :], X0[:, cc, :], ACT.Copy).then_inc(*act_b.step(f"xr{cc}" if cc == 0 else "xr"))
                    yield

            def convolved(b, cc):
                e.wait_ge(*pe_b.at(b - 1, "gram1"))
                for half in range(2):
                    e.wait_ge(*pe_a.at(b, f"xd{cc}_{half}"))
                    e.activation(U[:, cc, hs(half)], SLOT[f"aA{half}"][:, :], ACT.Identity, bias=col("conv_b", cc))\
                     .then_inc(*act_a.step(f"xd{cc}_{half}"))
                    yield

            def gate_z(b):
                for cc, half in BLOCKS:
                    e.wait_ge(*pe_b.at(b, f"z{cc}_{half}"))
                    e.activation(G[:, cc, hs(half)], SLOT[f"bA{half}"][:, :], ACT.Copy).then_inc(*act_b.step(f"z{cc}_{half}"))
                    yield

            def silu(b):
                table(SILU_TABLE)
                e.wait_ge(*act_b.at(b, "z1_1"))
                for cc in range(CC):
                    e.activation(U[:, cc, :], U[:, cc, :], ACT.Silu).then_inc(*act_b.step(f"u{cc}"))
                e.activation(G[:, :, :], G[:, :, :], ACT.Silu).then_inc(*act_b.step("zs"))
                table(EXP_LN_TABLE)
                yield

            def gate(b):
                e.wait_ge(*dve_b.at(b, "gate_in"))
                e.activation(GT[:, :], GT[:, :], ACT.Exp, scale=-1.0).then_inc(*act_b.step("gate_exp"))
                yield

            def delta(b):
                for cc, half in BLOCKS:
                    e.wait_ge(*pe_b.at(b, f"v{cc}_{half}"))
                    e.activation(PS[:, 2 * cc, hs(half)], SLOT[f"bA{half}"][:, :], ACT.Identity, bias=col("dt_b", cc))\
                     .then_inc(*act_b.step(f"v{cc}_{half}"))
                    yield
                for cc in range(CC):
                    e.wait_ge(*dve_b.at(b, f"vmin{cc}"))
                    e.activation(PS[:, 2 * cc + 1, :], PS[:, 2 * cc + 1, :], ACT.Exp).then_inc(*act_b.step(f"ev{cc}"))
                    yield
                    e.wait_ge(*act_b.at(b, f"ev{cc}"))
                    e.activation(PS[:, 2 * cc + 1, :], PS[:, 2 * cc + 1, :], ACT.Ln, bias=EPS[:, 1:2])\
                     .then_inc(*act_b.step(f"lv{cc}"))
                    yield
                for cc in range(CC):
                    e.wait_ge(*dve_b.at(b, f"delta{cc}"))
                    e.activation(PS[:, 2 * cc + 1, :], PS[:, 2 * cc, :], ACT.Exp, scale=NEGA[:, cc:cc + 1])\
                     .then_inc(*act_b.step(f"dA{cc}"))
                    yield

            def centred(b):
                for cc, half in BLOCKS:
                    e.wait_ge(*pe_b.at(b, f"yc{cc}_{half}"))
                    e.activation(PS[:, 2 * cc + 1, hs(half)], SLOT[f"bA{half}"][:, :], ACT.Copy).then_inc(*act_b.step(f"yc{cc}_{half}"))
                    yield
                    e.activation(SQ[:, cc, hs(half)], SLOT[f"bA{half}"][:, :], ACT.Square).then_inc(*act_b.step(f"ysq{cc}_{half}"))
                    yield

            def y_rstd(b):
                for cc in range(CC):
                    for half in range(2):
                        e.wait_ge(*pe_b.at(b, f"yv{cc}_{half}"))
                        e.activation(PS[:, 2 * cc, hs(half)], SLOT[f"bA{half}"][:, :], ACT.Ln, bias=EPS[:, 0:1])\
                         .then_inc(*act_b.step(f"yln{cc}_{half}"))
                        yield
                    e.wait_ge(*act_b.at(b, f"yln{cc}_1"))
                    e.activation(PS[:, 2 * cc, :], PS[:, 2 * cc, :], ACT.Exp, scale=-0.5).then_inc(*act_b.step(f"yrs{cc}"))
                    yield

            def y_affine(b):
                for cc in range(CC):
                    e.wait_ge(*dve_b.at(b, f"yn{cc}"))
                    e.activation(PS[:, 2 * cc + 1, :], PS[:, 2 * cc + 1, :], ACT.Identity, bias=col("ob", cc),
                                 scale=col("og", cc)).then_inc(*act_b.step(f"ya{cc}"))
                    yield

            def pixel_rows(b):
                for t in range(4):
                    e.wait_ge(*pe_b.at(b, f"xnT{t}"))
                    e.activation(XNT[:, 2 * t:2 * t + 2, 0:C], SLOT[f"bA{t % 2}"][:, :].rearrange("p (t c) -> p t c", t=2),
                                 ACT.Copy).then_inc(*act_b.step(f"xnt{t}"))
                    yield

            def evacuate(b, slot, dst, waited, step):
                e.wait_ge(*pe_b.at(b, waited))
                e.activation(dst[:, :, :], SLOT[slot][:, :].rearrange("p (c n) -> p c n", c=CC), ACT.Copy)\
                 .then_inc(*act_b.step(step))
                yield

            def channel_softmax(b):
                e.wait_ge(*dve_b.at(b, "amax"))
                for cc in range(CC):
                    e.activation(AEX[:, cc, :], AB[:, cc, :], ACT.Exp, bias=AMX[:, cc:cc + 1],
                                 accum_out=ASUM[:, cc:cc + 1]).then_inc(*act_b.step(f"aexp{cc}"))
                    yield

            def maxpool(b, k):
                if k == 1:
                    e.wait_ge(stored, 16 * b + 16)
                    e.wait_ge(*dve_b.at(b, "coef"))
                    for cc in range(CC):
                        e.activation(ACC[:, cc, :].rearrange("p (h w) -> p h w", h=H), interior(PA_, cc), ACT.Identity,
                                     bias=C1[:, cc:cc + 1], scale=C0[:, cc:cc + 1]).then_inc(*act_m.step(f"a{cc}"))
                        yield
                src = PA_ if k % 2 == 0 else PB_
                for cc, half in BLOCKS:
                    e.wait_ge(*dve_m.at(b, f"v{k}_{cc}"))
                    if cc == 1:
                        e.wait_ge(*pool_m.at(b, f"add{k}_0_{half}"))
                    elif k > 1:
                        e.wait_ge(*pool_m.at(b, f"add{k - 1}_1_{half}"))
                    else:
                        e.wait_ge(*pool_m.at(b - 1, f"add6_1_{half}"))
                    lo = cc * (H + 2) + 1 + 16 * half
                    e.activation(YK[:, half, :].rearrange("p (h w) -> p h w", w=W), src[:, lo:lo + 16, 1:1 + W], ACT.Copy,
                                 scale=COEF[:, cc, k:k + 1]).then_inc(*act_m.step(f"y{k}_{cc}_{half}"))
                    yield

            def stream_a(b, setup=None):
                yield from group_norm(b, 0, act_a, dve_a)
                if setup:
                    setup()
                yield from down(b)
                yield from query(b)
                yield from rstd(b, 0, VAR0[:, :], act_a, dve_a)
                yield from keys(b)
                for h in range(HEADS):
                    yield from probabilities(b, h)
                yield from transpose(b)
                yield from group_norm(b, 1, act_a, dve_a)
                yield from sums(b, 1, GA0, ("g1_0", "g1_1"))
                yield from scan_order(b)
                yield from convolved(b, 0)
                yield from convolved(b, 1)

            def stream_b(b):
                yield from copy_image(b)
                yield from gate_z(b)
                yield from gate(b)
                yield from silu(b)
                yield from delta(b)
                yield from centred(b)
                yield from y_rstd(b)
                yield from y_affine(b)
                yield from sums(b, 2, XM, ("xm1_1", "xm3_1"))
                yield from rstd(b, 2, VAR, act_b, dve_b)
                yield from group_norm(b, 2, act_b, dve_b)
                yield from sums(b, 3, G, ("g2_0", "g2_1"))
                yield from rstd(b, 3, VAR, act_b, dve_b)
                yield from pixel_rows(b)
                yield from evacuate(b, "bA0", T1, "T1", "t1")
                yield from channel_softmax(b)
                yield from evacuate(b, "bA1", PAT, "PAT", "pat")
                yield from evacuate(b, "bA0", WE, "WE", "we")
                yield from group_norm(b, 3, act_b, dve_b)

            def stream_m(b):
                for k in range(1, KPOOL):
                    yield from maxpool(b, k)

            table(EXP_LN_TABLE)
            e.wait_ge(*dve_set.at(0, "eps0"))

            def setup():
                e.wait_ge(early_loaded, 16 * EARLY_N)
                e.activation(NEGA[:, :], COL[:, :, COLS.index("A_log")], ACT.Exp).then_inc(*act_set.step("expA"))
                e.wait_ge(*act_set.at(0, "expA"))
                e.activation(NEGA[:, :], NEGA[:, :], ACT.Copy, scale=-1.0).then_inc(*act_set.step("negA"))
                e.wait_ge(*act_set.at(0, "negA"))
                e.wait_ge(*dve_set.at(0, "eps1"))
                e.wait_ge(*dve_set.at(0, "kb"))

            run(e, {"A": stream_a, "B": stream_b, "M": stream_m}, ACT_ORDER, setup=setup)

        @block.gpsimd
        def _(e):
            for s in (pool_a, pool_b, pool_m):
                e.sem_inc(*s.start())
            e.memset(KST[96:98, :, :], 1.0).then_inc(*pool_set.step("kst1"))
            e.wait_ge(*pool_set.at(0, "kst1"))
            e.memset(VT[:, :, :, HD:HD + 1], 1.0).then_inc(*pool_set.step("vt1"))
            e.memset(ABD[:, :, :], 0.0).then_inc(*pool_set.step("abd"))
            e.memset(XNP[:, :, :, :], 0.0).then_inc(*pool_set.step("xnp"))
            for t, n in ((PA_, "pa"), (PB_, "pb"), (HB, "hb")):
                e.memset(t[:, :, :], LOWEST).then_inc(*pool_set.step(n))

            e.wait_ge(late_loaded, 16 * LATE_N)
            taps = CW.rearrange("p a (t d) -> p a t d", d=P)
            for cc in range(CC):
                for a in range(3):
                    lo, hi = max(6 * a, 9 * cc), min(6 * a + 6, 9 * cc + 9)
                    if lo < hi:
                        e.tensor_tensor(WTAP[:, cc, lo - 9 * cc:hi - 9 * cc, :],
                                        IPX[:, cc, :].unsqueeze(1).broadcast_to([P, hi - lo, P]),
                                        taps[:, a, lo - 6 * a:hi - 6 * a, :], ALU.mult).then_inc(*pool_set.step(f"wtap{cc}_{a}"))

            def split(b):
                e.wait_ge(*dve_a.at(b, "kh"))
                e.tensor_tensor(KL[:, :, :], KF[:, :, :], KH[:, :, :], ALU.subtract).then_inc(*pool_a.step("kl"))
                yield
                for cc in range(CC):
                    e.wait_ge(*dve_a.at(b, f"qh{cc}"))
                    e.tensor_tensor(QL[:, cc, :], QF[:, cc, :], QH[:, cc, :], ALU.subtract)\
                     .then_inc(*pool_a.step(f"ql{cc}"))
                    yield

            def centre(b, l, t):
                pe, act, _, pool, _, _, mean, _ = NORM["A" if l == 1 else "B"]
                e.wait_ge(*pe.at(b, f"mean{l}_1"))
                e.wait_ge(*act.at(b, f"sq{l}_1"))
                e.wait_ge(*act.at(b, f"ln_mean{l}_1"))
                for cc in range(CC):
                    e.tensor_tensor(t[:, cc, :], t[:, cc, :], mean, ALU.subtract).then_inc(*pool.step(f"c{l}_{cc}"))
                    yield

            def delta_u(b):
                for cc in range(CC):
                    e.wait_ge(*dve_b.at(b, f"delta{cc}"))
                    e.tensor_tensor(SQ[:, cc, :], PS[:, 2 * cc, :], U[:, cc, :], ALU.mult)\
                     .then_inc(*pool_b.step(f"du{cc}"))
                    yield

            def maxpool(b, k):
                for cc, half in BLOCKS:
                    e.wait_ge(*act_m.at(b, f"y{k}_{cc}_{half}"))
                    if k > 1:
                        e.wait_ge(*pool_m.at(b, f"add{k - 1}_{cc}_{half}"))
                    e.tensor_tensor(ACC[:, cc, hs(half)], ACC[:, cc, hs(half)], YK[:, half, :], ALU.add)\
                     .then_inc(*pool_m.step(f"add{k}_{cc}_{half}"))
                    yield

            def stream_a(b, setup=None):
                yield from split(b)
                yield from centre(b, 1, GA0)

            def stream_b(b):
                yield from delta_u(b)
                yield from centre(b, 2, XM)
                yield from centre(b, 3, G)

            def stream_m(b):
                for k in range(1, KPOOL):
                    yield from maxpool(b, k)

            run(e, {"A": stream_a, "B": stream_b, "M": stream_m}, POOL_ORDER)

        @block.vector
        def _(e):
            for s in (dve_a, dve_b, dve_m):
                e.sem_inc(*s.start())
            e.memset(EPS[:, 0:1], 1e-5).then_inc(*dve_set.step("eps0"))
            e.memset(EPS[:, 1:2], 1.0).then_inc(*dve_set.step("eps1"))

            def setup():
                e.wait_ge(early_loaded, 16 * EARLY_N)
                e.tensor_scalar(QBS[:, :], COL[:, :, COLS.index("q_b")], SCALE, None, ALU.mult).then_inc(*dve_set.step("qbs"))
                e.wait_ge(*pe_set.at(0, "fold"))
                FOLD = SLOT["bD0"]
                e.tensor_tensor(KB[:, :], FOLD[:, 0:2], COL[:, :, COLS.index("k_b")], ALU.add).then_inc(*dve_set.step("kb"))
                e.tensor_tensor(VB[:, :], FOLD[:, 2:4], COL[:, :, COLS.index("v_b")], ALU.add).then_inc(*dve_set.step("vb"))
                e.tensor_tensor(PB1[:, :], FOLD[:, 4:6], COL[:, :, COLS.index("pb1")], ALU.add).then_inc(*dve_set.step("pb1"))
                for cc in range(CC):
                    for t, w, n in ((WK, "kv_ln_w", "wk"), (WV, "kv_ln_w", "wv"), (WP1, "ln_g", "wp1")):
                        e.tensor_scalar(t[:, cc, :], t[:, cc, :], col(w, cc), None, ALU.mult)\
                         .then_inc(*dve_set.step(f"{n}{cc}"))
                e.wait_ge(*pe_set.at(0, "wd"))
                e.tensor_copy(WD[:, :, :], SLOT["bD1"][:, 0:CC * P].rearrange("p (c n) -> p c n", c=CC)).then_inc(*dve_set.step("wd"))
                e.wait_ge(*pe_set.at(0, "fold0"))
                e.tensor_tensor(PB0[:, :], FOLD[:, 0:2], COL[:, :, COLS.index("pb0")], ALU.add).then_inc(*dve_set.step("pb0"))

            def group_norm(b, l, src, dst, out_tile, dve, pe, act, slot):
                STAT, MSQ, MV, GM, GV, GR, GB = GN["A" if l < 2 else "B"]
                for cc in range(CC):
                    for half in range(2):
                        e.bn_stats(STAT[:, cc, half, :], src(cc, half)).then_inc(*dve.step(f"gn_st{l}_{cc}{half}"))
                        yield
                means, m2s = (STAT[:, :, :, :].rearrange("p c a (s t) -> p c (a s) t", t=3)[:, :, :, n] for n in (1, 2))
                e.wait_ge(*dve.at(b, f"gn_st{l}_11"))
                e.tensor_tensor(MSQ[:, :, :], means, means, ALU.mult).then_inc(*dve.step(f"gn_m2{l}"))
                yield
                e.tensor_reduce(MV[:, :, 0], means, AX.X, ALU.add).then_inc(*dve.step(f"gn_m{l}"))
                yield
                e.wait_ge(*dve.at(b, f"gn_m2{l}"))
                e.scalar_tensor_tensor(out=MSQ[:, :, :], in0=m2s, scalar=4.0 / N, in1=MSQ[:, :, :], op0=ALU.mult,
                                       op1=ALU.add).then_inc(*dve.step(f"gn_sq{l}"))
                yield
                e.wait_ge(*dve.at(b, f"gn_sq{l}"))
                e.tensor_reduce(MV[:, :, 1], MSQ[:, :, :], AX.X, ALU.add).then_inc(*dve.step(f"gn_ex2{l}"))
                yield
                if l == 3:
                    e.tensor_scalar(GAP[:, :], MV[:, :, 0], 0.25, None, ALU.mult).then_inc(*dve.step("gap3"))
                    yield
                e.wait_ge(*pe.at(b, f"gn{l}"))
                e.tensor_copy(GM[:, :, :], SLOT[slot][:, 0:4].rearrange("p (c s) -> p c s", c=CC)).then_inc(*dve.step(f"gn_gm{l}"))
                yield
                e.wait_ge(*dve.at(b, f"gn_gm{l}"))
                e.tensor_tensor(GV[:, :], GM[:, :, 0], GM[:, :, 0], ALU.mult).then_inc(*dve.step(f"gn_gm2{l}"))
                yield
                e.wait_ge(*dve.at(b, f"gn_gm2{l}"))
                e.tensor_tensor(GV[:, :], GM[:, :, 1], GV[:, :], ALU.subtract).then_inc(*dve.step(f"gn_var{l}"))
                yield
                e.wait_ge(*act.at(b, f"gn_rstd{l}"))
                e.scalar_tensor_tensor(out=GB[:, :], in0=GM[:, :, 0], scalar=-1.0, in1=GR[:, :], op0=ALU.mult,
                                       op1=ALU.mult).then_inc(*dve.step(f"gn_b{l}"))
                yield
                e.wait_ge(*dve.at(b, f"gn_b{l}"))
                if dst is not None:
                    for cc in range(CC):
                        e.tensor_scalar(out_tile[:, cc, :], dst(cc), GR[:, cc:cc + 1], GB[:, cc:cc + 1], ALU.mult, ALU.add)\
                         .then_inc(*dve.step(f"g{l}_{cc}"))
                        yield

            def attention_norm(b):
                e.wait_ge(x_loaded, 16 * b + 16)
                yield from group_norm(b, 0, lambda cc, h: X0[:, cc, hs(h)], lambda cc: X0[:, cc, :], GA0, dve_a, pe_a, act_a, "aD0")

            def scan_norm(b):
                e.wait_ge(*dve_a.at(b, "x1_1_1"))
                yield from group_norm(b, 1, lambda cc, h: X0[:, cc, hs(h)], lambda cc: X0[:, cc, :], GA0, dve_a, pe_a, act_a, "aD0")

            def channel_norm(b):
                e.wait_ge(*dve_b.at(b, "x2_1_1"))
                yield from group_norm(b, 2, lambda cc, h: XR[:, cc, hs(h)], lambda cc: XR[:, cc, :], G, dve_b, pe_b, act_b, "bD0")

            def kv_norm(b):
                s = SLOT["aD0"]
                e.wait_ge(*pe_a.at(b, "msq0"))
                e.tensor_copy(MEAN0[:, :], s[:, 0:NK]).then_inc(*dve_a.step("ln_mean0"))
                yield
                e.wait_ge(*dve_a.at(b, "ln_mean0"))
                e.scalar_tensor_tensor(out=VAR0[:, :], in0=MEAN0[:, :], scalar=-1.0, in1=MEAN0[:, :], op0=ALU.mult,
                                       op1=ALU.mult).then_inc(*dve_a.step("ln_m20"))
                yield
                e.wait_ge(*dve_a.at(b, "ln_m20"))
                e.tensor_tensor(VAR0[:, :], VAR0[:, :], s[:, NK:2 * NK], ALU.add).then_inc(*dve_a.step("ln_var0"))
                yield
                for cc in range(CC):
                    e.tensor_tensor(XDS[:, cc, :], XDS[:, cc, :], MEAN0[:, :], ALU.subtract).then_inc(*dve_a.step(f"c0_{cc}"))
                    yield
                e.wait_ge(*act_a.at(b, "ln_rstd0"))
                for cc in range(CC):
                    e.wait_ge(*dve_a.at(b, f"c0_{cc}"))
                    e.tensor_tensor(XDS[:, cc, :], XDS[:, cc, :], VAR0[:, :], ALU.mult).then_inc(*dve_a.step(f"n0_{cc}"))
                    yield

            def variance(b, l):
                pe, act, dve, _, banks, _, _, var = NORM["A" if l == 1 else "B"]
                for half in range(2):
                    e.wait_ge(*pe.at(b, f"msq{l}_{half}"))
                    e.wait_ge(*act.at(b, f"ln_m2{l}_{half}"))
                    e.tensor_tensor(var[:, hs(half)], SLOT[f"{banks}D{half}"][:, :], var[:, hs(half)], ALU.subtract)\
                     .then_inc(*dve.step(f"ln_var{l}" if half else f"ln_var{l}_0"))
                    yield

            def normalise(b, l, t):
                _, act, dve, pool, _, _, _, var = NORM["A" if l == 1 else "B"]
                e.wait_ge(*act.at(b, f"ln_rstd{l}"))
                for cc in range(CC):
                    e.wait_ge(*pool.at(b, f"c{l}_{cc}"))
                    e.tensor_tensor(t[:, cc, :], t[:, cc, :], var, ALU.mult).then_inc(*dve.step(f"n{l}_{cc}"))
                    yield

            def split(b):
                e.wait_ge(*act_a.at(b, "kf1"))
                e.tensor_copy(KH[:, :, :], KF[:, :, :]).then_inc(*dve_a.step("kh"))
                yield
                for cc in range(CC):
                    e.wait_ge(*act_a.at(b, f"qf{cc}_1"))
                    e.tensor_copy(QH[:, cc, :], QF[:, cc, :]).then_inc(*dve_a.step(f"qh{cc}"))
                    yield
                e.wait_ge(*pe_a.at(b, "vT"))
                e.tensor_copy(VT[:, :, :, 0:HD],
                              SLOT["aD1"][:, 0:2 * C].rearrange("p (k h d) -> p k h d", k=2, h=HEADS)).then_inc(*dve_a.step("vt"))
                yield

            def maxima(b, h):
                for j in range(4):
                    e.wait_ge(*pe_a.at(b, f"s{h}_{j}"))
                    e.tensor_reduce(NEGMAX[:, h, 2 * j:2 * j + 2], SLOT[f"aD{j % 2}"][:, :].rearrange("p (t k) -> p t k", t=2),
                                    AX.X, ALU.max, negate=True).then_inc(*dve_a.step(f"mx{h}_{j}"))
                    yield

            def max_rows(b, g):
                e.wait_ge(*pe_a.at(b, f"mT{g}"))
                e.tensor_copy(MH[:, g, :], SLOT["aD0"][0:32, 0:P]).then_inc(*dve_a.step(f"mh{g}"))
                yield
                e.wait_ge(*dve_a.at(b, f"mh{g}"))
                e.tensor_tensor(ML[:, g, :], SLOT["aD0"][0:32, 0:P], MH[:, g, :], ALU.subtract).then_inc(*dve_a.step(f"ml{g}"))
                yield

            def weighted(b, h):
                e.wait_ge(*pe_a.at(b, f"pv{h}"))
                o = SLOT["aD1"][:, 0:QT * (HD + 1)].rearrange("p (t d) -> p t d", t=QT)
                e.reciprocal(RZ[:, h % 2, :], o[:, :, HD]).then_inc(*dve_a.step(f"rz{h}"))
                yield
                e.wait_ge(*dve_a.at(b, f"rz{h}"))
                e.tensor_tensor(OT[:, :, h * HD:(h + 1) * HD], o[:, :, 0:HD],
                                RZ[:, h % 2, :].unsqueeze(2).broadcast_to([P, QT, HD]), ALU.mult).then_inc(*dve_a.step(f"o{h}"))
                yield

            def add_to_image(b, label, dve, pe, s, offset, dst):
                for m, half in BLOCKS:
                    e.wait_ge(*pe.at(b, f"{s}_{m}_{half}"))
                    slot = SLOT[("aD" if pe is pe_a else "bD") + str(half)]
                    e.scalar_tensor_tensor(out=dst[:, m, hs(half)], in0=slot[:, :], scalar=offset[:, m:m + 1],
                                           in1=dst[:, m, hs(half)], op0=ALU.add, op1=ALU.add)\
                     .then_inc(*dve.step(f"{label}_{m}_{half}"))
                    yield

            def gate(b):
                e.wait_ge(*act_a.at(b, "xn3"))
                e.tensor_scalar(GAPX[:, :], GAPX[:, :], 1.0 / N, None, ALU.mult).then_inc(*dve_b.step("gap1"))
                yield
                e.wait_ge(*pe_b.at(b, "fc1"))
                e.tensor_scalar(HM[:, :], SLOT["bD0"][0:16, 0:1], S16[:, 2 * C:2 * C + 1], 0.0, ALU.add, ALU.max)\
                 .then_inc(*dve_b.step("hm1"))
                yield
                e.wait_ge(*pe_b.at(b, "fc2"))
                e.tensor_tensor(GT[:, :], SLOT["bD1"][:, 0:2], COL[:, :, COLS.index("fc2_b")], ALU.add).then_inc(*dve_b.step("gate_in"))
                yield

            def delta(b):
                e.wait_ge(*act_b.at(b, "gate_exp"))
                e.tensor_scalar(GT[:, :], GT[:, :], 1.0, None, ALU.add).then_inc(*dve_b.step("gate_1p"))
                yield
                for cc in range(CC):
                    e.wait_ge(*act_b.at(b, f"v{cc}_1"))
                    e.tensor_scalar(PS[:, 2 * cc + 1, :], PS[:, 2 * cc, :], SOFTPLUS_LINEAR, None, ALU.min)\
                     .then_inc(*dve_b.step(f"vmin{cc}"))
                    yield
                e.wait_ge(*dve_b.at(b, "gate_1p"))
                e.reciprocal(GS[:, :], GT[:, :]).then_inc(*dve_b.step("gate"))
                yield
                e.wait_ge(*dve_b.at(b, "gate"))
                e.tensor_tensor(GS[:, :], GS[:, :], COL[:, :, COLS.index("skip")], ALU.mult).then_inc(*dve_b.step("gs"))
                yield
                for cc in range(CC):
                    e.wait_ge(*act_b.at(b, f"lv{cc}"))
                    e.tensor_tensor(PS[:, 2 * cc, :], PS[:, 2 * cc, :], PS[:, 2 * cc + 1, :], ALU.max)\
                     .then_inc(*dve_b.step(f"delta{cc}"))
                    yield

            def scan(b, cc):
                e.wait_ge(*pool_b.at(b, f"du{cc}"))
                for half in range(2):
                    e.wait_ge(*pe_b.at(b, f"B{cc}_{half}"))
                    e.tensor_tensor(SQ[:, cc, hs(half)], SQ[:, cc, hs(half)], SLOT[f"bD{half}"][:, :], ALU.mult)\
                     .then_inc(*dve_b.step(f"dbu{cc}_{half}"))
                    yield
                e.wait_ge(*dve_b.at(b, f"dbu{cc}_1"))
                e.wait_ge(*act_b.at(b, f"dA{cc}"))
                e.tensor_tensor_scan(PS[:, 2 * cc, :], PS[:, 2 * cc + 1, :], SQ[:, cc, :], 0.0, ALU.mult, ALU.add)\
                 .then_inc(*dve_b.step(f"scan{cc}"))
                yield
                e.wait_ge(*dve_b.at(b, f"scan{cc}"))
                for half in range(2):
                    e.wait_ge(*pe_b.at(b, f"C{cc}_{half}"))
                    e.tensor_tensor(PS[:, 2 * cc, hs(half)], PS[:, 2 * cc, hs(half)], SLOT[f"bD{half}"][:, :], ALU.mult)\
                     .then_inc(*dve_b.step(f"hc{cc}_{half}"))
                    yield
                e.wait_ge(*dve_b.at(b, f"hc{cc}_1"))
                e.scalar_tensor_tensor(out=U[:, cc, :], in0=U[:, cc, :], scalar=col("Ds", cc), in1=PS[:, 2 * cc, :],
                                       op0=ALU.mult, op1=ALU.add).then_inc(*dve_b.step(f"y{cc}"))
                yield

            def gated(b):
                for cc in range(CC):
                    e.wait_ge(*act_b.at(b, f"yrs{cc}"))
                    e.tensor_tensor(PS[:, 2 * cc + 1, :], PS[:, 2 * cc + 1, :], PS[:, 2 * cc, :], ALU.mult)\
                     .then_inc(*dve_b.step(f"yn{cc}"))
                    yield
                for cc in range(CC):
                    e.wait_ge(*act_b.at(b, f"ya{cc}"))
                    e.tensor_tensor(G[:, cc, :], PS[:, 2 * cc + 1, :], G[:, cc, :], ALU.mult).then_inc(*dve_b.step(f"yz{cc}"))
                    yield
                for cc in range(CC):
                    for half in range(2):
                        e.wait_ge(*pe_b.at(b, f"op{cc}_{half}"))
                        for g in (2 * cc, 2 * cc + 1):
                            lo, rows = 64 * (g % 2), slice(16 * half, 16 * half + 16)
                            dst = XM[lo:lo + 64, cc, :].rearrange("p (h w) -> p h w", h=H)
                            if g % 2:
                                dst = dst.rearrange("p h w -> p w h")
                            if g >= 2:
                                dst = dst[:, ::-1, ::-1]
                            e.scalar_tensor_tensor(out=dst[:, rows, :],
                                                   in0=SLOT[f"bD{half}"][lo:lo + 64, :].rearrange("p (h w) -> p h w", w=W),
                                                   scalar=GS[lo:lo + 64, cc:cc + 1],
                                                   in1=XNP[lo:lo + 64, cc, 1 + 16 * half:17 + 16 * half, 1:1 + W],
                                                   op0=ALU.mult, op1=ALU.mult).then_inc(*dve_b.step(f"xm{g}_{half}"))
                            yield

            def ones_column(b):
                e.memset(XNT[:, :, C:C + 1], 1.0).then_inc(*dve_b.step("xnt_ones"))
                yield

            def gram(b):
                for m in range(CC):
                    e.wait_ge(*pe_b.at(b, f"gram{m}"))
                    e.tensor_copy(GRAM[:, m, :], SLOT[f"bD{m}"][:, 0:C + 1]).then_inc(*dve_b.step(f"gram{m}"))
                    yield

            def channel_softmax(b):
                e.wait_ge(*pe_b.at(b, "rows"))
                e.tensor_copy(SROW, SLOT["bD0"][0:1, 0:2 * C]).then_inc(*dve_b.step("srow"))
                yield
                e.wait_ge(*pe_b.at(b, "A"))
                S = SLOT["bD1"][:, 0:CC * P].rearrange("p (c j) -> p c j", c=CC)
                for j in range(4):
                    blk = slice(HD * j, HD * j + HD)
                    e.tensor_scalar(AB[blk, :, :], S[blk, :, blk], SCALE, 50.0, ALU.mult, ALU.min).then_inc(*dve_b.step(f"ab{j}"))
                    yield
                    e.tensor_copy(AOK[blk, :, :], S[blk, :, blk]).then_inc(*dve_b.step(f"aok{j}"))
                    yield
                e.wait_ge(*dve_b.at(b, "aok3"))
                e.tensor_scalar(AB[:, :, :], AB[:, :, :], -50.0, None, ALU.max).then_inc(*dve_b.step("aclip"))
                yield
                e.tensor_tensor(AOK[:, :, :], AOK[:, :, :], AOK[:, :, :], ALU.is_equal).then_inc(*dve_b.step("anan"))
                yield
                e.wait_ge(*dve_b.at(b, "anan"))
                e.tensor_reduce(AMX[:, :], AB[:, :, :], AX.X, ALU.max, negate=True).then_inc(*dve_b.step("amax"))
                yield
                e.tensor_reduce(ANN[:, :], AOK[:, :, :], AX.X, ALU.min).then_inc(*dve_b.step("arow"))
                yield

            def attended(b):
                e.wait_ge(*act_b.at(b, "aexp1"))
                e.reciprocal(ASUM[:, :], ASUM[:, :]).then_inc(*dve_b.step("arec"))
                yield
                e.wait_ge(*dve_b.at(b, "arec"))
                e.tensor_tensor(ASUM[:, :], ASUM[:, :], ANN[:, :], ALU.mult).then_inc(*dve_b.step("arok"))
                yield
                e.tensor_scalar(ANN[:, :], ANN[:, :], -1.0 / HD, 1.0 / HD, ALU.mult, ALU.add).then_inc(*dve_b.step("afill"))
                yield
                e.wait_ge(*dve_b.at(b, "afill"))
                for cc in range(CC):
                    e.tensor_scalar(AP_[:, cc, :], AEX[:, cc, :], ASUM[:, cc:cc + 1], ANN[:, cc:cc + 1], ALU.mult, ALU.add)\
                     .then_inc(*dve_b.step(f"ap{cc}"))
                    yield
                e.wait_ge(*dve_b.at(b, "ap1"))
                for j in range(4):
                    blk = slice(HD * j, HD * j + HD)
                    e.tensor_copy(ABD[blk, :, blk], AP_[blk, :, :]).then_inc(*dve_b.step(f"abd{j}"))
                    yield
                e.wait_ge(*pe_b.at(b, "be"))
                e.tensor_tensor(BE[:, :], SLOT["bD0"][:, 0:2], COL[:, :, COLS.index("pb2")], ALU.add).then_inc(*dve_b.step("be"))
                yield

            def block3_out(b):
                e.wait_ge(*dve_b.at(b, "be"))
                e.wait_ge(*act_m.at(b - 1, "y6_1_1"))
                for m, half in BLOCKS:
                    e.wait_ge(*pe_b.at(b, f"out_{m}_{half}"))
                    lo = m * (H + 2) + 1 + 16 * half
                    e.scalar_tensor_tensor(out=PA_[:, lo:lo + 16, 1:1 + W],
                                           in0=SLOT[f"bD{half}"][:, :].rearrange("p (h w) -> p h w", w=W),
                                           scalar=BE[:, m:m + 1], in1=XR[:, m, hs(half)].rearrange("p (h w) -> p h w", w=W),
                                           op0=ALU.add, op1=ALU.add).then_inc(*dve_b.step(f"x3_{m}_{half}"))
                    yield

            def pool_norm(b):
                e.wait_ge(*dve_b.at(b, "x3_1_1"))
                yield from group_norm(b, 3, lambda cc, h: PA_[:, cc * (H + 2) + 1 + 16 * h:cc * (H + 2) + 17 + 16 * h, 1:1 + W], None,
                           None, dve_b, pe_b, act_b, "bD0")

            def pool_score(b):
                GR, GB = GN["B"][5:7]
                e.tensor_tensor(GAP[:, :], GAP[:, :], GR[:, :], ALU.mult).then_inc(*dve_b.step("gap3a"))
                e.wait_ge(*dve_b.at(b, "gap3a"))
                e.tensor_tensor(GAP[:, :], GAP[:, :], GB[:, :], ALU.add).then_inc(*dve_b.step("gap3b"))
                yield
                e.wait_ge(*pe_b.at(b, "w1"))
                e.tensor_scalar(HM[:, :], SLOT["bD0"][0:16, 0:1], S16[:, 2 * C + 1:2 * C + 2], 0.0, ALU.add, ALU.max)\
                 .then_inc(*dve_b.step("hm3"))
                yield
                e.wait_ge(*pe_b.at(b, "w2"))
                e.tensor_tensor(SC[:, :], SLOT["bD1"][:, 0:2], COL[:, :, COLS.index("w2_b")], ALU.add).then_inc(*dve_b.step("sc0"))
                e.wait_ge(*dve_b.at(b, "sc0"))
                e.tensor_scalar(SC[:, :], SC[:, :], 0.0, None, ALU.max).then_inc(*dve_b.step("sc"))
                e.wait_ge(*dve_b.at(b, "sc"))
                for cc in range(CC):
                    e.tensor_scalar(CGE[:, cc, :], KIDX[:, :], SC[:, cc:cc + 1], None, ALU.is_le).then_inc(*dve_b.step(f"cge{cc}"))
                e.wait_ge(*dve_b.at(b, "cge1"))
                e.tensor_reduce(QS[:, :], CGE[:, :, 1:6], AX.X, ALU.add).then_inc(*dve_b.step("qs"))
                e.tensor_tensor(EQ[:, :, :], CGE[:, :, 0:KPOOL], CGE[:, :, 1:KPOOL + 1], ALU.subtract).then_inc(*dve_b.step("eq"))
                e.wait_ge(*dve_b.at(b, "eq"))
                e.tensor_tensor(FB[:, :], SC[:, :], QS[:, :], ALU.subtract).then_inc(*dve_b.step("fb"))
                e.tensor_scalar(FS[:, :], QS[:, :], 1.0, None, ALU.add).then_inc(*dve_b.step("fs0"))
                e.wait_ge(*dve_b.at(b, "fs0"))
                e.tensor_tensor(FS[:, :], FS[:, :], SC[:, :], ALU.subtract).then_inc(*dve_b.step("fs"))
                e.wait_ge(*dve_b.at(b, "fs"))
                for cc in range(CC):
                    e.tensor_scalar(WKP[:, cc, :], EQ[:, cc, :], FS[:, cc:cc + 1], None, ALU.mult).then_inc(*dve_b.step(f"ws{cc}"))
                e.wait_ge(*dve_b.at(b, "ws1"))
                for cc in range(CC):
                    e.scalar_tensor_tensor(out=WKP[:, cc, 1:KPOOL], in0=EQ[:, cc, 0:KPOOL - 1], scalar=FB[:, cc:cc + 1],
                                           in1=WKP[:, cc, 1:KPOOL], op0=ALU.mult, op1=ALU.add).then_inc(*dve_b.step(f"wb{cc}"))
                e.wait_ge(*dve_b.at(b, "wb1"))
                for cc in range(CC):
                    e.tensor_scalar(COEF[:, cc, :], WKP[:, cc, :], GR[:, cc:cc + 1], None, ALU.mult).then_inc(*dve_b.step(f"cf{cc}"))
                e.tensor_scalar(C1[:, :], GB[:, :], 2.0, None, ALU.mult).then_inc(*dve_b.step("c1"))
                e.wait_ge(*dve_b.at(b, "c1"))
                e.tensor_tensor(C0[:, :], COEF[:, :, 0], GR[:, :], ALU.add).then_inc(*dve_b.step("c0"))
                e.wait_ge(*dve_b.at(b, "c0"))
                e.tensor_scalar(C0[:, :], C0[:, :], 1.0, None, ALU.add).then_inc(*dve_b.step("coef"))

            def maxpool(b, k):
                src, dst = (PA_, PB_) if k % 2 else (PB_, PA_)
                for cc in range(CC):
                    lo = cc * (H + 2)
                    e.wait_ge(*(dve_m.at(b, f"v{k}_0") if cc else dve_m.at(b, f"v{k - 1}_1") if k > 1 else
                                dve_m.at(b - 1, f"v{KPOOL - 1}_1")))
                    e.tensor_tensor(PH[:, :, :], src[:, lo + 1:lo + 1 + H, 1:1 + W:2], src[:, lo + 1:lo + 1 + H, 2:2 + W:2],
                                    ALU.max).then_inc(*dve_m.step(f"hp{k}_{cc}"))
                    yield
                    e.wait_ge(*dve_m.at(b, f"hp{k}_{cc}"))
                    for s in range(2):
                        e.tensor_tensor(HB[:, 1:1 + H, s:W:2], src[:, lo + 1:lo + 1 + H, 3 * s:3 * s + W - 1:2], PH[:, :, :], ALU.max)\
                         .then_inc(*dve_m.step(f"h{k}_{cc}_{s}"))
                        yield
                    e.wait_ge(*dve_m.at(b, f"h{k}_{cc}_1"))
                    e.tensor_tensor(PV[:, :, :], HB[:, 1:1 + H:2, :], HB[:, 2:2 + H:2, :], ALU.max).then_inc(*dve_m.step(f"vp{k}_{cc}"))
                    yield
                    e.wait_ge(*dve_m.at(b, f"vp{k}_{cc}"))
                    if k >= 2:
                        e.wait_ge(*act_m.at(b, f"y{k - 2}_{cc}_1" if k > 2 else f"a{cc}"))
                    else:
                        e.wait_ge(*act_m.at(b - 1, f"y5_{cc}_1"))
                    for s in range(2):
                        e.tensor_tensor(dst[:, lo + 1 + s:lo + 1 + H:2, 1:1 + W], HB[:, 3 * s:3 * s + H - 1:2, :], PV[:, :, :],
                                        ALU.max).then_inc(*dve_m.step(f"v{k}_{cc}" if s else f"u{k}_{cc}"))
                        yield

            def stream_a(b, setup=None):
                yield from attention_norm(b)
                if setup:
                    setup()
                yield from kv_norm(b)
                yield from split(b)
                for h in range(4):
                    yield from maxima(b, h)
                yield from max_rows(b, 0)
                for h in range(4):
                    yield from maxima(b, 4 + h)
                    if h == 3:
                        yield from max_rows(b, 1)
                    if h >= 1:
                        yield from weighted(b, h - 1)
                for h in range(3, HEADS):
                    yield from weighted(b, h)
                yield from add_to_image(b, "x1", dve_a, pe_a, "proj0", PB0, X0)
                yield from scan_norm(b)
                yield from variance(b, 1)
                yield from normalise(b, 1, GA0)

            def stream_b(b):
                yield from gate(b)
                yield from delta(b)
                yield from scan(b, 0)
                yield from scan(b, 1)
                yield from gated(b)
                yield from variance(b, 2)
                yield from normalise(b, 2, XM)
                yield from add_to_image(b, "x2", dve_b, pe_b, "proj1", PB1, XR)
                yield from ones_column(b)
                yield from channel_norm(b)
                yield from variance(b, 3)
                yield from normalise(b, 3, G)
                yield from gram(b)
                yield from channel_softmax(b)
                yield from attended(b)
                yield from block3_out(b)
                yield from pool_norm(b)
                yield from pool_score(b)

            def stream_m(b):
                for k in range(1, KPOOL):
                    yield from maxpool(b, k)

            e.wait_ge(*pool_set.at(0, "hb"))
            run(e, {"A": stream_a, "B": stream_b, "M": stream_m}, DVE_ORDER, setup=setup)

        @block.tensor
        def _(e):
            for s in (pe_a, pe_b):
                e.sem_inc(*s.start())
            e.wait_ge(mats_loaded, 16)

            def columns(slot, at, w, name_or_tile):
                for m in range(CC):
                    for cc in range(CC):
                        v = col(name_or_tile, cc) if isinstance(name_or_tile, str) else name_or_tile[:, cc:cc + 1]
                        mm = e.matmul(SLOT[slot][:, at + m:at + m + 1], w[:, cc, m * P:(m + 1) * P], v,
                                      start=(cc == 0), stop=(cc == CC - 1))
                return mm

            def setup():
                e.wait_ge(early_loaded, 16 * EARLY_N)
                columns("bD0", 0, WK, "kv_ln_b")
                columns("bD0", 2, WV, "kv_ln_b")
                columns("bD0", 4, WP1, "ln_b").then_inc(*pe_set.step("fold"))
                for cc in range(CC):
                    mm = e.matmul(SLOT["bD1"][:, cc * P:(cc + 1) * P], XPR[:, cc, :], DTP[:, cc, :], start=True, stop=True)
                mm.then_inc(*pe_set.step("wd"))
                e.wait_ge(*dve_set.at(0, "pb1"))
                columns("bD0", 0, WP0, VB).then_inc(*pe_set.step("fold0"))

            LAST = {"aA0": (act_a, "xd1_0"), "aA1": (act_a, "xd1_1"), "aD0": (dve_a, "ln_var1_0"), "aD1": (dve_a, "ln_var1"),
                    "bA0": (act_b, "we"), "bA1": (act_b, "pat"), "bD0": (dve_b, "hm3"), "bD1": (dve_b, "sc0")}
            state = {}

            def take(b, slot, engine, label):
                if slot in state:
                    e.wait_ge(*state[slot][0].at(b, state[slot][1]))
                else:
                    e.wait_ge(*LAST[slot][0].at(b - 1, LAST[slot][1]))
                state[slot] = (engine, label)
                return SLOT[slot]

            def done(stream):
                for slot in [x for x in state if x[0] == stream]:
                    assert state[slot] == LAST[slot], slot
                    del state[slot]

            def group_norm(b, l, pe, dve, slot):
                MV = GN["A" if l < 2 else "B"][2]
                s = take(b, slot, dve, f"gn_gm{l}")
                e.wait_ge(*dve.at(b, f"gn_ex2{l}"))
                e.matmul(s[:, 0:4], mat("mean_group"), MV[:, :, :].rearrange("p c s -> p (c s)"), start=True, stop=True)\
                 .then_inc(*pe.step(f"gn{l}"))
                yield

            def product(s, w, src, half):
                for cc in range(CC):
                    mm = e.matmul(s[:, :], w(cc), src[:, cc, hs(half)], start=(cc == 0), stop=(cc == CC - 1))
                return mm

            def project(b, w, src, ready, pe, name, slots, engine, label):
                for m, half in BLOCKS:
                    s = take(b, f"{slots}{half}", engine, f"{label}{m}_{half}")
                    if ready:
                        e.wait_ge(*ready)
                    product(s, lambda cc: w[:, cc, m * P:(m + 1) * P], src, half).then_inc(*pe.step(f"{name}{m}_{half}"))
                    yield

            def sums(b, l, src, ready):
                pe, act, dve, _, banks, squares, _, _ = NORM["A" if l == 1 else "B"]
                for half in range(2):
                    s = take(b, f"{banks}A{half}", act, f"ln_m2{l}_{half}")
                    e.wait_ge(*dve.at(b, ready))
                    product(s, lambda cc: mat("mean256"), src, half).then_inc(*pe.step(f"mean{l}_{half}"))
                    yield
                for half in range(2):
                    s = take(b, f"{banks}D{half}", dve, f"ln_var{l}" if half else f"ln_var{l}_0")
                    e.wait_ge(*act.at(b, f"sq{l}_1"))
                    product(s, lambda cc: mat("mean256"), squares, half).then_inc(*pe.step(f"msq{l}_{half}"))
                    yield

            def down(b):
                s = take(b, "aA0", act_a, "xds1")
                e.wait_ge(*dve_a.at(b, "g0_1"))
                for m in range(CC):
                    for n in range(4 * CC):
                        cc, dy, dx = n // 4, n % 4 // 2, n % 2
                        src = GA0[:, cc, :].rearrange("p (h w) -> p h w", h=H)[:, dy::2, dx::2]
                        mm = e.matmul(s[:, m * NK:(m + 1) * NK], WDS[:, cc, n % 4, m * P:(m + 1) * P], src,
                                      start=(n == 0), stop=(n == 4 * CC - 1))
                mm.then_inc(*pe_a.step("ds"))
                yield

            def kv_norm(b):
                s = take(b, "aD0", dve_a, "ln_var0")
                e.wait_ge(*act_a.at(b, "sq_ds"))
                for at, src in ((0, XDS), (NK, SQD)):
                    for cc in range(CC):
                        mm = e.matmul(s[:, at:at + NK], mat("mean256"), src[:, cc, :], start=(cc == 0), stop=(cc == CC - 1))
                mm.then_inc(*pe_a.step("msq0"))
                yield

            def keys(b):
                s = take(b, "aA0", act_a, "kf1")
                e.wait_ge(*dve_set.at(0, "wp11"))
                e.wait_ge(*dve_a.at(b, "n0_1"))
                for m in range(CC):
                    for cc in range(CC):
                        mm = e.matmul(s[:, m * NK:(m + 1) * NK], WK[:, cc, m * P:(m + 1) * P], XDS[:, cc, :],
                                      start=(cc == 0), stop=(cc == CC - 1))
                mm.then_inc(*pe_a.step("k"))
                yield
                s = take(b, "aD1", dve_a, "vt")
                for kt in range(2):
                    for cc in range(CC):
                        mm = e.matmul(s[:, kt * C:(kt + 1) * C], XDS[:, cc, kt * P:(kt + 1) * P], WV[:, cc, :],
                                      start=(cc == 0), stop=(cc == CC - 1))
                mm.then_inc(*pe_a.step("vT"))
                yield

            def scores(b, h):
                if h == 0:
                    e.wait_ge(stacked, 16 * STACK_DMAS * b + 16 * STACK_DMAS)
                for j in range(4):
                    s = take(b, f"aD{j % 2}", dve_a, f"mx{h}_{j}")
                    for t in range(2):
                        qt = 2 * j + t
                        mm = e.matmul(s[:, t * NK:(t + 1) * NK], QST[0:96, h, qt * P:(qt + 1) * P], KST[0:96, h, :],
                                      start=True, stop=True)
                    mm.then_inc(*pe_a.step(f"s{h}_{j}"))
                    yield

            def max_rows(b, g):
                s = take(b, "aD0", dve_a, f"ml{g}")
                e.wait_ge(*dve_a.at(b, f"mx{4 * g + 3}_3"))
                e.transpose(s[0:32, 0:P], NEGMAX[:, 4 * g:4 * g + 4, :].rearrange("p h t -> p (h t)"), mat("ident"))\
                 .then_inc(*pe_a.step(f"mT{g}"))
                yield

            def scores_t(b, h):
                if h % 4 == 0:
                    e.wait_ge(maxed, 16 * MAX_DMAS * b + 16 * 2 * (h // 4 + 1))
                    e.wait_ge(*pool_set.at(0, "hb"))
                for kt, half in BLOCKS:
                    s = take(b, f"aA{half}", act_a, f"p{h}_{kt}_{half}")
                    e.matmul(s[:, :], KST[0:98, h, kt * P:(kt + 1) * P], QST[0:98, h, hs(half)], start=True, stop=True)\
                     .then_inc(*pe_a.step(f"st{h}_{kt}_{half}"))
                    yield

            def weighted(b, h):
                s = take(b, "aD1", dve_a, f"o{h}")
                e.wait_ge(*act_a.at(b, f"p{h}_1_1"))
                for qt in range(QT):
                    for kt in range(2):
                        mm = e.matmul(s[:, qt * (HD + 1):(qt + 1) * (HD + 1)],
                                      PT[:, 2 * (h % 2) + kt, qt * P:(qt + 1) * P], VT[:, kt, h, :],
                                      start=(kt == 0), stop=(kt == 1))
                mm.then_inc(*pe_a.step(f"pv{h}"))
                yield

            def transpose(b):
                for cc, half in BLOCKS:
                    s = take(b, f"aA{half}", act_a, f"oc{cc}_{half}")
                    e.wait_ge(*dve_a.at(b, f"o{4 * cc + 3}"))
                    for t in range(4):
                        mm = e.transpose(s[:, t * P:(t + 1) * P], OT[:, 4 * half + t, cc * P:(cc + 1) * P], mat("ident"))
                    mm.then_inc(*pe_a.step(f"oT{cc}_{half}"))
                    yield

            def convolve(b, cc):
                e.wait_ge(*pool_set.at(0, "wtap1_2"))
                e.wait_ge(*act_a.at(b, "xn3"))
                for half in range(2):
                    s = take(b, f"aA{half}", act_a, f"xd{cc}_{half}")
                    for n in range(TAPS):
                        dy, dx = n // 3, n % 3
                        mm = e.matmul(s[:, :], WTAP[:, cc, n, :], XNP[:, cc, dy + 16 * half:dy + 16 * half + 16, dx:dx + W],
                                      start=(n == 0), stop=(n == TAPS - 1))
                    mm.then_inc(*pe_a.step(f"xd{cc}_{half}"))
                    yield

            def gate_z(b):
                for cc, half in BLOCKS:
                    s = take(b, f"bA{half}", act_b, f"z{cc}_{half}")
                    e.matmul(s[:, :], IPZ[:, cc, :], XNP[:, cc, 1 + 16 * half:17 + 16 * half, 1:1 + W], start=True, stop=True)\
                     .then_inc(*pe_b.step(f"z{cc}_{half}"))
                    yield

            def small_mlp(b, at, means, sources, l, steps):
                s = take(b, "bD0", dve_b, f"hm{l}")
                e.wait_ge(*sources)
                for cc in range(CC):
                    mm = e.matmul(s[0:16, 0:1], W1S[:, cc, 16 * at:16 * at + 16], means[:, cc:cc + 1], start=(cc == 0), stop=(cc == 1))
                mm.then_inc(*pe_b.step(steps[0]))
                yield
                s = take(b, "bD1", dve_b, "sc0" if at else "gate_in")
                e.wait_ge(*dve_b.at(b, f"hm{l}"))
                for m in range(CC):
                    mm = e.matmul(s[:, m:m + 1], S16[:, at * C + m * P:at * C + (m + 1) * P], HM[:, :], start=True, stop=True)
                mm.then_inc(*pe_b.step(steps[1]))
                yield

            def by_chunk(b, cc, slots, engine, label, w, step, src):
                for half in range(2):
                    s = take(b, f"{slots}{half}", engine, f"{label}_{half}")
                    e.matmul(s[:, :], w, src[:, cc, hs(half)], start=True, stop=True).then_inc(*pe_b.step(f"{step}{cc}_{half}"))
                    yield

            def delta(b):
                for cc in range(CC):
                    e.wait_ge(*act_b.at(b, f"u{cc}"))
                    yield from by_chunk(b, cc, "bA", act_b, f"v{cc}", WD[:, cc, :], "v", U)

            def scan(b, cc):
                yield from by_chunk(b, cc, "bD", dve_b, f"dbu{cc}", XB[:, cc, :], "B", U)
                yield from by_chunk(b, cc, "bD", dve_b, f"hc{cc}", XC[:, cc, :], "C", U)

            def centred(b):
                for cc in range(CC):
                    e.wait_ge(*dve_b.at(b, f"y{cc}"))
                    yield from by_chunk(b, cc, "bA", act_b, f"ysq{cc}", mat("center64"), "yc", U)

            def y_variance(b):
                for cc in range(CC):
                    for half in range(2):
                        s = take(b, f"bA{half}", act_b, f"yln{cc}_{half}")
                        e.wait_ge(*act_b.at(b, f"ysq{cc}_{half}"))
                        e.matmul(s[:, :], mat("mean64"), SQ[:, cc, hs(half)], start=True, stop=True)\
                         .then_inc(*pe_b.step(f"yv{cc}_{half}"))
                        yield

            def gated(b):
                for cc in range(CC):
                    for half in range(2):
                        s = take(b, f"bD{half}", dve_b, f"xm{2 * cc + 1}_{half}")
                        e.wait_ge(*dve_b.at(b, f"yz{cc}"))
                        e.matmul(s[:, :], OPW[:, cc, :], G[:, cc, hs(half)], start=True, stop=True)\
                         .then_inc(*pe_b.step(f"op{cc}_{half}"))
                        yield

            def pixel_rows(b):
                for t in range(4):
                    s = take(b, f"bA{t % 2}", act_b, f"xnt{t}")
                    e.wait_ge(*dve_b.at(b, "n3_1"))
                    for i in range(2):
                        for cc in range(CC):
                            mm = e.transpose(s[:, i * C + cc * P:i * C + (cc + 1) * P],
                                             G[:, cc, (2 * t + i) * P:(2 * t + i + 1) * P], mat("ident"))
                    mm.then_inc(*pe_b.step(f"xnT{t}"))
                    yield

            def gram(b):
                for m in range(CC):
                    s = take(b, f"bD{m}", dve_b, f"gram{m}")
                    e.wait_ge(*act_b.at(b, "xnt3"))
                    e.wait_ge(*dve_b.at(b, "xnt_ones"))
                    for t in range(QT):
                        mm = e.matmul(s[:, 0:C + 1], XNT[:, t, m * P:(m + 1) * P], XNT[:, t, :],
                                      start=(t == 0), stop=(t == QT - 1))
                    mm.then_inc(*pe_b.step(f"gram{m}"))
                    yield

            def channel_scores(b):
                s = take(b, "bD0", dve_b, "srow")
                e.wait_ge(*dve_b.at(b, "gram1"))
                for cc in range(CC):
                    e.matmul(s[0:1, cc * P:(cc + 1) * P], GRAM[:, cc, C:C + 1], mat("ident"), start=True, stop=True)
                for cc in range(CC):
                    e.matmul(s[0:1, C:2 * C], GRAM[:, cc, C:C + 1], W2Q[:, cc, :], start=(cc == 0), stop=False)
                e.matmul(s[0:1, C:2 * C], ROWS[:, 2 * C:2 * C + 1], ROWS[:, 0:C], start=False, stop=True)\
                 .then_inc(*pe_b.step("rows"))
                yield
                s = take(b, "bA0", act_b, "t1")
                e.wait_ge(*dve_b.at(b, "srow"))
                for m in range(CC):
                    for cc in range(CC):
                        e.matmul(s[:, m * C:(m + 1) * C], GRAM[:, cc, m * P:(m + 1) * P], W2Q[:, cc, :], start=(cc == 0), stop=False)
                    mm = e.matmul(s[:, m * C:(m + 1) * C], SROW[:, m * P:(m + 1) * P], ROWS[:, 0:C], start=False, stop=True)
                mm.then_inc(*pe_b.step("T1"))
                yield
                s = take(b, "bD1", dve_b, "aok3")
                e.wait_ge(*act_b.at(b, "t1"))
                for m in range(CC):
                    for cc in range(CC):
                        e.matmul(s[:, m * P:(m + 1) * P], T1[:, cc, m * P:(m + 1) * P], W2K[:, cc, m * P:(m + 1) * P],
                                 start=(cc == 0), stop=False)
                    mm = e.matmul(s[:, m * P:(m + 1) * P], SROW[:, C + m * P:C + (m + 1) * P],
                                  ROWS[:, C + m * P:C + (m + 1) * P], start=False, stop=True)
                mm.then_inc(*pe_b.step("A"))
                yield

            def attended(b):
                s = take(b, "bA1", act_b, "pat")
                e.wait_ge(*dve_b.at(b, "abd3"))
                for m in range(CC):
                    mm = e.matmul(s[:, m * C:(m + 1) * C], ABD[:, m, :], WP2[:, m, :], start=True, stop=True)
                mm.then_inc(*pe_b.step("PAT"))
                yield
                s = take(b, "bA0", act_b, "we")
                e.wait_ge(*act_b.at(b, "pat"))
                for m in range(CC):
                    for cc in range(CC):
                        mm = e.matmul(s[:, m * C:(m + 1) * C], W2V[:, cc, m * P:(m + 1) * P], PAT[:, cc, :],
                                      start=(cc == 0), stop=(cc == 1))
                mm.then_inc(*pe_b.step("WE"))
                yield
                take(b, "bD0", dve_b, "be")
                columns("bD0", 0, PAT, "v2_b").then_inc(*pe_b.step("be"))
                yield

            def stream_a(b, setup=None):
                yield from group_norm(b, 0, pe_a, dve_a, "aD0")
                if setup:
                    setup()
                yield from down(b)
                yield from project(b, WQ, GA0, None, pe_a, "q", "aA", act_a, "qf")
                yield from kv_norm(b)
                yield from keys(b)
                for h in range(4):
                    yield from scores(b, h)
                yield from max_rows(b, 0)
                for h in range(HEADS):
                    if h < 4:
                        yield from scores(b, 4 + h)
                        if h == 3:
                            yield from max_rows(b, 1)
                    yield from scores_t(b, h)
                    if h >= 1:
                        yield from weighted(b, h - 1)
                yield from weighted(b, HEADS - 1)
                yield from transpose(b)
                yield from project(b, WP0, OC, act_a.at(b, "oc1_1"), pe_a, "proj0_", "aD", dve_a, "x1_")
                yield from group_norm(b, 1, pe_a, dve_a, "aD0")
                yield from sums(b, 1, GA0, "g1_1")
                yield from convolve(b, 0)
                yield from convolve(b, 1)
                done("a")

            def stream_b(b):
                yield from gate_z(b)
                yield from small_mlp(b, 0, GAPX, dve_b.at(b, "gap1"), 1, ("fc1", "fc2"))
                yield from delta(b)
                yield from scan(b, 0)
                yield from scan(b, 1)
                yield from centred(b)
                yield from y_variance(b)
                yield from gated(b)
                yield from sums(b, 2, XM, "xm3_1")
                yield from project(b, WP1, XM, dve_b.at(b, "n2_1"), pe_b, "proj1_", "bD", dve_b, "x2_")
                yield from group_norm(b, 2, pe_b, dve_b, "bD0")
                yield from sums(b, 3, G, "g2_1")
                yield from pixel_rows(b)
                yield from gram(b)
                yield from channel_scores(b)
                yield from attended(b)
                yield from project(b, WE, G, act_b.at(b, "we"), pe_b, "out_", "bD", dve_b, "x3_")
                yield from group_norm(b, 3, pe_b, dve_b, "bD0")
                yield from small_mlp(b, 1, GAP, dve_b.at(b, "gap3b"), 3, ("w1", "w2"))
                done("b")

            def before_b():
                e.wait_ge(*dve_set.at(0, "pb0"))
                e.wait_ge(late_loaded, 16 * LATE_N)

            run(e, {"A": stream_a, "B": stream_b}, PE_ORDER, before_b, setup)

        return {"PE_A": pe_a, "PE_B": pe_b, "ACT_A": act_a, "ACT_B": act_b, "ACT_M": act_m, "DVE_A": dve_a,
                "DVE_B": dve_b, "DVE_M": dve_m, "POOL_A": pool_a, "POOL_B": pool_b, "POOL_M": pool_m,
                "PE_SETUP": pe_set, "ACT_SETUP": act_set, "DVE_SETUP": dve_set, "POOL_SETUP": pool_set}


def _arrays(i):
    import numpy as np
    f = {k: np.ascontiguousarray(v) for k, v in i.items()}

    def t2(w):
        return w.T.reshape(CC, P, -1).transpose(1, 0, 2)

    def vec(v):
        return np.asarray(v).reshape(CC, P).T

    def pairs(blocks, rows=64):
        a = np.zeros((2 * rows, CC, P), np.float32)
        for g in range(GROUPS):
            h = g % 2
            a[rows * h:rows * h + rows, g // 2, 64 * h:64 * h + 64] = blocks[g]
        return a

    L0, L1, L2, L3 = "L0_conv_", "L1_conv_", "L2_conv_", "L3_conv_"
    kvw, kvb = f[L0 + "kv_w"], f[L0 + "kv_b"]
    vecs = dict(q_b=f[L0 + "q_b"], k_b=kvb[:C], v_b=kvb[C:], ds_b=f[L0 + "ds_b"], kv_ln_w=f[L0 + "ln_w"],
                kv_ln_b=f[L0 + "ln_b"], pb0=f[L0 + "proj_b"], ln_g=f[L1 + "ln_g"], ln_b=f[L1 + "ln_b"],
                fc2_b=f[L1 + "fc2_b"], skip=np.broadcast_to(f[L1 + "skip_scale"], (C,)), conv_b=f[L1 + "conv_b"],
                dt_b=f[L1 + "dt_proj_b"], A_log=f[L1 + "A_log"], Ds=f[L1 + "Ds_p"], og=f[L1 + "onorm_g"],
                ob=f[L1 + "onorm_b"], pb1=f[L1 + "proj_b"], v2_b=f[L2 + "qkv_b"][2 * C:], pb2=f[L2 + "proj_b"],
                w2_b=f[L3 + "b2"])
    eye, one = np.eye(P, dtype=np.float32), np.ones((P, P), np.float32)
    b64 = np.kron(np.eye(2), np.ones((64, 64))).astype(np.float32) / 64
    b8 = np.kron(np.eye(16), np.ones((8, 8))).astype(np.float32) / 32
    kern = []
    for g in range(GROUPS):
        k = f[L1 + "conv_w"][g, :, 0]
        k = k.transpose(0, 2, 1) if g % 2 else k
        kern.append(k[:, ::-1, ::-1] if g >= 2 else k)
    cw = np.stack([np.concatenate([kern[2 * c].reshape(64, 9), kern[2 * c + 1].reshape(64, 9)]).T for c in range(CC)])
    ip, xp = f[L1 + "in_proj_w"], f[L1 + "x_proj_w"]
    qkv, qb = f[L2 + "qkv_w"], f[L2 + "qkv_b"]
    kidx = np.broadcast_to(np.array([-1, 1, 2, 3, 4, 5, np.float32(3.4e38), np.float32(3.4e38)], np.float32), (P, 8))
    a = dict(
        x=f["x"], cols=np.stack([vec(vecs[n]) for n in COLS], -1),
        mats=np.stack([eye, one / 256, b64, eye - b64, b8], 1),
        wq=t2(f[L0 + "q_w"]), wk=t2(kvw[:C]), wv=t2(kvw[C:]),
        wds=f[L0 + "ds_w"].transpose(1, 2, 3, 0).reshape(CC, P, 4, C).transpose(1, 0, 2, 3), wp0=t2(f[L0 + "proj_w"]),
        small16=np.concatenate([f[L1 + "fc2_w"].T, f[L3 + "w2"].T, f[L1 + "fc1_b"][:, None], f[L3 + "b1"][:, None]], 1),
        w1s=np.concatenate([t2(f[L1 + "fc1_w"]), t2(f[L3 + "w1"])], 2),
        ipx=pairs([ip[g, :64].T for g in range(GROUPS)]), ipz=pairs([ip[g, 64:].T for g in range(GROUPS)]),
        cw=cw.reshape(3, 768),
        xpr=pairs([xp[g, :8] for g in range(GROUPS)], 8), dtp=pairs([f[L1 + "dt_proj_w"][g].T for g in range(GROUPS)], 8),
        xb=pairs([np.broadcast_to(xp[g, 8][:, None], (64, 64)) for g in range(GROUPS)]),
        xc=pairs([np.broadcast_to(xp[g, 9][:, None], (64, 64)) for g in range(GROUPS)]),
        opw=pairs([f[L1 + "out_proj_w"][g].T for g in range(GROUPS)]), wp1=t2(f[L1 + "proj_w"]),
        w2q=t2(qkv[:C]), w2k=t2(qkv[C:2 * C]), w2v=qkv[2 * C:].reshape(CC, P, C).transpose(1, 0, 2), wp2=t2(f[L2 + "proj_w"]),
        rows=np.concatenate([qb[:C], qb[C:2 * C], np.array([N], np.float32)])[None], kidx=kidx)
    return {k: np.ascontiguousarray(v) for k, v in a.items()}


def kernel(**inputs):
    import concourse.bacc as _bacc
    from concourse import mybir as _mybir
    from concourse.bass_utils import run_bass_kernel_spmd as _run

    nc = _bacc.Bacc("TRN2", target_bir_lowering=False, num_devices=1)
    arrays, args = {}, []
    for name, v in _arrays(inputs).items():
        arrays[f"in_{name}"] = v
        args.append(nc.dram_tensor(f"in_{name}", v.shape, _mybir.dt.from_np(v.dtype), kind="ExternalInput").ap())
    args.append(nc.dram_tensor("out_0", (B, C, H, W), _mybir.dt.float32, kind="ExternalOutput").ap())
    program(nc, *args)
    r = _run(nc, [arrays], core_ids=[0])
    return r.results[0]["out_0"]
```

```python
import concourse.bass as bass
from concourse import mybir
from contextlib import ExitStack

B, C, H, W = 4, 256, 32, 32
N = H * W
P = 128
CC = C // P
HALF = 512
HEADS, HD = 8, 32
NK = N // 4
QT = N // P
GROUPS = 4
TAPS = 9
KPOOL = 7
LOWEST = -3.0e38
SOFTPLUS_LINEAR = 20.0
EXP_LN_TABLE, SILU_TABLE = 6, 18
STREAMS = "ABM"
COLS = ["q_b", "k_b", "v_b", "ds_b", "kv_ln_w", "kv_ln_b", "pb0", "ln_g", "ln_b", "fc2_b", "skip",
        "conv_b", "dt_b", "A_log", "Ds", "og", "ob", "pb1", "v2_b", "pb2", "w2_b"]
MATS = ["ident", "mean256", "mean64", "center64", "mean_group"]

PE_A = """
gn0 ds q0_0 q0_1 q1_0 q1_1 msq0 k vT s0_0 s0_1 s0_2 s0_3 s1_0 s1_1 s1_2 s1_3 s2_0 s2_1 s2_2 s2_3
s3_0 s3_1 s3_2 s3_3 mT0 st0_0_0 st0_0_1 st0_0_2 st0_0_3 st0_1_0 st0_1_1 st0_1_2 st0_1_3 s4_0 s4_1
s4_2 s4_3 s5_0 s5_1 s5_2 s5_3 pv0_0 st1_0_0 st1_0_1 st1_0_2 st1_0_3 pv0_1 s6_0 s6_1 s6_2 s6_3 s7_0
s7_1 s7_2 s7_3 mT1 st1_1_0 st1_1_1 st1_1_2 st1_1_3 pv1_0 pv1_1 st2_0_0 st2_0_1 st2_0_2 st2_0_3
st2_1_0 st2_1_1 st2_1_2 st2_1_3 pv2_0 st3_0_0 st3_0_1 st3_0_2 st3_0_3 pv2_1 st3_1_0 st3_1_1 st3_1_2
st3_1_3 pv3_0 pv3_1 proj0_0_0 proj0_0_1 proj0_1_0 proj0_1_1 gn1 sums1_0 sums1_1 xd0_0 xd0_1 xd1_0
xd1_1
"""
PE_B = """
z0_0 z0_1 z1_0 z1_1 fc1 fc2 v0_0 v0_1 v1_0 v1_1 B0_0 B0_1 C0_0 C0_1 B1_0 B1_1 C1_0 C1_1 yc0_0 yc0_1
yc1_0 yc1_1 yv0_0 yv0_1 yv1_0 yv1_1 op0_0 op0_1 op1_0 op1_1 sums2_0 sums2_1 proj1_0_0 proj1_0_1
proj1_1_0 proj1_1_1 gn2 sums3_0 sums3_1 xnT0 xnT1 xnT2 xnT3 gram0 gram1 rows T1 A PAT WE be out_0_0
out_0_1 out_1_0 out_1_1 gn3 w1 w2
"""
ACT_A = """
gn_ln0 gn_rstd0 xds0 xds1 sq_ds qf0_0 qf0_1 qf1_0 qf1_1 ln_ln0 ln_rstd0 kf0 kf1 p0_0_0 p0_0_1 p0_0_2
p0_0_3 p0_1_0 p0_1_1 p0_1_2 p0_1_3 p1_0_0 p1_0_1 p1_0_2 p1_0_3 lz0 rz0 p1_1_0 p1_1_1 p1_1_2 p1_1_3
p2_0_0 p2_0_1 p2_0_2 p2_0_3 lz1 rz1 p2_1_0 p2_1_1 p2_1_2 p2_1_3 p3_0_0 p3_0_1 p3_0_2 p3_0_3 lz2 rz2
p3_1_0 p3_1_1 p3_1_2 p3_1_3 lz3 rz3 gn_ln1 gn_rstd1 sq1_0 sq1_1 ln_mean1_0_0 ln_mean1_0_64 ln_m21_0
ln_mean1_1_0 ln_mean1_1_64 ln_m21_1 ln_ln1 ln_rstd_high1 ln_rstd1 xn0 xn1 xn2 xn3 xr0 xr xd0_0 xd0_1
xd1_0 xd1_1
"""
ACT_B = """
z0_0 z0_1 z1_0 z1_1 gate_exp u0 u1 zs v0_0 v0_1 v1_0 v1_1 ev0 lv0 ev1 lv1 dA0 dA1 yc0_0 ysq0_0 yc0_1
ysq0_1 yc1_0 ysq1_0 yc1_1 ysq1_1 yln0_0 yln0_1 yrs0 yln1_0 yln1_1 yrs1 ya0 ya1 sq2_0 sq2_1
ln_mean2_0_0 ln_mean2_0_64 ln_m22_0 ln_mean2_1_0 ln_mean2_1_64 ln_m22_1 ln_ln2 ln_rstd_high2
ln_rstd2 gn_ln2 gn_rstd2 sq3_0 sq3_1 ln_mean3_0_0 ln_mean3_0_64 ln_m23_0 ln_mean3_1_0 ln_mean3_1_64
ln_m23_1 ln_ln3 ln_rstd_high3 ln_rstd3 xnt0 xnt1 xnt2 xnt3 t1 aexp0 aexp1 pat we gn_ln3 gn_rstd3
"""
ACT_M = """
a0 a1 y1_0_0 y1_0_1 y1_1_0 y1_1_1 y2_0_0 y2_0_1 y2_1_0 y2_1_1 y3_0_0 y3_0_1 y3_1_0 y3_1_1 y4_0_0
y4_0_1 y4_1_0 y4_1_1 y5_0_0 y5_0_1 y5_1_0 y5_1_1 y6_0_0 y6_0_1 y6_1_0 y6_1_1
"""
DVE_A = """
gn_st0_00 gn_st0_01 gn_st0_10 gn_st0_11 gn_m20 gn_m0 gn_sq0 gn_ex20 gn_gm0 gn_gm20 gn_var0 gn_b0
g0_0 g0_1 qh0 qh1 ln_mean0 ln_m20 ln_var0 c0_0 c0_1 n0_0 n0_1 kh vt mx0_0 mx0_1 mx0_2 mx0_3 mx1_0
mx1_1 mx1_2 mx1_3 mx2_0 mx2_1 mx2_2 mx2_3 mx3_0 mx3_1 mx3_2 mx3_3 mh0 ml0 mx4_0 mx4_1 mx4_2 mx4_3
mx5_0 mx5_1 mx5_2 mx5_3 o0 mx6_0 mx6_1 mx6_2 mx6_3 mx7_0 mx7_1 mx7_2 mx7_3 mh1 ml1 o1 o2 o3 x1_0_0
x1_0_1 x1_1_0 x1_1_1 gn_st1_00 gn_st1_01 gn_st1_10 gn_st1_11 gn_m21 gn_m1 gn_sq1 gn_ex21 gn_gm1
gn_gm21 gn_var1 gn_b1 g1_0 g1_1 ln_var1_0 ln_var1 n1_0 n1_1
"""
DVE_B = """
gap1 hm1 gate_in gate_1p vmin0 vmin1 gate gs delta0 du0 delta1 du1 dbu0_0 dbu0_1 scan0 hc0_0 hc0_1
y0 dbu1_0 dbu1_1 scan1 hc1_0 hc1_1 y1 yn0 yn1 yz0 yz1 xm0_0 xm1_0 xm0_1 xm1_1 xm2_0 xm3_0 xm2_1
xm3_1 ln_var2_0 ln_var2 n2_0 n2_1 x2_0_0 x2_0_1 x2_1_0 x2_1_1 gn_st2_00 gn_st2_01 gn_st2_10
gn_st2_11 gn_m22 gn_m2 gn_sq2 gn_ex22 gn_gm2 gn_gm22 gn_var2 gn_b2 g2_0 g2_1 ln_var3_0 ln_var3
xnt_ones n3_0 n3_1 gram0 gram1 srow ab0 aok0 ab1 aok1 ab2 aok2 ab3 aok3 aclip anan amax arow arec
arok afill ap0 ap1 abd0 abd1 abd2 abd3 be x3_0_0 x3_0_1 x3_1_0 x3_1_1 gn_st3_00 gn_st3_01 gn_st3_10
gn_st3_11 gn_m23 gn_m3 gn_sq3 gn_ex23 gap3 gn_gm3 gn_gm23 gn_var3 gn_b3 gap3a gap3b hm3 sc0 sc cge0
cge1 qs eq fb fs0 fs ws0 ws1 wb0 wb1 cf0 cf1 c1 c0 coef
"""
DVE_M = """
hp1_0 h1_0_0 h1_0_1 vp1_0 u1_0 v1_0 hp1_1 h1_1_0 h1_1_1 vp1_1 u1_1 v1_1 hp2_0 h2_0_0 h2_0_1 vp2_0
u2_0 v2_0 hp2_1 h2_1_0 h2_1_1 vp2_1 u2_1 v2_1 hp3_0 h3_0_0 h3_0_1 vp3_0 u3_0 v3_0 hp3_1 h3_1_0
h3_1_1 vp3_1 u3_1 v3_1 hp4_0 h4_0_0 h4_0_1 vp4_0 u4_0 v4_0 hp4_1 h4_1_0 h4_1_1 vp4_1 u4_1 v4_1 hp5_0
h5_0_0 h5_0_1 vp5_0 u5_0 v5_0 hp5_1 h5_1_0 h5_1_1 vp5_1 u5_1 v5_1 hp6_0 h6_0_0 h6_0_1 vp6_0 u6_0
v6_0 hp6_1 h6_1_0 h6_1_1 vp6_1 u6_1 v6_1
"""
POOL_A = """
ql0 ql1 kl c1_0 c1_1
"""
POOL_B = """
c2_0 c2_1 c3_0 c3_1
"""
POOL_M = """
add1_0_0 add1_0_1 add1_1_0 add1_1_1 add2_0_0 add2_0_1 add2_1_0 add2_1_1 add3_0_0 add3_0_1 add3_1_0
add3_1_1 add4_0_0 add4_0_1 add4_1_0 add4_1_1 add5_0_0 add5_0_1 add5_1_0 add5_1_1 add6_0_0 add6_0_1
add6_1_0 add6_1_1
"""
PE_SETUP = """
fold wd fold0
"""
ACT_SETUP = """
expA negA
"""
DVE_SETUP = """
eps0 eps1 qbs kb vb pb1 wk0 wv0 wp10 wk1 wv1 wp11 wd pb0
"""
POOL_SETUP = """
kst1 ones abd xnp pa pb hb wtap0_0 wtap0_1 wtap1_1 wtap1_2
"""
PE_ORDER = """
A1 B6 A1 B4 A4 B1 A1 B3 A1 B6 A1 B1 A2 B1 A1 B1 A2 B1 A2 B1 A1 B1 A9 B2 A1 B1 A3 B1 A8 B1 A2 B1 A8
B1 A1 B1 A2 B1 A2 B1 A12 B1 A9 B1 A1 B1 A8 B2 A1 B2 A3 B3 A1 B2 A2 B7 A1 B1 A1 B2 A2
"""
ACT_ORDER = """
B1 A2 B1 M1 B2 M1 B1 M1 B1 A2 B1 M1 B2 A1 B3 A1 B1 A1 B2 A1 M2 A1 B1 A1 M1 A3 M1 B16 A1 M1 A2 M1 A3
B2 A1 B4 A1 B5 A6 M2 A3 M2 A4 B1 A2 B1 A3 B1 A1 M1 B1 A1 M1 A1 M1 B1 A1 B1 A1 M1 B2 A1 M1 B2 A5 B1
A1 B2 M2 A2 B4 M2 A1 M1 A1 M1 A1 B1 A1 M1 B2 A6 B1 A3 B1 A4 B1 A3 B1 A3
"""
DVE_ORDER = """
A2 B1 A3 M2 A6 M2 A3 B1 M1 B1 M2 B1 M9 B1 M2 B2 M3 B4 A1 B1 A1 B1 A2 B1 A1 B1 A1 B1 A3 M1 B2 A1 M1
B6 M2 A8 B1 A5 M1 A2 B1 A2 B2 A2 B8 A2 M1 A2 M1 A1 M1 A1 B1 A2 B1 M5 B2 M3 A2 B2 A3 B1 A1 B1 A3 B1
A1 B1 A1 M2 B1 M1 B1 M3 B7 M1 B1 A1 M1 B2 M14 B2 M1 A1 B1 M2 B2 A1 M1 A1 M1 A1 M2 A1 M2 A1 M1 A1 M2
A2 B1 M1 A2 B1 A4 B1 A5 B20 A1 B1 A1 B1 A2 B20
"""
POOL_ORDER = """
M2 A2 M4 A1 M1 B1 M1 B1 M9 B2 M5 A2 M2
"""


def unpack(order):
    return [s for word in order.split() for s in word[0] * int(word[1:])]


class Steps:

    def __init__(self, sem, text, lead=1):
        self.lead = lead
        self.sem, self.labels, self.said = sem, text.split(), []
        self.index = {x: n for n, x in enumerate(self.labels)}

    def step(self, label):
        n = len(self.said) % max(len(self.labels), 1)
        assert self.labels[n] == label, (label, self.labels[n])
        self.said.append(label)
        return self.sem, 1

    def at(self, b, label):
        return self.sem, (b + self.lead) * len(self.labels) + self.index[label] + 1

    def start(self):
        return self.sem, max(self.lead * len(self.labels), 1)


def program(nc, x, cols, mats, wq, wk, wv, wds, wp0, small16, w1s, ipx, ipz, cw, xpr, dtp, xb, xc, opw,
            wp1, w2q, w2k, w2v, wp2, rows, kidx, out):
    f32, f16 = mybir.dt.float32, mybir.dt.float16
    ALU, ACT, AX = mybir.AluOpType, mybir.ActivationFunctionType, mybir.AxisListType
    SCALE = HD ** -0.5
    ctx = ExitStack()
    with ctx:
        def sb(name, shape, dt=f32):
            return ctx.enter_context(nc.sbuf_tensor(name, shape, dt))

        def sem(name):
            return ctx.enter_context(nc.semaphore(name))

        COL = sb("COL", [P, CC, len(COLS)])
        MAT = sb("MAT", [P, len(MATS), P])
        WQ, WK, WV, WP0 = (sb(n, [P, CC, C]) for n in ("WQ", "WK", "WV", "WP0"))
        WDS = sb("WDS", [P, CC, 4, C])
        S16 = sb("S16", [16, 2 * C + 2])
        W1S = sb("W1S", [P, CC, 32])
        IPZ, XB, XC, WD, OPW = (sb(n, [P, CC, P]) for n in ("IPZ", "XB", "XC", "WD", "OPW"))
        WTAP = sb("WTAP", [P, CC, TAPS, P])
        WP1, W2Q, W2K, W2V, WP2 = (sb(n, [P, CC, C]) for n in ("WP1", "W2Q", "W2K", "W2V", "WP2"))
        ROWS = sb("ROWS", [1, 2 * C + 1])
        KIDX = sb("KIDX", [P, KPOOL + 1])
        EPS = sb("EPS", [P, 2])
        QBS, KB, VB, PB0, PB1, NEGA = (sb(n, [P, CC]) for n in ("QBS", "KB", "VB", "PB0", "PB1", "NEGA"))

        def mat(name):
            return MAT[:, MATS.index(name), :]

        def col(name, cc):
            return COL[:, cc, COLS.index(name):COLS.index(name) + 1]

        X0, XR = sb("X0", [P, CC, N]), sb("XR", [P, CC, N])
        GA0 = sb("GA0", [P, CC, N])
        PT = sb("PT", [P, 4, N])
        PROB = PT[:, :, :].rearrange("p a (k n) -> p (a k) n", n=HALF)
        QF = PT[:, 0:2, :]
        QH, QL = (PT[:, n, :].bitcast(f16).rearrange("p (c n) -> p c n", c=CC) for n in (2, 3))
        QST = sb("QST", [P, HEADS, N], f16)
        KST = sb("KST", [P, HEADS, NK], f16)
        VT, ONES = sb("VT", [P, 2, HEADS, HD]), sb("ONES", [P, HD])
        XDS, SQD = sb("XDS", [P, CC, NK]), sb("SQD", [P, CC, NK])
        KF = SQD
        KH, KL = sb("KH", [P, CC, NK], f16), sb("KL", [P, CC, NK], f16)
        MEAN0, VAR0 = sb("MEAN0", [P, NK]), sb("VAR0", [P, NK])
        NEGMAX = sb("NEGMAX", [P, HEADS, QT])
        MH, ML = sb("MH", [32, 2, P], f16), sb("ML", [32, 2, P], f16)
        G, U, PS = sb("G", [P, CC, N]), sb("U", [P, CC, N]), sb("PS", [P, 4, N])
        SQX = sb("SQX", [P, QT * (C + 1)])
        SQ = SQX[:, 0:CC * N].rearrange("p (c n) -> p c n", c=CC)
        XNT = SQX[:, :].rearrange("p (t c) -> p t c", t=QT)
        MEAN, VAR = PS[:, 0, :], PS[:, 2, :]
        XM = PS[:, 1::2, :]
        GRAM = PS[:, 0, 0:CC * (C + 1)].rearrange("p (c n) -> p c n", c=CC)
        SROW = PS[0:1, 2, 0:2 * C]
        T1, PAT = (PS[:, 1, n * CC * C:(n + 1) * CC * C].rearrange("p (c n) -> p c n", c=CC) for n in range(2))
        WE = PS[:, 3, 0:CC * C].rearrange("p (c n) -> p c n", c=CC)
        XNP = sb("XNP", [P, CC, H + 2, W + 2])
        GN = {s: [sb(f"{n}_{s}", shape) for n, shape in (("STAT", [P, CC, 2, 6]), ("MSQ", [P, CC, 4]), ("MV", [P, CC, 2]),
                                                        ("GM", [P, CC, 2]), ("GV", [P, CC]), ("GR", [P, CC]), ("GB", [P, CC]))]
              for s in "AB"}
        GAPX, GAP, HM = sb("GAPX", [P, CC]), sb("GAP", [P, CC]), sb("HM", [16, 1])
        GT, GS = sb("GT", [P, CC]), sb("GS", [P, CC])
        AB, AP_, ABD = sb("AB", [P, CC, HD]), sb("AP_", [P, CC, HD]), sb("ABD", [P, CC, P])
        AOK, AEX = sb("AOK", [P, CC, HD]), sb("AEX", [P, CC, HD])
        AMX, ASUM, ANN = sb("AMX", [P, CC]), sb("ASUM", [P, CC]), sb("ANN", [P, CC])
        BE = sb("BE", [P, CC])
        PA_, PB_ = sb("PA_", [P, CC * (H + 2), W + 2]), sb("PB_", [P, CC * (H + 2), W + 2])
        HB, PH = sb("HB", [P, H + 2, W]), sb("PH", [P, H, W // 2])
        PV = PH[:, :, :].rearrange("p h w -> p (h w)").rearrange("p (h w) -> p h w", w=W)
        ACC, YK = sb("ACC", [P, CC, N]), sb("YK", [P, 2, HALF])
        SC, CGE, QS = sb("SC", [P, CC]), sb("CGE", [P, CC, KPOOL + 1]), sb("QS", [P, CC])
        FB, FS, EQ = sb("FB", [P, CC]), sb("FS", [P, CC]), sb("EQ", [P, CC, KPOOL])
        WKP, COEF, C0, C1 = sb("WKP", [P, CC, KPOOL]), sb("COEF", [P, CC, KPOOL]), sb("C0", [P, CC]), sb("C1", [P, CC])
        CW = PS[:, 0:3, 0:768]
        IPX = PS[:, 3, 0:CC * P].rearrange("p (c n) -> p c n", c=CC)
        XPR, DTP = (SQ[0:16, n, 0:CC * P].rearrange("p (c n) -> p c n", c=CC) for n in range(2))

        SLOT = {n: ctx.enter_context(nc.psum_tensor(n, [P, HALF], f32))
                for n in ("aA0", "aA1", "aD0", "aD1", "bA0", "bA1", "bD0", "bD1")}

        pe_a, pe_b = Steps(sem("pe_a_steps"), PE_A), Steps(sem("pe_b_steps"), PE_B)
        act_a, act_b, act_m = Steps(sem("act_a_steps"), ACT_A), Steps(sem("act_b_steps"), ACT_B), Steps(sem("act_m_steps"), ACT_M)
        dve_a, dve_b, dve_m = Steps(sem("dve_a_steps"), DVE_A), Steps(sem("dve_b_steps"), DVE_B), Steps(sem("dve_m_steps"), DVE_M)
        pool_a, pool_b, pool_m = (Steps(sem(n), t) for n, t in
                                  (("pool_a_steps", POOL_A), ("pool_b_steps", POOL_B), ("pool_m_steps", POOL_M)))
        pe_set, act_set = Steps(sem("pe_setup_steps"), PE_SETUP, 0), Steps(sem("act_setup_steps"), ACT_SETUP, 0)
        dve_set, pool_set = Steps(sem("dve_setup_steps"), DVE_SETUP, 0), Steps(sem("pool_setup_steps"), POOL_SETUP, 0)
        mats_loaded = sem("mats_loaded")
        x_loaded, early_loaded, late_loaded = sem("x_loaded"), sem("early_weights_loaded"), sem("late_weights_loaded")
        stacked, maxed, stored = sem("q_k_stacked"), sem("max_rows_stacked"), sem("out_stored")
        EARLY_N, LATE_N = 9, 14
        STACK_DMAS, MAX_DMAS = 24, 4
        NORM = {"A": (pe_a, act_a, dve_a, pool_a, "a", PT[:, 2:4, :], PT[:, 0, :], PT[:, 1, :]),
                "B": (pe_b, act_b, dve_b, pool_b, "b", SQ, MEAN, VAR)}
        BLOCKS = [(m, half) for m in range(CC) for half in range(2)]

        block = ctx.enter_context(nc.Block())

        def take_turn(streams, order, t, active="ABM"):
            going = {s: streams[s](t - STREAMS.index(s)) for s in active if s in streams}
            for s in order:
                if s in going:
                    next(going[s], None)
            for s in going:
                assert next(going[s], "end") == "end", s

        def run(eng, streams, order, before_b=None, setup=None):
            order = unpack(order)
            take_turn({"A": lambda b: streams["A"](b, setup)}, order, 0, "A")
            if before_b:
                before_b()
            take_turn(streams, order, 1, "AB")
            with eng.Fori(2, B) as t:
                take_turn(streams, order, t)
            take_turn(streams, order, B, "BM")
            take_turn(streams, order, B + 1, "M")

        def hs(half):
            return slice(half * HALF, (half + 1) * HALF)

        def interior(t, cc, dy=1, dx=1):
            r = cc * (H + 2) + dy
            return t[:, r:r + H, dx:dx + W]

        @block.sync
        def _(sp):
            x_v = x.rearrange("b (c p) h w -> p (b c) (h w)", p=P)
            out_v = out.rearrange("b (c p) h w -> p (b c) (h w)", p=P)
            sp.sem_inc(stored, 16)
            sp.dma_start(X0[:, :, :], x_v[:, 0:CC, :]).then_inc(x_loaded, 16)
            sp.dma_start(MAT[:, :, :], mats).then_inc(mats_loaded, 16)
            for dst, src in ((COL, cols), (WDS, wds), (WQ, wq), (WK, wk), (WV, wv), (WP0, wp0),
                             (WP1, wp1), (XPR, xpr), (DTP, dtp)):
                sp.dma_start(dst[tuple(slice(None) for _ in dst.shape)], src).then_inc(early_loaded, 16)

            def stack(b):
                for wait, dst, quads, src in ((dve_a.at(b, "qh1"), QST, (0, 2), QH), (pool_a.at(b, "ql1"), QST, (1,), QL),
                                              (dve_a.at(b, "kh"), KST, (0, 1), KH), (pool_a.at(b, "kl"), KST, (2,), KL)):
                    sp.wait_ge(*wait)
                    for quad in quads:
                        for j in range(4):
                            sp.dma_start(dst[32 * quad:32 * quad + 32, j:HEADS:4, :], src[32 * j:32 * j + 32, :, :])\
                              .then_inc(stacked, 16)

            def max_rows(b, g):
                sp.wait_ge(*dve_a.at(b, f"ml{g}"))
                for r, src in ((96, MH), (97, ML)):
                    sp.dma_start(QST[r:r + 1, 4 * g:4 * g + 4, :].rearrange("a h (t q) -> a (h t) q", t=QT),
                                 src[:, g, :]).then_inc(maxed, 16)

            def next_image(b):
                sp.wait_ge(*act_a.at(b, "xr"))
                sp.wait_ge(*dve_a.at(b, "g1_1"))
                sp.dma_start(X0[:, :, :], x_v[:, bass.ds(b * CC + CC, CC), :]).then_inc(x_loaded, 16)

            def store(b):
                sp.wait_ge(*pool_m.at(b, "add6_1_1"))
                sp.dma_start(out_v[:, bass.ds(b * CC, CC), :], ACC[:, :, :]).then_inc(stored, 16)

            def turn(t, active="ABM"):
                if "A" in active:
                    stack(t)
                    max_rows(t, 0)
                    max_rows(t, 1)
                    if not isinstance(t, int) or t + 1 < B:
                        next_image(t)
                if "M" in active:
                    store(t - 2)

            turn(0, "A")
            turn(1, "AB")
            with sp.Fori(2, B - 1) as t:
                turn(t)
            turn(B - 1)
            turn(B, "BM")
            turn(B + 1, "M")
            sp.wait_ge(stored, 16 * (B + 1))

        @block.scalar
        def _(e):
            for dst, src in ((S16, small16), (W1S, w1s), (IPX, ipx), (IPZ, ipz), (XB, xb), (XC, xc), (OPW, opw),
                             (W2Q, w2q), (W2K, w2k), (W2V, w2v), (WP2, wp2), (ROWS, rows), (KIDX, kidx)):
                e.dma_start(dst[tuple(slice(None) for _ in dst.shape)], src).then_inc(late_loaded, 16)
            e.dma_start(CW, cw.partition_broadcast(P)).then_inc(late_loaded, 16)
            for s in (act_a, act_b, act_m):
                e.sem_inc(*s.start())

            def table(n):
                e.add_instruction(mybir.InstLoadActFuncSet(act_func_set_id=n, name=nc.get_next_instruction_name(),
                                                           engine=mybir.EngineType.Activation))

            def group_norm(b, l, act, dve):
                GV, GR = GN["A" if l < 2 else "B"][4:6]
                e.wait_ge(*dve.at(b, f"gn_var{l}"))
                e.activation(GR[:, :], GV[:, :], ACT.Ln, bias=EPS[:, 0:1]).then_inc(*act.step(f"gn_ln{l}"))
                yield
                e.wait_ge(*act.at(b, f"gn_ln{l}"))
                e.activation(GR[:, :], GR[:, :], ACT.Exp, scale=-0.5).then_inc(*act.step(f"gn_rstd{l}"))
                yield

            def rstd(b, l, var, act, dve):
                e.wait_ge(*dve.at(b, f"ln_var{l}"))
                e.activation(var, var, ACT.Ln, bias=EPS[:, 0:1]).then_inc(*act.step(f"ln_ln{l}"))
                yield
                e.wait_ge(*act.at(b, f"ln_ln{l}"))
                e.activation(var, var, ACT.Exp, scale=-0.5).then_inc(*act.step(f"ln_rstd{l}"))
                yield

            def down(b):
                e.wait_ge(*pe_a.at(b, "ds"))
                for cc in range(CC):
                    e.activation(XDS[:, cc, :], SLOT["aA0"][:, cc * NK:(cc + 1) * NK], ACT.Identity,
                                 bias=col("ds_b", cc)).then_inc(*act_a.step(f"xds{cc}"))
                    yield
                e.wait_ge(*act_a.at(b, "xds1"))
                e.activation(SQD[:, :, :], XDS[:, :, :], ACT.Square).then_inc(*act_a.step("sq_ds"))
                yield

            def query(b):
                for m, half in BLOCKS:
                    e.wait_ge(*pe_a.at(b, f"q{m}_{half}"))
                    e.activation(QF[:, m, hs(half)], SLOT[f"aA{half}"][:, :], ACT.Identity, bias=QBS[:, m:m + 1],
                                 scale=SCALE).then_inc(*act_a.step(f"qf{m}_{half}"))
                    yield

            def keys(b):
                e.wait_ge(*pe_a.at(b, "k"))
                for cc in range(CC):
                    e.activation(KF[:, cc, :], SLOT["aA0"][:, cc * NK:(cc + 1) * NK], ACT.Identity,
                                 bias=KB[:, cc:cc + 1]).then_inc(*act_a.step(f"kf{cc}"))
                    yield

            def probabilities(b, g, kt):
                if g:
                    e.wait_ge(*pe_a.at(b, f"pv{g - 1}_{kt}"))
                for j in range(4):
                    e.wait_ge(*pe_a.at(b, f"st{g}_{kt}_{j}"))
                    e.activation(PROB[:, 4 * kt + j, :], SLOT[f"aA{j % 2}"][:, :], ACT.Exp)\
                     .then_inc(*act_a.step(f"p{g}_{kt}_{j}"))
                    yield

            def inverse_sums(b, g):
                z = GA0[:, g // 2, hs(g % 2)]
                e.wait_ge(*pe_a.at(b, f"pv{g}_1"))
                e.activation(z, SLOT["aD0"][:, :], ACT.Ln).then_inc(*act_a.step(f"lz{g}"))
                yield
                e.wait_ge(*act_a.at(b, f"lz{g}"))
                e.activation(z, z, ACT.Exp, scale=-1.0).then_inc(*act_a.step(f"rz{g}"))
                yield

            def sums(b, l, src, ready):
                pe, act, dve, _, banks, squares, mean, var = NORM["A" if l == 1 else "B"]
                for cc in range(CC):
                    e.wait_ge(*dve.at(b, ready[cc]))
                    e.activation(squares[:, cc, :], src[:, cc, :], ACT.Square).then_inc(*act.step(f"sq{l}_{cc}"))
                    yield
                for half in range(2):
                    e.wait_ge(*pe.at(b, f"sums{l}_{half}"))
                    for lo in (0, 64):
                        e.activation(mean[lo:lo + 64, hs(half)], SLOT[f"{banks}A{half}"][0:64, :], ACT.Copy)\
                         .then_inc(*act.step(f"ln_mean{l}_{half}_{lo}"))
                        yield
                    e.activation(var[0:64, hs(half)], SLOT[f"{banks}A{half}"][0:64, :], ACT.Square).then_inc(*act.step(f"ln_m2{l}_{half}"))
                    yield

            def spread_rstd(b, l):
                _, act, dve, _, _, _, _, var = NORM["A" if l == 1 else "B"]
                e.wait_ge(*dve.at(b, f"ln_var{l}"))
                e.activation(var[0:64, :], var[0:64, :], ACT.Ln, bias=EPS[0:64, 0:1]).then_inc(*act.step(f"ln_ln{l}"))
                yield
                e.wait_ge(*act.at(b, f"ln_ln{l}"))
                e.activation(var[64:128, :], var[0:64, :], ACT.Exp, scale=-0.5).then_inc(*act.step(f"ln_rstd_high{l}"))
                yield
                e.activation(var[0:64, :], var[0:64, :], ACT.Exp, scale=-0.5).then_inc(*act.step(f"ln_rstd{l}"))
                yield

            def scan_order(b):
                yield from spread_rstd(b, 1)
                e.wait_ge(*dve_b.at(b - 1, "xm3_1"))
                for g in range(GROUPS):
                    cc, lo = g // 2, 64 * (g % 2)
                    e.wait_ge(*dve_a.at(b, f"n1_{cc}"))
                    dst = XNP[lo:lo + 64, cc, 1:1 + H, 1:1 + W]
                    if g % 2:
                        dst = dst.rearrange("p h w -> p w h")
                    if g >= 2:
                        dst = dst[:, ::-1, ::-1]
                    e.activation(dst, GA0[lo:lo + 64, cc, :].rearrange("p (h w) -> p h w", h=H), ACT.Identity,
                                 bias=COL[lo:lo + 64, cc, COLS.index("ln_b"):COLS.index("ln_b") + 1],
                                 scale=COL[lo:lo + 64, cc, COLS.index("ln_g"):COLS.index("ln_g") + 1],
                                 accum_out=GAPX[lo:lo + 64, cc:cc + 1]).then_inc(*act_a.step(f"xn{g}"))
                    yield

            def copy_image(b):
                e.wait_ge(*dve_b.at(b - 1, "x3_1_1"))
                for cc in range(CC):
                    e.activation(XR[:, cc, :], X0[:, cc, :], ACT.Copy).then_inc(*act_a.step("xr" if cc else "xr0"))
                    yield

            def convolved(b, cc):
                e.wait_ge(*pe_b.at(b - 1, "yc1_1"))
                for half in range(2):
                    e.wait_ge(*pe_a.at(b, f"xd{cc}_{half}"))
                    e.activation(U[:, cc, hs(half)], SLOT[f"aA{half}"][:, :], ACT.Identity, bias=col("conv_b", cc))\
                     .then_inc(*act_a.step(f"xd{cc}_{half}"))
                    yield

            def gate_z(b):
                for cc, half in BLOCKS:
                    e.wait_ge(*pe_b.at(b, f"z{cc}_{half}"))
                    e.activation(G[:, cc, hs(half)], SLOT[f"bA{half}"][:, :], ACT.Copy).then_inc(*act_b.step(f"z{cc}_{half}"))
                    yield

            def silu(b):
                table(SILU_TABLE)
                e.wait_ge(*act_b.at(b, "z1_1"))
                for cc in range(CC):
                    e.activation(U[:, cc, :], U[:, cc, :], ACT.Silu).then_inc(*act_b.step(f"u{cc}"))
                e.activation(G[:, :, :], G[:, :, :], ACT.Silu).then_inc(*act_b.step("zs"))
                table(EXP_LN_TABLE)
                yield

            def gate(b):
                e.wait_ge(*dve_b.at(b, "gate_in"))
                e.activation(GT[:, :], GT[:, :], ACT.Exp, scale=-1.0).then_inc(*act_b.step("gate_exp"))
                yield

            def delta(b):
                for cc, half in BLOCKS:
                    e.wait_ge(*pe_b.at(b, f"v{cc}_{half}"))
                    e.activation(PS[:, 2 * cc, hs(half)], SLOT[f"bA{half}"][:, :], ACT.Identity, bias=col("dt_b", cc))\
                     .then_inc(*act_b.step(f"v{cc}_{half}"))
                    yield
                for cc in range(CC):
                    e.wait_ge(*dve_b.at(b, f"vmin{cc}"))
                    e.activation(PS[:, 2 * cc + 1, :], PS[:, 2 * cc + 1, :], ACT.Exp).then_inc(*act_b.step(f"ev{cc}"))
                    yield
                    e.wait_ge(*act_b.at(b, f"ev{cc}"))
                    e.activation(PS[:, 2 * cc + 1, :], PS[:, 2 * cc + 1, :], ACT.Ln, bias=EPS[:, 1:2])\
                     .then_inc(*act_b.step(f"lv{cc}"))
                    yield
                for cc in range(CC):
                    e.wait_ge(*dve_b.at(b, f"delta{cc}"))
                    e.activation(PS[:, 2 * cc + 1, :], PS[:, 2 * cc, :], ACT.Exp, scale=NEGA[:, cc:cc + 1])\
                     .then_inc(*act_b.step(f"dA{cc}"))
                    yield

            def centred(b):
                for cc, half in BLOCKS:
                    e.wait_ge(*pe_b.at(b, f"yc{cc}_{half}"))
                    e.activation(PS[:, 2 * cc + 1, hs(half)], SLOT[f"bA{half}"][:, :], ACT.Copy).then_inc(*act_b.step(f"yc{cc}_{half}"))
                    yield
                    e.activation(SQ[:, cc, hs(half)], SLOT[f"bA{half}"][:, :], ACT.Square).then_inc(*act_b.step(f"ysq{cc}_{half}"))
                    yield

            def y_rstd(b):
                for cc in range(CC):
                    for half in range(2):
                        e.wait_ge(*pe_b.at(b, f"yv{cc}_{half}"))
                        e.activation(PS[:, 2 * cc, hs(half)], SLOT[f"bA{half}"][:, :], ACT.Ln, bias=EPS[:, 0:1])\
                         .then_inc(*act_b.step(f"yln{cc}_{half}"))
                        yield
                    e.wait_ge(*act_b.at(b, f"yln{cc}_1"))
                    e.activation(PS[:, 2 * cc, :], PS[:, 2 * cc, :], ACT.Exp, scale=-0.5).then_inc(*act_b.step(f"yrs{cc}"))
                    yield

            def y_affine(b):
                for cc in range(CC):
                    e.wait_ge(*dve_b.at(b, f"yn{cc}"))
                    e.activation(PS[:, 2 * cc + 1, :], PS[:, 2 * cc + 1, :], ACT.Identity, bias=col("ob", cc),
                                 scale=col("og", cc)).then_inc(*act_b.step(f"ya{cc}"))
                    yield

            def pixel_rows(b):
                for t in range(4):
                    e.wait_ge(*pe_b.at(b, f"xnT{t}"))
                    e.activation(XNT[:, 2 * t:2 * t + 2, 0:C], SLOT[f"bA{t % 2}"][:, :].rearrange("p (t c) -> p t c", t=2),
                                 ACT.Copy).then_inc(*act_b.step(f"xnt{t}"))
                    yield

            def evacuate(b, slot, dst, waited, step):
                e.wait_ge(*pe_b.at(b, waited))
                e.activation(dst[:, :, :], SLOT[slot][:, :].rearrange("p (c n) -> p c n", c=CC), ACT.Copy)\
                 .then_inc(*act_b.step(step))
                yield

            def channel_softmax(b):
                e.wait_ge(*dve_b.at(b, "amax"))
                for cc in range(CC):
                    e.activation(AEX[:, cc, :], AB[:, cc, :], ACT.Exp, bias=AMX[:, cc:cc + 1],
                                 accum_out=ASUM[:, cc:cc + 1]).then_inc(*act_b.step(f"aexp{cc}"))
                    yield

            def maxpool(b, k):
                if k == 1:
                    e.wait_ge(stored, 16 * b + 16)
                    e.wait_ge(*dve_b.at(b, "coef"))
                    for cc in range(CC):
                        e.activation(ACC[:, cc, :].rearrange("p (h w) -> p h w", h=H), interior(PA_, cc), ACT.Identity,
                                     bias=C1[:, cc:cc + 1], scale=C0[:, cc:cc + 1]).then_inc(*act_m.step(f"a{cc}"))
                        yield
                src = PA_ if k % 2 == 0 else PB_
                for cc, half in BLOCKS:
                    e.wait_ge(*dve_m.at(b, f"v{k}_{cc}"))
                    if cc == 1:
                        e.wait_ge(*pool_m.at(b, f"add{k}_0_{half}"))
                    elif k > 1:
                        e.wait_ge(*pool_m.at(b, f"add{k - 1}_1_{half}"))
                    else:
                        e.wait_ge(*pool_m.at(b - 1, f"add6_1_{half}"))
                    lo = cc * (H + 2) + 1 + 16 * half
                    e.activation(YK[:, half, :].rearrange("p (h w) -> p h w", w=W), src[:, lo:lo + 16, 1:1 + W], ACT.Copy,
                                 scale=COEF[:, cc, k:k + 1]).then_inc(*act_m.step(f"y{k}_{cc}_{half}"))
                    yield

            def stream_a(b, setup=None):
                yield from group_norm(b, 0, act_a, dve_a)
                if setup:
                    setup()
                yield from down(b)
                yield from query(b)
                yield from rstd(b, 0, VAR0[:, :], act_a, dve_a)
                yield from keys(b)
                for g in range(4):
                    yield from probabilities(b, g, 0)
                    if g:
                        yield from inverse_sums(b, g - 1)
                    yield from probabilities(b, g, 1)
                yield from inverse_sums(b, 3)
                yield from group_norm(b, 1, act_a, dve_a)
                yield from sums(b, 1, GA0, ("g1_0", "g1_1"))
                yield from scan_order(b)
                yield from copy_image(b)
                yield from convolved(b, 0)
                yield from convolved(b, 1)

            def stream_b(b):
                yield from gate_z(b)
                yield from gate(b)
                yield from silu(b)
                yield from delta(b)
                yield from centred(b)
                yield from y_rstd(b)
                yield from y_affine(b)
                yield from sums(b, 2, XM, ("xm1_1", "xm3_1"))
                yield from spread_rstd(b, 2)
                yield from group_norm(b, 2, act_b, dve_b)
                yield from sums(b, 3, G, ("g2_0", "g2_1"))
                yield from spread_rstd(b, 3)
                yield from pixel_rows(b)
                yield from evacuate(b, "bA0", T1, "T1", "t1")
                yield from channel_softmax(b)
                yield from evacuate(b, "bA1", PAT, "PAT", "pat")
                yield from evacuate(b, "bA0", WE, "WE", "we")
                yield from group_norm(b, 3, act_b, dve_b)

            def stream_m(b):
                for k in range(1, KPOOL):
                    yield from maxpool(b, k)

            table(EXP_LN_TABLE)
            e.wait_ge(*dve_set.at(0, "eps0"))

            def setup():
                e.wait_ge(early_loaded, 16 * EARLY_N)
                e.activation(NEGA[:, :], COL[:, :, COLS.index("A_log")], ACT.Exp).then_inc(*act_set.step("expA"))
                e.wait_ge(*act_set.at(0, "expA"))
                e.activation(NEGA[:, :], NEGA[:, :], ACT.Copy, scale=-1.0).then_inc(*act_set.step("negA"))
                e.wait_ge(*act_set.at(0, "negA"))
                e.wait_ge(*dve_set.at(0, "eps1"))
                e.wait_ge(*dve_set.at(0, "kb"))

            run(e, {"A": stream_a, "B": stream_b, "M": stream_m}, ACT_ORDER, setup=setup)

        @block.gpsimd
        def _(e):
            for s in (pool_a, pool_b, pool_m):
                e.sem_inc(*s.start())
            e.memset(KST[96:98, :, :], 1.0).then_inc(*pool_set.step("kst1"))
            e.wait_ge(*pool_set.at(0, "kst1"))
            e.memset(ONES[:, :], 1.0).then_inc(*pool_set.step("ones"))
            e.memset(ABD[:, :, :], 0.0).then_inc(*pool_set.step("abd"))
            e.memset(XNP[:, :, :, :], 0.0).then_inc(*pool_set.step("xnp"))
            for t, n in ((PA_, "pa"), (PB_, "pb"), (HB, "hb")):
                e.memset(t[:, :, :], LOWEST).then_inc(*pool_set.step(n))

            e.wait_ge(late_loaded, 16 * LATE_N)
            taps = CW.rearrange("p a (t d) -> p a t d", d=P)
            for cc in range(CC):
                for a in range(3):
                    lo, hi = max(6 * a, 9 * cc), min(6 * a + 6, 9 * cc + 9)
                    if lo < hi:
                        e.tensor_tensor(WTAP[:, cc, lo - 9 * cc:hi - 9 * cc, :],
                                        IPX[:, cc, :].unsqueeze(1).broadcast_to([P, hi - lo, P]),
                                        taps[:, a, lo - 6 * a:hi - 6 * a, :], ALU.mult).then_inc(*pool_set.step(f"wtap{cc}_{a}"))

            def split(b):
                for cc in range(CC):
                    e.wait_ge(*dve_a.at(b, f"qh{cc}"))
                    e.tensor_tensor(QL[:, cc, :], QF[:, cc, :], QH[:, cc, :], ALU.subtract)\
                     .then_inc(*pool_a.step(f"ql{cc}"))
                    yield
                e.wait_ge(*dve_a.at(b, "kh"))
                e.tensor_tensor(KL[:, :, :], KF[:, :, :], KH[:, :, :], ALU.subtract).then_inc(*pool_a.step("kl"))
                yield

            def centre(b, l, t):
                pe, act, _, pool, _, _, mean, _ = NORM["A" if l == 1 else "B"]
                e.wait_ge(*act.at(b, f"sq{l}_1"))
                e.wait_ge(*act.at(b, f"ln_mean{l}_1_64"))
                for cc in range(CC):
                    e.tensor_tensor(t[:, cc, :], t[:, cc, :], mean, ALU.subtract).then_inc(*pool.step(f"c{l}_{cc}"))
                    yield

            def maxpool(b, k):
                for cc, half in BLOCKS:
                    e.wait_ge(*act_m.at(b, f"y{k}_{cc}_{half}"))
                    if k > 1:
                        e.wait_ge(*pool_m.at(b, f"add{k - 1}_{cc}_{half}"))
                    e.tensor_tensor(ACC[:, cc, hs(half)], ACC[:, cc, hs(half)], YK[:, half, :], ALU.add)\
                     .then_inc(*pool_m.step(f"add{k}_{cc}_{half}"))
                    yield

            def stream_a(b, setup=None):
                yield from split(b)
                yield from centre(b, 1, GA0)

            def stream_b(b):
                yield from centre(b, 2, XM)
                yield from centre(b, 3, G)

            def stream_m(b):
                for k in range(1, KPOOL):
                    yield from maxpool(b, k)

            run(e, {"A": stream_a, "B": stream_b, "M": stream_m}, POOL_ORDER)

        @block.vector
        def _(e):
            for s in (dve_a, dve_b, dve_m):
                e.sem_inc(*s.start())
            e.memset(EPS[:, 0:1], 1e-5).then_inc(*dve_set.step("eps0"))
            e.memset(EPS[:, 1:2], 1.0).then_inc(*dve_set.step("eps1"))

            def setup():
                e.wait_ge(early_loaded, 16 * EARLY_N)
                e.tensor_scalar(QBS[:, :], COL[:, :, COLS.index("q_b")], SCALE, None, ALU.mult).then_inc(*dve_set.step("qbs"))
                e.wait_ge(*pe_set.at(0, "fold"))
                FOLD = SLOT["bD0"]
                e.tensor_tensor(KB[:, :], FOLD[:, 0:2], COL[:, :, COLS.index("k_b")], ALU.add).then_inc(*dve_set.step("kb"))
                e.tensor_tensor(VB[:, :], FOLD[:, 2:4], COL[:, :, COLS.index("v_b")], ALU.add).then_inc(*dve_set.step("vb"))
                e.tensor_tensor(PB1[:, :], FOLD[:, 4:6], COL[:, :, COLS.index("pb1")], ALU.add).then_inc(*dve_set.step("pb1"))
                for cc in range(CC):
                    for t, w, n in ((WK, "kv_ln_w", "wk"), (WV, "kv_ln_w", "wv"), (WP1, "ln_g", "wp1")):
                        e.tensor_scalar(t[:, cc, :], t[:, cc, :], col(w, cc), None, ALU.mult)\
                         .then_inc(*dve_set.step(f"{n}{cc}"))
                e.wait_ge(*pe_set.at(0, "wd"))
                e.tensor_copy(WD[:, :, :], SLOT["bD1"][:, 0:CC * P].rearrange("p (c n) -> p c n", c=CC)).then_inc(*dve_set.step("wd"))
                e.wait_ge(*pe_set.at(0, "fold0"))
                e.tensor_tensor(PB0[:, :], FOLD[:, 0:2], COL[:, :, COLS.index("pb0")], ALU.add).then_inc(*dve_set.step("pb0"))

            def group_norm(b, l, src, dst, out_tile, dve, pe, act, slot):
                STAT, MSQ, MV, GM, GV, GR, GB = GN["A" if l < 2 else "B"]
                for cc in range(CC):
                    for half in range(2):
                        e.bn_stats(STAT[:, cc, half, :], src(cc, half)).then_inc(*dve.step(f"gn_st{l}_{cc}{half}"))
                        yield
                means, m2s = (STAT[:, :, :, :].rearrange("p c a (s t) -> p c (a s) t", t=3)[:, :, :, n] for n in (1, 2))
                e.wait_ge(*dve.at(b, f"gn_st{l}_11"))
                e.tensor_tensor(MSQ[:, :, :], means, means, ALU.mult).then_inc(*dve.step(f"gn_m2{l}"))
                yield
                e.tensor_reduce(MV[:, :, 0], means, AX.X, ALU.add).then_inc(*dve.step(f"gn_m{l}"))
                yield
                e.wait_ge(*dve.at(b, f"gn_m2{l}"))
                e.scalar_tensor_tensor(out=MSQ[:, :, :], in0=m2s, scalar=4.0 / N, in1=MSQ[:, :, :], op0=ALU.mult,
                                       op1=ALU.add).then_inc(*dve.step(f"gn_sq{l}"))
                yield
                e.wait_ge(*dve.at(b, f"gn_sq{l}"))
                e.tensor_reduce(MV[:, :, 1], MSQ[:, :, :], AX.X, ALU.add).then_inc(*dve.step(f"gn_ex2{l}"))
                yield
                if l == 3:
                    e.tensor_scalar(GAP[:, :], MV[:, :, 0], 0.25, None, ALU.mult).then_inc(*dve.step("gap3"))
                    yield
                e.wait_ge(*pe.at(b, f"gn{l}"))
                e.tensor_copy(GM[:, :, :], SLOT[slot][:, 0:4].rearrange("p (c s) -> p c s", c=CC)).then_inc(*dve.step(f"gn_gm{l}"))
                yield
                e.wait_ge(*dve.at(b, f"gn_gm{l}"))
                e.tensor_tensor(GV[:, :], GM[:, :, 0], GM[:, :, 0], ALU.mult).then_inc(*dve.step(f"gn_gm2{l}"))
                yield
                e.wait_ge(*dve.at(b, f"gn_gm2{l}"))
                e.tensor_tensor(GV[:, :], GM[:, :, 1], GV[:, :], ALU.subtract).then_inc(*dve.step(f"gn_var{l}"))
                yield
                e.wait_ge(*act.at(b, f"gn_rstd{l}"))
                e.scalar_tensor_tensor(out=GB[:, :], in0=GM[:, :, 0], scalar=-1.0, in1=GR[:, :], op0=ALU.mult,
                                       op1=ALU.mult).then_inc(*dve.step(f"gn_b{l}"))
                yield
                e.wait_ge(*dve.at(b, f"gn_b{l}"))
                if dst is not None:
                    for cc in range(CC):
                        e.tensor_scalar(out_tile[:, cc, :], dst(cc), GR[:, cc:cc + 1], GB[:, cc:cc + 1], ALU.mult, ALU.add)\
                         .then_inc(*dve.step(f"g{l}_{cc}"))
                        yield

            def attention_norm(b):
                e.wait_ge(x_loaded, 16 * b + 16)
                yield from group_norm(b, 0, lambda cc, h: X0[:, cc, hs(h)], lambda cc: X0[:, cc, :], GA0, dve_a, pe_a, act_a, "aD0")

            def scan_norm(b):
                e.wait_ge(*dve_a.at(b, "x1_1_1"))
                yield from group_norm(b, 1, lambda cc, h: X0[:, cc, hs(h)], lambda cc: X0[:, cc, :], GA0, dve_a, pe_a, act_a, "aD0")

            def channel_norm(b):
                e.wait_ge(*dve_b.at(b, "x2_1_1"))
                yield from group_norm(b, 2, lambda cc, h: XR[:, cc, hs(h)], lambda cc: XR[:, cc, :], G, dve_b, pe_b, act_b, "bD0")

            def kv_norm(b):
                s = SLOT["aD0"]
                e.wait_ge(*pe_a.at(b, "msq0"))
                e.tensor_copy(MEAN0[:, :], s[:, 0:NK]).then_inc(*dve_a.step("ln_mean0"))
                yield
                e.wait_ge(*dve_a.at(b, "ln_mean0"))
                e.scalar_tensor_tensor(out=VAR0[:, :], in0=MEAN0[:, :], scalar=-1.0, in1=MEAN0[:, :], op0=ALU.mult,
                                       op1=ALU.mult).then_inc(*dve_a.step("ln_m20"))
                yield
                e.wait_ge(*dve_a.at(b, "ln_m20"))
                e.tensor_tensor(VAR0[:, :], VAR0[:, :], s[:, NK:2 * NK], ALU.add).then_inc(*dve_a.step("ln_var0"))
                yield
                for cc in range(CC):
                    e.tensor_tensor(XDS[:, cc, :], XDS[:, cc, :], MEAN0[:, :], ALU.subtract).then_inc(*dve_a.step(f"c0_{cc}"))
                    yield
                e.wait_ge(*act_a.at(b, "ln_rstd0"))
                for cc in range(CC):
                    e.wait_ge(*dve_a.at(b, f"c0_{cc}"))
                    e.tensor_tensor(XDS[:, cc, :], XDS[:, cc, :], VAR0[:, :], ALU.mult).then_inc(*dve_a.step(f"n0_{cc}"))
                    yield

            def variance(b, l):
                pe, act, dve, _, banks, _, _, var = NORM["A" if l == 1 else "B"]
                for half in range(2):
                    e.wait_ge(*pe.at(b, f"sums{l}_{half}"))
                    e.wait_ge(*act.at(b, f"ln_m2{l}_{half}"))
                    e.tensor_tensor(var[0:64, hs(half)], SLOT[f"{banks}A{half}"][64:128, :], var[0:64, hs(half)], ALU.subtract)\
                     .then_inc(*dve.step(f"ln_var{l}" if half else f"ln_var{l}_0"))
                    yield

            def normalise(b, l, t):
                _, act, dve, pool, _, _, _, var = NORM["A" if l == 1 else "B"]
                e.wait_ge(*act.at(b, f"ln_rstd{l}"))
                for cc in range(CC):
                    e.wait_ge(*pool.at(b, f"c{l}_{cc}"))
                    e.tensor_tensor(t[:, cc, :], t[:, cc, :], var, ALU.mult).then_inc(*dve.step(f"n{l}_{cc}"))
                    yield

            def split_queries(b):
                for cc in range(CC):
                    e.wait_ge(*act_a.at(b, f"qf{cc}_1"))
                    e.tensor_copy(QH[:, cc, :], QF[:, cc, :]).then_inc(*dve_a.step(f"qh{cc}"))
                    yield

            def split_keys(b):
                e.wait_ge(*act_a.at(b, "kf1"))
                e.tensor_copy(KH[:, :, :], KF[:, :, :]).then_inc(*dve_a.step("kh"))
                yield
                e.wait_ge(*pe_a.at(b, "vT"))
                e.tensor_copy(VT[:, :, :, :],
                              SLOT["aD1"][:, 0:2 * C].rearrange("p (k h d) -> p k h d", k=2, h=HEADS)).then_inc(*dve_a.step("vt"))
                yield

            def maxima(b, h):
                for j in range(4):
                    e.wait_ge(*pe_a.at(b, f"s{h}_{j}"))
                    e.tensor_reduce(NEGMAX[:, h, 2 * j:2 * j + 2], SLOT[f"aD{j % 2}"][:, :].rearrange("p (t k) -> p t k", t=2),
                                    AX.X, ALU.max, negate=True).then_inc(*dve_a.step(f"mx{h}_{j}"))
                    yield

            def max_rows(b, g):
                e.wait_ge(*pe_a.at(b, f"mT{g}"))
                e.tensor_copy(MH[:, g, :], SLOT["aD0"][0:32, 0:P]).then_inc(*dve_a.step(f"mh{g}"))
                yield
                e.wait_ge(*dve_a.at(b, f"mh{g}"))
                e.tensor_tensor(ML[:, g, :], SLOT["aD0"][0:32, 0:P], MH[:, g, :], ALU.subtract).then_inc(*dve_a.step(f"ml{g}"))
                yield

            def weighted(b, g):
                cc, half = g // 2, g % 2
                e.wait_ge(*pe_a.at(b, f"pv{g}_1"))
                e.wait_ge(*act_a.at(b, f"rz{g}"))
                e.tensor_tensor(GA0[:, cc, hs(half)], GA0[:, cc, hs(half)], SLOT["aD1"][:, :], ALU.mult)\
                 .then_inc(*dve_a.step(f"o{g}"))
                yield

            def add_to_image(b, label, dve, pe, s, offset, dst):
                for m, half in BLOCKS:
                    e.wait_ge(*pe.at(b, f"{s}_{m}_{half}"))
                    slot = SLOT[("aD" if pe is pe_a else "bD") + str(half)]
                    e.scalar_tensor_tensor(out=dst[:, m, hs(half)], in0=slot[:, :], scalar=offset[:, m:m + 1],
                                           in1=dst[:, m, hs(half)], op0=ALU.add, op1=ALU.add)\
                     .then_inc(*dve.step(f"{label}_{m}_{half}"))
                    yield

            def gate(b):
                e.wait_ge(*act_a.at(b, "xn3"))
                e.tensor_scalar(GAPX[:, :], GAPX[:, :], 1.0 / N, None, ALU.mult).then_inc(*dve_b.step("gap1"))
                yield
                e.wait_ge(*pe_b.at(b, "fc1"))
                e.tensor_scalar(HM[:, :], SLOT["bD0"][0:16, 0:1], S16[:, 2 * C:2 * C + 1], 0.0, ALU.add, ALU.max)\
                 .then_inc(*dve_b.step("hm1"))
                yield
                e.wait_ge(*pe_b.at(b, "fc2"))
                e.tensor_tensor(GT[:, :], SLOT["bD1"][:, 0:2], COL[:, :, COLS.index("fc2_b")], ALU.add).then_inc(*dve_b.step("gate_in"))
                yield

            def delta(b):
                e.wait_ge(*act_b.at(b, "gate_exp"))
                e.tensor_scalar(GT[:, :], GT[:, :], 1.0, None, ALU.add).then_inc(*dve_b.step("gate_1p"))
                yield
                for cc in range(CC):
                    e.wait_ge(*act_b.at(b, f"v{cc}_1"))
                    e.tensor_scalar(PS[:, 2 * cc + 1, :], PS[:, 2 * cc, :], SOFTPLUS_LINEAR, None, ALU.min)\
                     .then_inc(*dve_b.step(f"vmin{cc}"))
                    yield
                e.wait_ge(*dve_b.at(b, "gate_1p"))
                e.reciprocal(GS[:, :], GT[:, :]).then_inc(*dve_b.step("gate"))
                yield
                e.wait_ge(*dve_b.at(b, "gate"))
                e.tensor_tensor(GS[:, :], GS[:, :], COL[:, :, COLS.index("skip")], ALU.mult).then_inc(*dve_b.step("gs"))
                yield
                for cc in range(CC):
                    e.wait_ge(*act_b.at(b, f"lv{cc}"))
                    e.tensor_tensor(PS[:, 2 * cc, :], PS[:, 2 * cc, :], PS[:, 2 * cc + 1, :], ALU.max)\
                     .then_inc(*dve_b.step(f"delta{cc}"))
                    yield
                    e.wait_ge(*dve_b.at(b, f"delta{cc}"))
                    e.tensor_tensor(SQ[:, cc, :], PS[:, 2 * cc, :], U[:, cc, :], ALU.mult).then_inc(*dve_b.step(f"du{cc}"))
                    yield

            def scan(b, cc):
                e.wait_ge(*dve_b.at(b, f"du{cc}"))
                for half in range(2):
                    e.wait_ge(*pe_b.at(b, f"B{cc}_{half}"))
                    e.tensor_tensor(SQ[:, cc, hs(half)], SQ[:, cc, hs(half)], SLOT[f"bD{half}"][:, :], ALU.mult)\
                     .then_inc(*dve_b.step(f"dbu{cc}_{half}"))
                    yield
                e.wait_ge(*dve_b.at(b, f"dbu{cc}_1"))
                e.wait_ge(*act_b.at(b, f"dA{cc}"))
                e.tensor_tensor_scan(PS[:, 2 * cc, :], PS[:, 2 * cc + 1, :], SQ[:, cc, :], 0.0, ALU.mult, ALU.add)\
                 .then_inc(*dve_b.step(f"scan{cc}"))
                yield
                e.wait_ge(*dve_b.at(b, f"scan{cc}"))
                for half in range(2):
                    e.wait_ge(*pe_b.at(b, f"C{cc}_{half}"))
                    e.tensor_tensor(PS[:, 2 * cc, hs(half)], PS[:, 2 * cc, hs(half)], SLOT[f"bD{half}"][:, :], ALU.mult)\
                     .then_inc(*dve_b.step(f"hc{cc}_{half}"))
                    yield
                e.wait_ge(*dve_b.at(b, f"hc{cc}_1"))
                e.scalar_tensor_tensor(out=U[:, cc, :], in0=U[:, cc, :], scalar=col("Ds", cc), in1=PS[:, 2 * cc, :],
                                       op0=ALU.mult, op1=ALU.add).then_inc(*dve_b.step(f"y{cc}"))
                yield

            def gated(b):
                for cc in range(CC):
                    e.wait_ge(*act_b.at(b, f"yrs{cc}"))
                    e.tensor_tensor(PS[:, 2 * cc + 1, :], PS[:, 2 * cc + 1, :], PS[:, 2 * cc, :], ALU.mult)\
                     .then_inc(*dve_b.step(f"yn{cc}"))
                    yield
                for cc in range(CC):
                    e.wait_ge(*act_b.at(b, f"ya{cc}"))
                    e.tensor_tensor(G[:, cc, :], PS[:, 2 * cc + 1, :], G[:, cc, :], ALU.mult).then_inc(*dve_b.step(f"yz{cc}"))
                    yield
                for cc in range(CC):
                    for half in range(2):
                        e.wait_ge(*pe_b.at(b, f"op{cc}_{half}"))
                        for g in (2 * cc, 2 * cc + 1):
                            lo, rows = 64 * (g % 2), slice(16 * half, 16 * half + 16)
                            dst = XM[lo:lo + 64, cc, :].rearrange("p (h w) -> p h w", h=H)
                            if g % 2:
                                dst = dst.rearrange("p h w -> p w h")
                            if g >= 2:
                                dst = dst[:, ::-1, ::-1]
                            e.scalar_tensor_tensor(out=dst[:, rows, :],
                                                   in0=SLOT[f"bD{half}"][lo:lo + 64, :].rearrange("p (h w) -> p h w", w=W),
                                                   scalar=GS[lo:lo + 64, cc:cc + 1],
                                                   in1=XNP[lo:lo + 64, cc, 1 + 16 * half:17 + 16 * half, 1:1 + W],
                                                   op0=ALU.mult, op1=ALU.mult).then_inc(*dve_b.step(f"xm{g}_{half}"))
                            yield

            def ones_column(b):
                e.memset(XNT[:, :, C:C + 1], 1.0).then_inc(*dve_b.step("xnt_ones"))
                yield

            def gram(b):
                for m in range(CC):
                    e.wait_ge(*pe_b.at(b, f"gram{m}"))
                    e.tensor_copy(GRAM[:, m, :], SLOT[f"bD{m}"][:, 0:C + 1]).then_inc(*dve_b.step(f"gram{m}"))
                    yield

            def channel_softmax(b):
                e.wait_ge(*pe_b.at(b, "rows"))
                e.tensor_copy(SROW, SLOT["bD0"][0:1, 0:2 * C]).then_inc(*dve_b.step("srow"))
                yield
                e.wait_ge(*pe_b.at(b, "A"))
                S = SLOT["bD1"][:, 0:CC * P].rearrange("p (c j) -> p c j", c=CC)
                for j in range(4):
                    blk = slice(HD * j, HD * j + HD)
                    e.tensor_scalar(AB[blk, :, :], S[blk, :, blk], SCALE, 50.0, ALU.mult, ALU.min).then_inc(*dve_b.step(f"ab{j}"))
                    yield
                    e.tensor_copy(AOK[blk, :, :], S[blk, :, blk]).then_inc(*dve_b.step(f"aok{j}"))
                    yield
                e.wait_ge(*dve_b.at(b, "aok3"))
                e.tensor_scalar(AB[:, :, :], AB[:, :, :], -50.0, None, ALU.max).then_inc(*dve_b.step("aclip"))
                yield
                e.tensor_tensor(AOK[:, :, :], AOK[:, :, :], AOK[:, :, :], ALU.is_equal).then_inc(*dve_b.step("anan"))
                yield
                e.wait_ge(*dve_b.at(b, "anan"))
                e.tensor_reduce(AMX[:, :], AB[:, :, :], AX.X, ALU.max, negate=True).then_inc(*dve_b.step("amax"))
                yield
                e.tensor_reduce(ANN[:, :], AOK[:, :, :], AX.X, ALU.min).then_inc(*dve_b.step("arow"))
                yield

            def attended(b):
                e.wait_ge(*act_b.at(b, "aexp1"))
                e.reciprocal(ASUM[:, :], ASUM[:, :]).then_inc(*dve_b.step("arec"))
                yield
                e.wait_ge(*dve_b.at(b, "arec"))
                e.tensor_tensor(ASUM[:, :], ASUM[:, :], ANN[:, :], ALU.mult).then_inc(*dve_b.step("arok"))
                yield
                e.tensor_scalar(ANN[:, :], ANN[:, :], -1.0 / HD, 1.0 / HD, ALU.mult, ALU.add).then_inc(*dve_b.step("afill"))
                yield
                e.wait_ge(*dve_b.at(b, "afill"))
                for cc in range(CC):
                    e.tensor_scalar(AP_[:, cc, :], AEX[:, cc, :], ASUM[:, cc:cc + 1], ANN[:, cc:cc + 1], ALU.mult, ALU.add)\
                     .then_inc(*dve_b.step(f"ap{cc}"))
                    yield
                e.wait_ge(*dve_b.at(b, "ap1"))
                for j in range(4):
                    blk = slice(HD * j, HD * j + HD)
                    e.tensor_copy(ABD[blk, :, blk], AP_[blk, :, :]).then_inc(*dve_b.step(f"abd{j}"))
                    yield
                e.wait_ge(*pe_b.at(b, "be"))
                e.tensor_tensor(BE[:, :], SLOT["bD0"][:, 0:2], COL[:, :, COLS.index("pb2")], ALU.add).then_inc(*dve_b.step("be"))
                yield

            def block3_out(b):
                e.wait_ge(*dve_b.at(b, "be"))
                e.wait_ge(*act_m.at(b - 1, "y6_1_1"))
                for m, half in BLOCKS:
                    e.wait_ge(*pe_b.at(b, f"out_{m}_{half}"))
                    lo = m * (H + 2) + 1 + 16 * half
                    e.scalar_tensor_tensor(out=PA_[:, lo:lo + 16, 1:1 + W],
                                           in0=SLOT[f"bD{half}"][:, :].rearrange("p (h w) -> p h w", w=W),
                                           scalar=BE[:, m:m + 1], in1=XR[:, m, hs(half)].rearrange("p (h w) -> p h w", w=W),
                                           op0=ALU.add, op1=ALU.add).then_inc(*dve_b.step(f"x3_{m}_{half}"))
                    yield

            def pool_norm(b):
                e.wait_ge(*dve_b.at(b, "x3_1_1"))
                yield from group_norm(b, 3, lambda cc, h: PA_[:, cc * (H + 2) + 1 + 16 * h:cc * (H + 2) + 17 + 16 * h, 1:1 + W], None,
                           None, dve_b, pe_b, act_b, "bD0")

            def pool_score(b):
                GR, GB = GN["B"][5:7]
                e.tensor_tensor(GAP[:, :], GAP[:, :], GR[:, :], ALU.mult).then_inc(*dve_b.step("gap3a"))
                e.wait_ge(*dve_b.at(b, "gap3a"))
                e.tensor_tensor(GAP[:, :], GAP[:, :], GB[:, :], ALU.add).then_inc(*dve_b.step("gap3b"))
                yield
                e.wait_ge(*pe_b.at(b, "w1"))
                e.tensor_scalar(HM[:, :], SLOT["bD0"][0:16, 0:1], S16[:, 2 * C + 1:2 * C + 2], 0.0, ALU.add, ALU.max)\
                 .then_inc(*dve_b.step("hm3"))
                yield
                e.wait_ge(*pe_b.at(b, "w2"))
                e.tensor_tensor(SC[:, :], SLOT["bD1"][:, 0:2], COL[:, :, COLS.index("w2_b")], ALU.add).then_inc(*dve_b.step("sc0"))
                e.wait_ge(*dve_b.at(b, "sc0"))
                e.tensor_scalar(SC[:, :], SC[:, :], 0.0, None, ALU.max).then_inc(*dve_b.step("sc"))
                e.wait_ge(*dve_b.at(b, "sc"))
                for cc in range(CC):
                    e.tensor_scalar(CGE[:, cc, :], KIDX[:, :], SC[:, cc:cc + 1], None, ALU.is_le).then_inc(*dve_b.step(f"cge{cc}"))
                e.wait_ge(*dve_b.at(b, "cge1"))
                e.tensor_reduce(QS[:, :], CGE[:, :, 1:6], AX.X, ALU.add).then_inc(*dve_b.step("qs"))
                e.tensor_tensor(EQ[:, :, :], CGE[:, :, 0:KPOOL], CGE[:, :, 1:KPOOL + 1], ALU.subtract).then_inc(*dve_b.step("eq"))
                e.wait_ge(*dve_b.at(b, "eq"))
                e.tensor_tensor(FB[:, :], SC[:, :], QS[:, :], ALU.subtract).then_inc(*dve_b.step("fb"))
                e.tensor_scalar(FS[:, :], QS[:, :], 1.0, None, ALU.add).then_inc(*dve_b.step("fs0"))
                e.wait_ge(*dve_b.at(b, "fs0"))
                e.tensor_tensor(FS[:, :], FS[:, :], SC[:, :], ALU.subtract).then_inc(*dve_b.step("fs"))
                e.wait_ge(*dve_b.at(b, "fs"))
                for cc in range(CC):
                    e.tensor_scalar(WKP[:, cc, :], EQ[:, cc, :], FS[:, cc:cc + 1], None, ALU.mult).then_inc(*dve_b.step(f"ws{cc}"))
                e.wait_ge(*dve_b.at(b, "ws1"))
                for cc in range(CC):
                    e.scalar_tensor_tensor(out=WKP[:, cc, 1:KPOOL], in0=EQ[:, cc, 0:KPOOL - 1], scalar=FB[:, cc:cc + 1],
                                           in1=WKP[:, cc, 1:KPOOL], op0=ALU.mult, op1=ALU.add).then_inc(*dve_b.step(f"wb{cc}"))
                e.wait_ge(*dve_b.at(b, "wb1"))
                for cc in range(CC):
                    e.tensor_scalar(COEF[:, cc, :], WKP[:, cc, :], GR[:, cc:cc + 1], None, ALU.mult).then_inc(*dve_b.step(f"cf{cc}"))
                e.tensor_scalar(C1[:, :], GB[:, :], 2.0, None, ALU.mult).then_inc(*dve_b.step("c1"))
                e.wait_ge(*dve_b.at(b, "c1"))
                e.tensor_tensor(C0[:, :], COEF[:, :, 0], GR[:, :], ALU.add).then_inc(*dve_b.step("c0"))
                e.wait_ge(*dve_b.at(b, "c0"))
                e.tensor_scalar(C0[:, :], C0[:, :], 1.0, None, ALU.add).then_inc(*dve_b.step("coef"))

            def maxpool(b, k):
                src, dst = (PA_, PB_) if k % 2 else (PB_, PA_)
                for cc in range(CC):
                    lo = cc * (H + 2)
                    e.wait_ge(*(dve_m.at(b, f"v{k}_0") if cc else dve_m.at(b, f"v{k - 1}_1") if k > 1 else
                                dve_m.at(b - 1, f"v{KPOOL - 1}_1")))
                    e.tensor_tensor(PH[:, :, :], src[:, lo + 1:lo + 1 + H, 1:1 + W:2], src[:, lo + 1:lo + 1 + H, 2:2 + W:2],
                                    ALU.max).then_inc(*dve_m.step(f"hp{k}_{cc}"))
                    yield
                    e.wait_ge(*dve_m.at(b, f"hp{k}_{cc}"))
                    for s in range(2):
                        e.tensor_tensor(HB[:, 1:1 + H, s:W:2], src[:, lo + 1:lo + 1 + H, 3 * s:3 * s + W - 1:2], PH[:, :, :], ALU.max)\
                         .then_inc(*dve_m.step(f"h{k}_{cc}_{s}"))
                        yield
                    e.wait_ge(*dve_m.at(b, f"h{k}_{cc}_1"))
                    e.tensor_tensor(PV[:, :, :], HB[:, 1:1 + H:2, :], HB[:, 2:2 + H:2, :], ALU.max).then_inc(*dve_m.step(f"vp{k}_{cc}"))
                    yield
                    e.wait_ge(*dve_m.at(b, f"vp{k}_{cc}"))
                    if k >= 2:
                        e.wait_ge(*act_m.at(b, f"y{k - 2}_{cc}_1" if k > 2 else f"a{cc}"))
                    else:
                        e.wait_ge(*act_m.at(b - 1, f"y5_{cc}_1"))
                    for s in range(2):
                        e.tensor_tensor(dst[:, lo + 1 + s:lo + 1 + H:2, 1:1 + W], HB[:, 3 * s:3 * s + H - 1:2, :], PV[:, :, :],
                                        ALU.max).then_inc(*dve_m.step(f"v{k}_{cc}" if s else f"u{k}_{cc}"))
                        yield

            def stream_a(b, setup=None):
                yield from attention_norm(b)
                if setup:
                    setup()
                yield from split_queries(b)
                yield from kv_norm(b)
                yield from split_keys(b)
                for h in range(4):
                    yield from maxima(b, h)
                yield from max_rows(b, 0)
                yield from maxima(b, 4)
                yield from maxima(b, 5)
                yield from weighted(b, 0)
                yield from maxima(b, 6)
                yield from maxima(b, 7)
                yield from max_rows(b, 1)
                for g in range(1, 4):
                    yield from weighted(b, g)
                yield from add_to_image(b, "x1", dve_a, pe_a, "proj0", PB0, X0)
                yield from scan_norm(b)
                yield from variance(b, 1)
                yield from normalise(b, 1, GA0)

            def stream_b(b):
                yield from gate(b)
                yield from delta(b)
                yield from scan(b, 0)
                yield from scan(b, 1)
                yield from gated(b)
                yield from variance(b, 2)
                yield from normalise(b, 2, XM)
                yield from add_to_image(b, "x2", dve_b, pe_b, "proj1", PB1, XR)
                yield from channel_norm(b)
                yield from variance(b, 3)
                yield from ones_column(b)
                yield from normalise(b, 3, G)
                yield from gram(b)
                yield from channel_softmax(b)
                yield from attended(b)
                yield from block3_out(b)
                yield from pool_norm(b)
                yield from pool_score(b)

            def stream_m(b):
                for k in range(1, KPOOL):
                    yield from maxpool(b, k)

            e.wait_ge(*pool_set.at(0, "hb"))
            run(e, {"A": stream_a, "B": stream_b, "M": stream_m}, DVE_ORDER, setup=setup)

        @block.tensor
        def _(e):
            for s in (pe_a, pe_b):
                e.sem_inc(*s.start())
            e.wait_ge(mats_loaded, 16)

            def columns(slot, at, w, name_or_tile):
                for m in range(CC):
                    for cc in range(CC):
                        v = col(name_or_tile, cc) if isinstance(name_or_tile, str) else name_or_tile[:, cc:cc + 1]
                        mm = e.matmul(SLOT[slot][:, at + m:at + m + 1], w[:, cc, m * P:(m + 1) * P], v,
                                      start=(cc == 0), stop=(cc == CC - 1))
                return mm

            def setup():
                e.wait_ge(early_loaded, 16 * EARLY_N)
                columns("bD0", 0, WK, "kv_ln_b")
                columns("bD0", 2, WV, "kv_ln_b")
                columns("bD0", 4, WP1, "ln_b").then_inc(*pe_set.step("fold"))
                for cc in range(CC):
                    mm = e.matmul(SLOT["bD1"][:, cc * P:(cc + 1) * P], XPR[:, cc, :], DTP[:, cc, :], start=True, stop=True)
                mm.then_inc(*pe_set.step("wd"))
                e.wait_ge(*dve_set.at(0, "pb1"))
                columns("bD0", 0, WP0, VB).then_inc(*pe_set.step("fold0"))

            LAST = {"aA0": (act_a, "xd1_0"), "aA1": (act_a, "xd1_1"), "aD0": (dve_a, "gn_gm1"), "aD1": (dve_a, "x1_1_1"),
                    "bA0": (act_b, "we"), "bA1": (act_b, "pat"), "bD0": (dve_b, "hm3"), "bD1": (dve_b, "sc0")}
            state = {}

            def take(b, slot, engine, label):
                if slot in state:
                    e.wait_ge(*state[slot][0].at(b, state[slot][1]))
                else:
                    e.wait_ge(*LAST[slot][0].at(b - 1, LAST[slot][1]))
                state[slot] = (engine, label)
                return SLOT[slot]

            def done(stream):
                for slot in [x for x in state if x[0] == stream]:
                    assert state[slot] == LAST[slot], slot
                    del state[slot]

            def group_norm(b, l, pe, dve, slot):
                MV = GN["A" if l < 2 else "B"][2]
                s = take(b, slot, dve, f"gn_gm{l}")
                e.wait_ge(*dve.at(b, f"gn_ex2{l}"))
                e.matmul(s[:, 0:4], mat("mean_group"), MV[:, :, :].rearrange("p c s -> p (c s)"), start=True, stop=True)\
                 .then_inc(*pe.step(f"gn{l}"))
                yield

            def product(s, w, src, half):
                for cc in range(CC):
                    mm = e.matmul(s[:, :], w(cc), src[:, cc, hs(half)], start=(cc == 0), stop=(cc == CC - 1))
                return mm

            def project(b, w, src, ready, pe, name, slots, engine, label):
                for m, half in BLOCKS:
                    s = take(b, f"{slots}{half}", engine, f"{label}{m}_{half}")
                    if ready:
                        e.wait_ge(*ready)
                    product(s, lambda cc: w[:, cc, m * P:(m + 1) * P], src, half).then_inc(*pe.step(f"{name}{m}_{half}"))
                    yield

            def sums(b, l, src, ready):
                pe, act, dve, _, banks, squares, _, _ = NORM["A" if l == 1 else "B"]
                e.wait_ge(*dve.at(b, ready))
                e.wait_ge(*act.at(b, f"sq{l}_1"))
                for half in range(2):
                    s = take(b, f"{banks}A{half}", dve, f"ln_var{l}" if half else f"ln_var{l}_0")
                    for cc in range(CC):
                        for lo, of in ((0, src), (64, squares)):
                            mm = e.matmul(s[lo:lo + 64, :], mat("mean256")[:, 0:64], of[:, cc, hs(half)], start=(cc == 0), stop=(cc == 1))
                    mm.then_inc(*pe.step(f"sums{l}_{half}"))
                    yield

            def down(b):
                s = take(b, "aA0", act_a, "xds1")
                e.wait_ge(*dve_a.at(b, "g0_1"))
                for m in range(CC):
                    for n in range(4 * CC):
                        cc, dy, dx = n // 4, n % 4 // 2, n % 2
                        src = GA0[:, cc, :].rearrange("p (h w) -> p h w", h=H)[:, dy::2, dx::2]
                        mm = e.matmul(s[:, m * NK:(m + 1) * NK], WDS[:, cc, n % 4, m * P:(m + 1) * P], src,
                                      start=(n == 0), stop=(n == 4 * CC - 1))
                mm.then_inc(*pe_a.step("ds"))
                yield

            def kv_norm(b):
                s = take(b, "aD0", dve_a, "ln_var0")
                e.wait_ge(*act_a.at(b, "sq_ds"))
                for at, src in ((0, XDS), (NK, SQD)):
                    for cc in range(CC):
                        mm = e.matmul(s[:, at:at + NK], mat("mean256"), src[:, cc, :], start=(cc == 0), stop=(cc == CC - 1))
                mm.then_inc(*pe_a.step("msq0"))
                yield

            def keys(b):
                s = take(b, "aA0", act_a, "kf1")
                e.wait_ge(*dve_set.at(0, "wp11"))
                e.wait_ge(*dve_a.at(b, "n0_1"))
                for m in range(CC):
                    for cc in range(CC):
                        mm = e.matmul(s[:, m * NK:(m + 1) * NK], WK[:, cc, m * P:(m + 1) * P], XDS[:, cc, :],
                                      start=(cc == 0), stop=(cc == CC - 1))
                mm.then_inc(*pe_a.step("k"))
                yield
                s = take(b, "aD1", dve_a, "vt")
                for kt in range(2):
                    for cc in range(CC):
                        mm = e.matmul(s[:, kt * C:(kt + 1) * C], XDS[:, cc, kt * P:(kt + 1) * P], WV[:, cc, :],
                                      start=(cc == 0), stop=(cc == CC - 1))
                mm.then_inc(*pe_a.step("vT"))
                yield

            def scores(b, h):
                if h == 0:
                    e.wait_ge(stacked, 16 * STACK_DMAS * b + 16 * STACK_DMAS)
                for j in range(4):
                    s = take(b, f"aD{j % 2}", dve_a, f"mx{h}_{j}")
                    for t in range(2):
                        qt = 2 * j + t
                        mm = e.matmul(s[:, t * NK:(t + 1) * NK], QST[0:96, h, qt * P:(qt + 1) * P], KST[0:96, h, :],
                                      start=True, stop=True)
                    mm.then_inc(*pe_a.step(f"s{h}_{j}"))
                    yield

            def max_rows(b, g):
                s = take(b, "aD0", dve_a, f"ml{g}")
                e.wait_ge(*dve_a.at(b, f"mx{4 * g + 3}_3"))
                e.transpose(s[0:32, 0:P], NEGMAX[:, 4 * g:4 * g + 4, :].rearrange("p h t -> p (h t)"), mat("ident"))\
                 .then_inc(*pe_a.step(f"mT{g}"))
                yield

            def scores_t(b, g, kt):
                if g % 2 == 0 and kt == 0:
                    e.wait_ge(maxed, 16 * MAX_DMAS * b + 16 * 2 * (g // 2 + 1))
                    e.wait_ge(*pool_set.at(0, "hb"))
                for j in range(4):
                    h = 4 * (g // 2) + j
                    s = take(b, f"aA{j % 2}", act_a, f"p{g}_{kt}_{j}")
                    e.matmul(s[:, :], KST[0:98, h, kt * P:(kt + 1) * P], QST[0:98, h, hs(g % 2)], start=True, stop=True)\
                     .then_inc(*pe_a.step(f"st{g}_{kt}_{j}"))
                    yield

            def weighted(b, g, kt):
                if kt == 0:
                    take(b, "aD0", act_a, f"lz{g}")
                    take(b, "aD1", dve_a, f"o{g}")
                e.wait_ge(*act_a.at(b, f"p{g}_{kt}_3"))
                for slot in ("aD1", "aD0"):
                    for j in range(4):
                        w = VT[:, kt, 4 * (g // 2) + j, :] if slot == "aD1" else ONES[:, :]
                        mm = e.matmul(SLOT[slot][HD * j:HD * j + HD, :], w, PROB[:, 4 * kt + j, :],
                                      start=(kt == 0), stop=(kt == 1))
                mm.then_inc(*pe_a.step(f"pv{g}_{kt}"))
                yield

            def convolve(b, cc):
                e.wait_ge(*pool_set.at(0, "wtap1_2"))
                e.wait_ge(*act_a.at(b, "xn3"))
                for half in range(2):
                    s = take(b, f"aA{half}", act_a, f"xd{cc}_{half}")
                    for n in range(TAPS):
                        dy, dx = n // 3, n % 3
                        mm = e.matmul(s[:, :], WTAP[:, cc, n, :], XNP[:, cc, dy + 16 * half:dy + 16 * half + 16, dx:dx + W],
                                      start=(n == 0), stop=(n == TAPS - 1))
                    mm.then_inc(*pe_a.step(f"xd{cc}_{half}"))
                    yield

            def gate_z(b):
                for cc, half in BLOCKS:
                    s = take(b, f"bA{half}", act_b, f"z{cc}_{half}")
                    e.matmul(s[:, :], IPZ[:, cc, :], XNP[:, cc, 1 + 16 * half:17 + 16 * half, 1:1 + W], start=True, stop=True)\
                     .then_inc(*pe_b.step(f"z{cc}_{half}"))
                    yield

            def small_mlp(b, at, means, sources, l, steps):
                s = take(b, "bD0", dve_b, f"hm{l}")
                e.wait_ge(*sources)
                for cc in range(CC):
                    mm = e.matmul(s[0:16, 0:1], W1S[:, cc, 16 * at:16 * at + 16], means[:, cc:cc + 1], start=(cc == 0), stop=(cc == 1))
                mm.then_inc(*pe_b.step(steps[0]))
                yield
                s = take(b, "bD1", dve_b, "sc0" if at else "gate_in")
                e.wait_ge(*dve_b.at(b, f"hm{l}"))
                for m in range(CC):
                    mm = e.matmul(s[:, m:m + 1], S16[:, at * C + m * P:at * C + (m + 1) * P], HM[:, :], start=True, stop=True)
                mm.then_inc(*pe_b.step(steps[1]))
                yield

            def by_chunk(b, cc, slots, engine, label, w, step, src):
                for half in range(2):
                    s = take(b, f"{slots}{half}", engine, f"{label}_{half}")
                    e.matmul(s[:, :], w, src[:, cc, hs(half)], start=True, stop=True).then_inc(*pe_b.step(f"{step}{cc}_{half}"))
                    yield

            def delta(b):
                for cc in range(CC):
                    e.wait_ge(*act_b.at(b, f"u{cc}"))
                    yield from by_chunk(b, cc, "bA", act_b, f"v{cc}", WD[:, cc, :], "v", U)

            def scan(b, cc):
                yield from by_chunk(b, cc, "bD", dve_b, f"dbu{cc}", XB[:, cc, :], "B", U)
                yield from by_chunk(b, cc, "bD", dve_b, f"hc{cc}", XC[:, cc, :], "C", U)

            def centred(b):
                for cc in range(CC):
                    e.wait_ge(*dve_b.at(b, f"y{cc}"))
                    yield from by_chunk(b, cc, "bA", act_b, f"ysq{cc}", mat("center64"), "yc", U)

            def y_variance(b):
                for cc in range(CC):
                    for half in range(2):
                        s = take(b, f"bA{half}", act_b, f"yln{cc}_{half}")
                        e.wait_ge(*act_b.at(b, f"ysq{cc}_{half}"))
                        e.matmul(s[:, :], mat("mean64"), SQ[:, cc, hs(half)], start=True, stop=True)\
                         .then_inc(*pe_b.step(f"yv{cc}_{half}"))
                        yield

            def gated(b):
                for cc in range(CC):
                    for half in range(2):
                        s = take(b, f"bD{half}", dve_b, f"xm{2 * cc + 1}_{half}")
                        e.wait_ge(*dve_b.at(b, f"yz{cc}"))
                        e.matmul(s[:, :], OPW[:, cc, :], G[:, cc, hs(half)], start=True, stop=True)\
                         .then_inc(*pe_b.step(f"op{cc}_{half}"))
                        yield

            def pixel_rows(b):
                for t in range(4):
                    s = take(b, f"bA{t % 2}", act_b, f"xnt{t}")
                    e.wait_ge(*dve_b.at(b, "n3_1"))
                    for i in range(2):
                        for cc in range(CC):
                            mm = e.transpose(s[:, i * C + cc * P:i * C + (cc + 1) * P],
                                             G[:, cc, (2 * t + i) * P:(2 * t + i + 1) * P], mat("ident"))
                    mm.then_inc(*pe_b.step(f"xnT{t}"))
                    yield

            def gram(b):
                for m in range(CC):
                    s = take(b, f"bD{m}", dve_b, f"gram{m}")
                    e.wait_ge(*act_b.at(b, "xnt3"))
                    e.wait_ge(*dve_b.at(b, "xnt_ones"))
                    for t in range(QT):
                        mm = e.matmul(s[:, 0:C + 1], XNT[:, t, m * P:(m + 1) * P], XNT[:, t, :],
                                      start=(t == 0), stop=(t == QT - 1))
                    mm.then_inc(*pe_b.step(f"gram{m}"))
                    yield

            def channel_scores(b):
                s = take(b, "bD0", dve_b, "srow")
                e.wait_ge(*dve_b.at(b, "gram1"))
                for cc in range(CC):
                    e.matmul(s[0:1, cc * P:(cc + 1) * P], GRAM[:, cc, C:C + 1], mat("ident"), start=True, stop=True)
                for cc in range(CC):
                    e.matmul(s[0:1, C:2 * C], GRAM[:, cc, C:C + 1], W2Q[:, cc, :], start=(cc == 0), stop=False)
                e.matmul(s[0:1, C:2 * C], ROWS[:, 2 * C:2 * C + 1], ROWS[:, 0:C], start=False, stop=True)\
                 .then_inc(*pe_b.step("rows"))
                yield
                s = take(b, "bA0", act_b, "t1")
                e.wait_ge(*dve_b.at(b, "srow"))
                for m in range(CC):
                    for cc in range(CC):
                        e.matmul(s[:, m * C:(m + 1) * C], GRAM[:, cc, m * P:(m + 1) * P], W2Q[:, cc, :], start=(cc == 0), stop=False)
                    mm = e.matmul(s[:, m * C:(m + 1) * C], SROW[:, m * P:(m + 1) * P], ROWS[:, 0:C], start=False, stop=True)
                mm.then_inc(*pe_b.step("T1"))
                yield
                s = take(b, "bD1", dve_b, "aok3")
                e.wait_ge(*act_b.at(b, "t1"))
                for m in range(CC):
                    for cc in range(CC):
                        e.matmul(s[:, m * P:(m + 1) * P], T1[:, cc, m * P:(m + 1) * P], W2K[:, cc, m * P:(m + 1) * P],
                                 start=(cc == 0), stop=False)
                    mm = e.matmul(s[:, m * P:(m + 1) * P], SROW[:, C + m * P:C + (m + 1) * P],
                                  ROWS[:, C + m * P:C + (m + 1) * P], start=False, stop=True)
                mm.then_inc(*pe_b.step("A"))
                yield

            def attended(b):
                s = take(b, "bA1", act_b, "pat")
                e.wait_ge(*dve_b.at(b, "abd3"))
                for m in range(CC):
                    mm = e.matmul(s[:, m * C:(m + 1) * C], ABD[:, m, :], WP2[:, m, :], start=True, stop=True)
                mm.then_inc(*pe_b.step("PAT"))
                yield
                s = take(b, "bA0", act_b, "we")
                e.wait_ge(*act_b.at(b, "pat"))
                for m in range(CC):
                    for cc in range(CC):
                        mm = e.matmul(s[:, m * C:(m + 1) * C], W2V[:, cc, m * P:(m + 1) * P], PAT[:, cc, :],
                                      start=(cc == 0), stop=(cc == 1))
                mm.then_inc(*pe_b.step("WE"))
                yield
                take(b, "bD0", dve_b, "be")
                columns("bD0", 0, PAT, "v2_b").then_inc(*pe_b.step("be"))
                yield

            def stream_a(b, setup=None):
                yield from group_norm(b, 0, pe_a, dve_a, "aD0")
                if setup:
                    setup()
                yield from down(b)
                yield from project(b, WQ, GA0, None, pe_a, "q", "aA", act_a, "qf")
                yield from kv_norm(b)
                yield from keys(b)
                for h in range(4):
                    yield from scores(b, h)
                yield from max_rows(b, 0)
                for g in range(4):
                    if g == 0:
                        yield from scores_t(b, 0, 0)
                        yield from scores_t(b, 0, 1)
                        yield from scores(b, 4)
                        yield from scores(b, 5)
                    yield from weighted(b, g, 0)
                    if g < 3 and g != 1:
                        yield from scores_t(b, g + 1, 0)
                    yield from weighted(b, g, 1)
                    if g == 0:
                        yield from scores(b, 6)
                        yield from scores(b, 7)
                        yield from max_rows(b, 1)
                    if g == 1:
                        yield from scores_t(b, 2, 0)
                    if g < 3:
                        yield from scores_t(b, g + 1, 1)
                yield from project(b, WP0, GA0, dve_a.at(b, "o3"), pe_a, "proj0_", "aD", dve_a, "x1_")
                yield from group_norm(b, 1, pe_a, dve_a, "aD0")
                yield from sums(b, 1, GA0, "g1_1")
                yield from convolve(b, 0)
                yield from convolve(b, 1)
                done("a")

            def stream_b(b):
                yield from gate_z(b)
                yield from small_mlp(b, 0, GAPX, dve_b.at(b, "gap1"), 1, ("fc1", "fc2"))
                yield from delta(b)
                yield from scan(b, 0)
                yield from scan(b, 1)
                yield from centred(b)
                yield from y_variance(b)
                yield from gated(b)
                yield from sums(b, 2, XM, "xm3_1")
                yield from project(b, WP1, XM, dve_b.at(b, "n2_1"), pe_b, "proj1_", "bD", dve_b, "x2_")
                yield from group_norm(b, 2, pe_b, dve_b, "bD0")
                yield from sums(b, 3, G, "g2_1")
                yield from pixel_rows(b)
                yield from gram(b)
                yield from channel_scores(b)
                yield from attended(b)
                yield from project(b, WE, G, act_b.at(b, "we"), pe_b, "out_", "bD", dve_b, "x3_")
                yield from group_norm(b, 3, pe_b, dve_b, "bD0")
                yield from small_mlp(b, 1, GAP, dve_b.at(b, "gap3b"), 3, ("w1", "w2"))
                done("b")

            def before_b():
                e.wait_ge(*dve_set.at(0, "pb0"))
                e.wait_ge(late_loaded, 16 * LATE_N)

            run(e, {"A": stream_a, "B": stream_b}, PE_ORDER, before_b, setup)

        return {"PE_A": pe_a, "PE_B": pe_b, "ACT_A": act_a, "ACT_B": act_b, "ACT_M": act_m, "DVE_A": dve_a,
                "DVE_B": dve_b, "DVE_M": dve_m, "POOL_A": pool_a, "POOL_B": pool_b, "POOL_M": pool_m,
                "PE_SETUP": pe_set, "ACT_SETUP": act_set, "DVE_SETUP": dve_set, "POOL_SETUP": pool_set}


def _arrays(i):
    import numpy as np
    f = {k: np.ascontiguousarray(v) for k, v in i.items()}

    def t2(w):
        return w.T.reshape(CC, P, -1).transpose(1, 0, 2)

    def vec(v):
        return np.asarray(v).reshape(CC, P).T

    def pairs(blocks, rows=64):
        a = np.zeros((2 * rows, CC, P), np.float32)
        for g in range(GROUPS):
            h = g % 2
            a[rows * h:rows * h + rows, g // 2, 64 * h:64 * h + 64] = blocks[g]
        return a

    L0, L1, L2, L3 = "L0_conv_", "L1_conv_", "L2_conv_", "L3_conv_"
    kvw, kvb = f[L0 + "kv_w"], f[L0 + "kv_b"]
    vecs = dict(q_b=f[L0 + "q_b"], k_b=kvb[:C], v_b=kvb[C:], ds_b=f[L0 + "ds_b"], kv_ln_w=f[L0 + "ln_w"],
                kv_ln_b=f[L0 + "ln_b"], pb0=f[L0 + "proj_b"], ln_g=f[L1 + "ln_g"], ln_b=f[L1 + "ln_b"],
                fc2_b=f[L1 + "fc2_b"], skip=np.broadcast_to(f[L1 + "skip_scale"], (C,)), conv_b=f[L1 + "conv_b"],
                dt_b=f[L1 + "dt_proj_b"], A_log=f[L1 + "A_log"], Ds=f[L1 + "Ds_p"], og=f[L1 + "onorm_g"],
                ob=f[L1 + "onorm_b"], pb1=f[L1 + "proj_b"], v2_b=f[L2 + "qkv_b"][2 * C:], pb2=f[L2 + "proj_b"],
                w2_b=f[L3 + "b2"])
    eye, one = np.eye(P, dtype=np.float32), np.ones((P, P), np.float32)
    b64 = np.kron(np.eye(2), np.ones((64, 64))).astype(np.float32) / 64
    b8 = np.kron(np.eye(16), np.ones((8, 8))).astype(np.float32) / 32
    kern = []
    for g in range(GROUPS):
        k = f[L1 + "conv_w"][g, :, 0]
        k = k.transpose(0, 2, 1) if g % 2 else k
        kern.append(k[:, ::-1, ::-1] if g >= 2 else k)
    cw = np.stack([np.concatenate([kern[2 * c].reshape(64, 9), kern[2 * c + 1].reshape(64, 9)]).T for c in range(CC)])
    ip, xp = f[L1 + "in_proj_w"], f[L1 + "x_proj_w"]
    qkv, qb = f[L2 + "qkv_w"], f[L2 + "qkv_b"]
    kidx = np.broadcast_to(np.array([-1, 1, 2, 3, 4, 5, np.float32(3.4e38), np.float32(3.4e38)], np.float32), (P, 8))
    a = dict(
        x=f["x"], cols=np.stack([vec(vecs[n]) for n in COLS], -1),
        mats=np.stack([eye, one / 256, b64, eye - b64, b8], 1),
        wq=t2(f[L0 + "q_w"]), wk=t2(kvw[:C]), wv=t2(kvw[C:]),
        wds=f[L0 + "ds_w"].transpose(1, 2, 3, 0).reshape(CC, P, 4, C).transpose(1, 0, 2, 3), wp0=t2(f[L0 + "proj_w"]),
        small16=np.concatenate([f[L1 + "fc2_w"].T, f[L3 + "w2"].T, f[L1 + "fc1_b"][:, None], f[L3 + "b1"][:, None]], 1),
        w1s=np.concatenate([t2(f[L1 + "fc1_w"]), t2(f[L3 + "w1"])], 2),
        ipx=pairs([ip[g, :64].T for g in range(GROUPS)]), ipz=pairs([ip[g, 64:].T for g in range(GROUPS)]),
        cw=cw.reshape(3, 768),
        xpr=pairs([xp[g, :8] for g in range(GROUPS)], 8), dtp=pairs([f[L1 + "dt_proj_w"][g].T for g in range(GROUPS)], 8),
        xb=pairs([np.broadcast_to(xp[g, 8][:, None], (64, 64)) for g in range(GROUPS)]),
        xc=pairs([np.broadcast_to(xp[g, 9][:, None], (64, 64)) for g in range(GROUPS)]),
        opw=pairs([f[L1 + "out_proj_w"][g].T for g in range(GROUPS)]), wp1=t2(f[L1 + "proj_w"]),
        w2q=t2(qkv[:C]), w2k=t2(qkv[C:2 * C]), w2v=qkv[2 * C:].reshape(CC, P, C).transpose(1, 0, 2), wp2=t2(f[L2 + "proj_w"]),
        rows=np.concatenate([qb[:C], qb[C:2 * C], np.array([N], np.float32)])[None], kidx=kidx)
    return {k: np.ascontiguousarray(v) for k, v in a.items()}


def kernel(**inputs):
    import concourse.bacc as _bacc
    from concourse import mybir as _mybir
    from concourse.bass_utils import run_bass_kernel_spmd as _run

    nc = _bacc.Bacc("TRN2", target_bir_lowering=False, num_devices=1)
    arrays, args = {}, []
    for name, v in _arrays(inputs).items():
        arrays[f"in_{name}"] = v
        args.append(nc.dram_tensor(f"in_{name}", v.shape, _mybir.dt.from_np(v.dtype), kind="ExternalInput").ap())
    args.append(nc.dram_tensor("out_0", (B, C, H, W), _mybir.dt.float32, kind="ExternalOutput").ap())
    program(nc, *args)
    r = _run(nc, [arrays], core_ids=[0])
    return r.results[0]["out_0"]
```
